# Optimizing a Trainium2 kernel written in Bass

```python
import numpy as np
import jax
import jax.numpy as jnp

def _softmax(x, axis=-1):
    return jax.nn.softmax(x, axis=axis)

def _gelu(x):
    return jax.nn.gelu(x, approximate=True)

def _silu(x):
    return jax.nn.silu(x)

def _sigmoid(x):
    return jax.nn.sigmoid(x)

def _layernorm(x, axis=-1, eps=1e-05):
    m = jnp.mean(x, axis=axis, keepdims=True)
    v = jnp.var(x, axis=axis, keepdims=True)
    return (x - m) / jnp.sqrt(v + eps)

def _scatter_add(tgt, idx, src, axis=0):
    return tgt.at[idx].add(src)

def _segment_sum(src, seg, n):
    return jax.ops.segment_sum(src, seg, n)
kernel_name = 'mk_perceiver_d1_seqx_r8_c69397'

def setup_inputs(seed: int=0):
    np.random.seed(seed)
    _w = jnp.asarray

    def _rec_inputs():
        import jax
        import jax.numpy as jnp
        _rk = jax.random.key(seed)
        x = -0.0002928 + 1 * jax.random.normal(jax.random.fold_in(_rk, 1), (4, 128, 128), jnp.float32)
        _lenS = 128 - jax.random.randint(jax.random.fold_in(_rk, 7), (4,), 0, max(1, 128 // 4) + 1, jnp.int32)
        _lenS2 = 2048 - jax.random.randint(jax.random.fold_in(_rk, 8), (4,), 0, max(1, 2048 // 4) + 1, jnp.int32)
        _ctx_1024P = jax.random.normal(jax.random.fold_in(_rk, 11), (4, 16, 128), jnp.float32)
        _ctx_1024c = jax.random.dirichlet(jax.random.fold_in(_rk, 511), 0.3 * jnp.ones((16,), jnp.float32), (4, 2048))
        _ctx_1024t = jnp.einsum('bsk,bkd->bsd', _ctx_1024c, _ctx_1024P)
        _ctx_1024t = _ctx_1024t * jax.lax.rsqrt(jnp.mean(jnp.square(_ctx_1024t)) + 1e-12) * 0.953939
        ctx_1024 = -1.39393e-06 + 0.999914 * (_ctx_1024t + 0.3 * jax.random.normal(jax.random.fold_in(_rk, 611), (4, 2048, 128), jnp.float32))
        _validS = jnp.arange(128)[None, :] < _lenS[:, None]
        _validS2 = jnp.arange(2048)[None, :] < _lenS2[:, None]
        _causal = jnp.tril(jnp.ones((128, 128), dtype=bool))
        mask_BxSxS2_bk1 = jnp.broadcast_to(_validS2[:, None, :], (4, 128, 2048))
        return (x, ctx_1024, mask_BxSxS2_bk1)
    x, ctx_1024, mask_BxSxS2_bk1 = _rec_inputs()

    def _L0_xattn_setup():
        import jax, jax.numpy as jnp
        import numpy as np
        B, TQ, TK, D, H = (2, 256, 256, 128, 16)
        key = jax.random.key(seed)
        ks = jax.random.split(key, 8)
        s = 1.0 / np.sqrt(D)
        x_q = jax.random.normal(ks[0], (B, TQ, D), jnp.float32)
        x_k = jax.random.normal(ks[1], (B, TK, D), jnp.float32)
        x_v = jax.random.normal(ks[2], (B, TK, D), jnp.float32)
        causal = jnp.triu(jnp.ones((TQ, TK), jnp.bool_), k=1)
        attn_mask = jnp.broadcast_to(causal, (B, TQ, TK))
        Wq = jax.random.normal(ks[3], (D, D), jnp.float32) * s
        Wk = jax.random.normal(ks[4], (D, D), jnp.float32) * s
        Wv = jax.random.normal(ks[5], (D, D), jnp.float32) * s
        Wo = jax.random.normal(ks[6], (D, D), jnp.float32) * s
        z = jnp.zeros((D,), jnp.float32)
        return {'x_q': x_q, 'x_k': x_k, 'x_v': x_v, 'attn_mask': attn_mask, 'Wq': Wq, 'bq': z, 'Wk': Wk, 'bk': z, 'Wv': Wv, 'bv': z, 'Wo': Wo, 'bo': z, 'n_heads': H}
    _L0_xattn_all = _L0_xattn_setup()
    _L0_xattn_in = {k: v for k, v in _L0_xattn_all.items() if k in ('Wq', 'bq', 'Wk', 'bk', 'Wv', 'bv', 'Wo', 'bo')}
    del _L0_xattn_all

    def _L0_attn_setup():
        import jax, jax.numpy as jnp
        import numpy as np
        B, L, DM, DI, H = (4, 256, 128, 256, 16)
        HD = DI // H
        KS = 4
        ROPE_BASE = 10000.0
        GATING_C = 8.0
        EPS_NORM = 1e-06
        EPS_DT = 0.0001
        GN_GROUPS = 16
        GN_EPS = 1e-05

        def _rms_norm(x, w):
            v = jnp.mean(x * x, axis=-1, keepdims=True)
            return x * jax.lax.rsqrt(v + EPS_NORM) * w

        def _conv_silu(x, w, b):
            k = w.shape[1]
            xp = jnp.pad(x, ((0, 0), (k - 1, 0), (0, 0)))
            y = b
            for j in range(k):
                y = y + xp[:, j:j + x.shape[1], :] * w[:, j]
            return y * jax.nn.sigmoid(y)

        def _forward(x, rms_w, in_proj_w, in_proj_b, conv_w, conv_b, gate_w, gate_b, log_dt_scale, Q_w, readout_w, out_w, gn_w, gn_b, D_param):
            b, l, _ = x.shape
            di = conv_w.shape[0]
            h = log_dt_scale.shape[0]
            hd = di // h
            residual = x
            xn = _rms_norm(x, rms_w)
            proj = xn @ in_proj_w + in_proj_b
            z = proj[..., :di]
            x_gate = proj[..., di:2 * di]
            K = proj[..., 2 * di:3 * di].reshape(b, l, h, hd)
            V = proj[..., 3 * di:].reshape(b, l, h, 2)
            x_conv = _conv_silu(x_gate, conv_w, conv_b)
            gates = (x_conv @ gate_w + gate_b).reshape(b, l, 7, h)
            alpha_raw, omega_raw = (gates[..., 0, :], gates[..., 1, :])
            sel_B, sel_C = (gates[..., 2, :], gates[..., 3, :])
            sel_dt, beta_raw, r_raw = (gates[..., 4, :], gates[..., 5, :], gates[..., 6, :])
            freqs = 1.0 / ROPE_BASE ** (jnp.arange(h, dtype=jnp.float32) / h)
            dt = jax.nn.softplus(sel_dt) * jnp.exp(log_dt_scale) + EPS_DT
            alpha = jax.nn.softplus(alpha_raw)
            omega = freqs * (1.0 + jnp.tanh(omega_raw))
            ah, wh = (0.5 * dt * alpha, 0.5 * dt * omega)
            det = (1.0 + ah) ** 2 + wh ** 2
            c = (1.0 - ah ** 2 - wh ** 2) / det
            s = 2.0 * wh / det
            mag = jnp.sqrt(c * c + s * s)
            theta = jnp.arctan2(s, c)
            r = jax.nn.sigmoid(r_raw)
            mag2 = jnp.exp(GATING_C * r * jnp.log(jnp.clip(mag, 1e-08, 1.0)))
            cbar, sbar = (mag2 * jnp.cos(theta), mag2 * jnp.sin(theta))
            vp_scale = jax.nn.sigmoid(sel_B) * jnp.sqrt(jnp.clip(1.0 - mag2 ** 2, 0.0, 1.0) + 1e-06)
            beta = jax.nn.sigmoid(beta_raw)
            sel_C_gate = jax.nn.sigmoid(sel_C)
            Q = (x_conv @ Q_w).reshape(b, l, h, hd)
            K = K / (jnp.linalg.norm(K, axis=-1, keepdims=True) + 1e-06)
            Q = Q / (jnp.linalg.norm(Q, axis=-1, keepdims=True) + 1e-06)
            Vg = V * vp_scale[..., None]

            def step(S, inp):
                ct, st, kt, vt, bt = inp
                S0, S1 = (S[:, :, 0], S[:, :, 1])
                Sd = jnp.stack([ct[..., None] * S0 + st[..., None] * S1, -st[..., None] * S0 + ct[..., None] * S1], axis=2)
                pred = jnp.einsum('bhsd,bhd->bhs', Sd, kt)
                Sn = Sd + bt[:, :, None, None] * (vt - pred)[..., None] * kt[:, :, None, :]
                return (Sn, Sn)
            xs = (jnp.moveaxis(cbar, 1, 0), jnp.moveaxis(sbar, 1, 0), jnp.moveaxis(K, 1, 0), jnp.moveaxis(Vg, 1, 0), jnp.moveaxis(beta, 1, 0))
            S0 = jnp.zeros((b, h, 2, hd), dtype=x.dtype)
            _, Ys = jax.lax.scan(step, S0, xs)
            Y = jnp.moveaxis(Ys, 0, 1)
            retrieved = jnp.einsum('blhsd,blhd->blhs', Y, Q) * sel_C_gate[..., None]
            y = retrieved.reshape(b, l, h * 2) @ readout_w
            yf = y.astype(jnp.float32).reshape(b, l, GN_GROUPS, di // GN_GROUPS)
            mean = jnp.mean(yf, axis=(1, 3), keepdims=True)
            var = jnp.mean((yf - mean) ** 2, axis=(1, 3), keepdims=True)
            yn = ((yf - mean) * jax.lax.rsqrt(var + GN_EPS)).reshape(b, l, di)
            y = (yn * gn_w + gn_b).astype(x.dtype)
            y = y * (z * jax.nn.sigmoid(z))
            y = y + D_param * x_conv
            out = y @ out_w
            return residual + out
        key = jax.random.key(seed)
        ks = jax.random.split(key, 16)
        in_sz = 3 * DI + 2 * H
        gate_b = jnp.concatenate([jnp.zeros(2 * H), jnp.full((H,), 1.0), jnp.full((H,), 1.0), jnp.full((H,), -4.0), jnp.zeros(H), jnp.full((H,), -2.0)])
        return {'x': jax.random.normal(ks[0], (B, L, DM), jnp.float32), 'rms_w': jnp.ones((DM,), jnp.float32), 'in_proj_w': jax.random.normal(ks[1], (DM, in_sz), jnp.float32) / np.sqrt(DM), 'in_proj_b': jnp.zeros((in_sz,), jnp.float32), 'conv_w': jax.random.normal(ks[2], (DI, KS), jnp.float32) / np.sqrt(KS), 'conv_b': jnp.zeros((DI,), jnp.float32), 'gate_w': jax.random.normal(ks[3], (DI, 7 * H), jnp.float32) / np.sqrt(DI), 'gate_b': gate_b.astype(jnp.float32), 'log_dt_scale': 0.1 * jax.random.normal(ks[4], (H,), jnp.float32), 'Q_w': jnp.eye(DI, dtype=jnp.float32), 'readout_w': jax.random.normal(ks[5], (2 * H, DI), jnp.float32) / np.sqrt(2 * H), 'out_w': jax.random.normal(ks[6], (DI, DM), jnp.float32) / np.sqrt(DI), 'gn_w': jnp.ones((DI,), jnp.float32) + 0.1 * jax.random.normal(ks[7], (DI,), jnp.float32), 'gn_b': 0.1 * jax.random.normal(ks[8], (DI,), jnp.float32), 'D_param': 0.1 * jax.random.normal(ks[9], (DI,), jnp.float32)}
    _L0_attn_all = _L0_attn_setup()
    _L0_attn_in = {k: v for k, v in _L0_attn_all.items() if k in ('rms_w', 'in_proj_w', 'in_proj_b', 'conv_w', 'conv_b', 'gate_w', 'gate_b', 'log_dt_scale', 'Q_w', 'readout_w', 'out_w', 'gn_w', 'gn_b', 'D_param')}
    del _L0_attn_all

    def _L0_ffn_setup():
        import jax, jax.numpy as jnp
        import numpy as np
        INT4_QMAX = 7.0

        def simulate_quantize_int4(w):
            scale = jnp.max(jnp.abs(w)) / INT4_QMAX
            q = jnp.clip(jnp.round(w / scale), -8.0, 7.0)
            return q * scale
        key = jax.random.key(seed)
        k_x, k_w, k_bias, k_a, k_b = jax.random.split(key, 5)
        d_in, features, rank = (128, 128, 16)
        x = jax.random.normal(k_x, (4, 1024, d_in), dtype=jnp.float32)
        kernel = jax.random.normal(k_w, (d_in, features), dtype=jnp.float32)
        bias = jax.random.normal(k_bias, (features,), dtype=jnp.float32)
        a = jax.random.normal(k_a, (d_in, rank), dtype=jnp.float32) * (1.0 / np.sqrt(d_in))
        b = jax.random.normal(k_b, (rank, features), dtype=jnp.float32) * 0.01
        return {'x': x, 'kernel': kernel, 'bias': bias, 'a': a, 'b': b}
    _L0_ffn_all = _L0_ffn_setup()
    _L0_ffn_in = {k: v for k, v in _L0_ffn_all.items() if k in ('kernel', 'bias', 'a', 'b')}
    del _L0_ffn_all
    return {'x': x, 'ctx_1024': ctx_1024, 'mask_BxSxS2_bk1': mask_BxSxS2_bk1, 'L0_xattn_Wq': _L0_xattn_in['Wq'], 'L0_xattn_bq': _L0_xattn_in['bq'], 'L0_xattn_Wk': _L0_xattn_in['Wk'], 'L0_xattn_bk': _L0_xattn_in['bk'], 'L0_xattn_Wv': _L0_xattn_in['Wv'], 'L0_xattn_bv': _L0_xattn_in['bv'], 'L0_xattn_Wo': _L0_xattn_in['Wo'], 'L0_xattn_bo': _L0_xattn_in['bo'], 'L0_attn_rms_w': _L0_attn_in['rms_w'], 'L0_attn_in_proj_w': _L0_attn_in['in_proj_w'], 'L0_attn_in_proj_b': _L0_attn_in['in_proj_b'], 'L0_attn_conv_w': _L0_attn_in['conv_w'], 'L0_attn_conv_b': _L0_attn_in['conv_b'], 'L0_attn_gate_w': _L0_attn_in['gate_w'], 'L0_attn_gate_b': _L0_attn_in['gate_b'], 'L0_attn_log_dt_scale': _L0_attn_in['log_dt_scale'], 'L0_attn_Q_w': _L0_attn_in['Q_w'], 'L0_attn_readout_w': _L0_attn_in['readout_w'], 'L0_attn_out_w': _L0_attn_in['out_w'], 'L0_attn_gn_w': _L0_attn_in['gn_w'], 'L0_attn_gn_b': _L0_attn_in['gn_b'], 'L0_attn_D_param': _L0_attn_in['D_param'], 'L0_ffn_kernel': _L0_ffn_in['kernel'], 'L0_ffn_bias': _L0_ffn_in['bias'], 'L0_ffn_a': _L0_ffn_in['a'], 'L0_ffn_b': _L0_ffn_in['b']}

def reference(x, ctx_1024, mask_BxSxS2_bk1, L0_xattn_Wq, L0_xattn_bq, L0_xattn_Wk, L0_xattn_bk, L0_xattn_Wv, L0_xattn_bv, L0_xattn_Wo, L0_xattn_bo, L0_attn_rms_w, L0_attn_in_proj_w, L0_attn_in_proj_b, L0_attn_conv_w, L0_attn_conv_b, L0_attn_gate_w, L0_attn_gate_b, L0_attn_log_dt_scale, L0_attn_Q_w, L0_attn_readout_w, L0_attn_out_w, L0_attn_gn_w, L0_attn_gn_b, L0_attn_D_param, L0_ffn_kernel, L0_ffn_bias, L0_ffn_a, L0_ffn_b):
    import jax
    import jax.numpy as jnp

    def _L0_xattn_ref(x_q, x_k, x_v, attn_mask, Wq, bq, Wk, bk, Wv, bv, Wo, bo, n_heads):
        import jax, jax.numpy as jnp
        import numpy as np
        B, TQ, TK, D, H = (2, 256, 256, 128, 16)
        Bv, Tq, Dm = x_q.shape
        Tk = x_k.shape[1]
        dh = Dm // n_heads
        Q = (jnp.einsum('btd,od->bto', x_q, Wq) + bq).reshape(Bv, Tq, n_heads, dh).transpose(0, 2, 1, 3)
        K = (jnp.einsum('btd,od->bto', x_k, Wk) + bk).reshape(Bv, Tk, n_heads, dh).transpose(0, 2, 1, 3)
        V = (jnp.einsum('btd,od->bto', x_v, Wv) + bv).reshape(Bv, Tk, n_heads, dh).transpose(0, 2, 1, 3)
        scale = 1.0 / np.sqrt(dh).astype(np.float32)
        scores = jnp.einsum('bhqd,bhkd->bhqk', Q, K) * scale
        scores = jnp.where(attn_mask[:, None, :, :], -jnp.inf, scores)
        A = jax.nn.softmax(scores, axis=-1)
        out = jnp.einsum('bhqk,bhkd->bhqd', A, V)
        out = out.transpose(0, 2, 1, 3).reshape(Bv, Tq, Dm)
        return jnp.einsum('btd,od->bto', out, Wo) + bo

    def _L0_attn_ref(x, rms_w, in_proj_w, in_proj_b, conv_w, conv_b, gate_w, gate_b, log_dt_scale, Q_w, readout_w, out_w, gn_w, gn_b, D_param):
        import jax, jax.numpy as jnp
        import numpy as np
        B, L, DM, DI, H = (4, 256, 128, 256, 16)
        HD = DI // H
        KS = 4
        ROPE_BASE = 10000.0
        GATING_C = 8.0
        EPS_NORM = 1e-06
        EPS_DT = 0.0001
        GN_GROUPS = 16
        GN_EPS = 1e-05

        def _rms_norm(x, w):
            v = jnp.mean(x * x, axis=-1, keepdims=True)
            return x * jax.lax.rsqrt(v + EPS_NORM) * w

        def _conv_silu(x, w, b):
            k = w.shape[1]
            xp = jnp.pad(x, ((0, 0), (k - 1, 0), (0, 0)))
            y = b
            for j in range(k):
                y = y + xp[:, j:j + x.shape[1], :] * w[:, j]
            return y * jax.nn.sigmoid(y)

        def _forward(x, rms_w, in_proj_w, in_proj_b, conv_w, conv_b, gate_w, gate_b, log_dt_scale, Q_w, readout_w, out_w, gn_w, gn_b, D_param):
            b, l, _ = x.shape
            di = conv_w.shape[0]
            h = log_dt_scale.shape[0]
            hd = di // h
            residual = x
            xn = _rms_norm(x, rms_w)
            proj = xn @ in_proj_w + in_proj_b
            z = proj[..., :di]
            x_gate = proj[..., di:2 * di]
            K = proj[..., 2 * di:3 * di].reshape(b, l, h, hd)
            V = proj[..., 3 * di:].reshape(b, l, h, 2)
            x_conv = _conv_silu(x_gate, conv_w, conv_b)
            gates = (x_conv @ gate_w + gate_b).reshape(b, l, 7, h)
            alpha_raw, omega_raw = (gates[..., 0, :], gates[..., 1, :])
            sel_B, sel_C = (gates[..., 2, :], gates[..., 3, :])
            sel_dt, beta_raw, r_raw = (gates[..., 4, :], gates[..., 5, :], gates[..., 6, :])
            freqs = 1.0 / ROPE_BASE ** (jnp.arange(h, dtype=jnp.float32) / h)
            dt = jax.nn.softplus(sel_dt) * jnp.exp(log_dt_scale) + EPS_DT
            alpha = jax.nn.softplus(alpha_raw)
            omega = freqs * (1.0 + jnp.tanh(omega_raw))
            ah, wh = (0.5 * dt * alpha, 0.5 * dt * omega)
            det = (1.0 + ah) ** 2 + wh ** 2
            c = (1.0 - ah ** 2 - wh ** 2) / det
            s = 2.0 * wh / det
            mag = jnp.sqrt(c * c + s * s)
            theta = jnp.arctan2(s, c)
            r = jax.nn.sigmoid(r_raw)
            mag2 = jnp.exp(GATING_C * r * jnp.log(jnp.clip(mag, 1e-08, 1.0)))
            cbar, sbar = (mag2 * jnp.cos(theta), mag2 * jnp.sin(theta))
            vp_scale = jax.nn.sigmoid(sel_B) * jnp.sqrt(jnp.clip(1.0 - mag2 ** 2, 0.0, 1.0) + 1e-06)
            beta = jax.nn.sigmoid(beta_raw)
            sel_C_gate = jax.nn.sigmoid(sel_C)
            Q = (x_conv @ Q_w).reshape(b, l, h, hd)
            K = K / (jnp.linalg.norm(K, axis=-1, keepdims=True) + 1e-06)
            Q = Q / (jnp.linalg.norm(Q, axis=-1, keepdims=True) + 1e-06)
            Vg = V * vp_scale[..., None]

            def step(S, inp):
                ct, st, kt, vt, bt = inp
                S0, S1 = (S[:, :, 0], S[:, :, 1])
                Sd = jnp.stack([ct[..., None] * S0 + st[..., None] * S1, -st[..., None] * S0 + ct[..., None] * S1], axis=2)
                pred = jnp.einsum('bhsd,bhd->bhs', Sd, kt)
                Sn = Sd + bt[:, :, None, None] * (vt - pred)[..., None] * kt[:, :, None, :]
                return (Sn, Sn)
            xs = (jnp.moveaxis(cbar, 1, 0), jnp.moveaxis(sbar, 1, 0), jnp.moveaxis(K, 1, 0), jnp.moveaxis(Vg, 1, 0), jnp.moveaxis(beta, 1, 0))
            S0 = jnp.zeros((b, h, 2, hd), dtype=x.dtype)
            _, Ys = jax.lax.scan(step, S0, xs)
            Y = jnp.moveaxis(Ys, 0, 1)
            retrieved = jnp.einsum('blhsd,blhd->blhs', Y, Q) * sel_C_gate[..., None]
            y = retrieved.reshape(b, l, h * 2) @ readout_w
            yf = y.astype(jnp.float32).reshape(b, l, GN_GROUPS, di // GN_GROUPS)
            mean = jnp.mean(yf, axis=(1, 3), keepdims=True)
            var = jnp.mean((yf - mean) ** 2, axis=(1, 3), keepdims=True)
            yn = ((yf - mean) * jax.lax.rsqrt(var + GN_EPS)).reshape(b, l, di)
            y = (yn * gn_w + gn_b).astype(x.dtype)
            y = y * (z * jax.nn.sigmoid(z))
            y = y + D_param * x_conv
            out = y @ out_w
            return residual + out
        return _forward(x, rms_w, in_proj_w, in_proj_b, conv_w, conv_b, gate_w, gate_b, log_dt_scale, Q_w, readout_w, out_w, gn_w, gn_b, D_param)

    def _L0_ffn_ref(x, kernel, bias, a, b):
        import jax, jax.numpy as jnp
        import numpy as np
        INT4_QMAX = 7.0

        def simulate_quantize_int4(w):
            scale = jnp.max(jnp.abs(w)) / INT4_QMAX
            q = jnp.clip(jnp.round(w / scale), -8.0, 7.0)
            return q * scale
        w = simulate_quantize_int4(kernel)
        y = jnp.einsum('bsd,df->bsf', x, w) + bias
        lora = jnp.einsum('bsr,rf->bsf', jnp.einsum('bsd,dr->bsr', x, a), b)
        return y + lora
    x = x + _L0_xattn_ref(_layernorm(x, axis=-1), ctx_1024, ctx_1024, mask_BxSxS2_bk1, L0_xattn_Wq, L0_xattn_bq, L0_xattn_Wk, L0_xattn_bk, L0_xattn_Wv, L0_xattn_bv, L0_xattn_Wo, L0_xattn_bo, 16)
    x = x + _L0_attn_ref(_layernorm(x, axis=-1), L0_attn_rms_w, L0_attn_in_proj_w, L0_attn_in_proj_b, L0_attn_conv_w, L0_attn_conv_b, L0_attn_gate_w, L0_attn_gate_b, L0_attn_log_dt_scale, L0_attn_Q_w, L0_attn_readout_w, L0_attn_out_w, L0_attn_gn_w, L0_attn_gn_b, L0_attn_D_param)
    x = x + _L0_ffn_ref(_layernorm(x, axis=-1), L0_ffn_kernel, L0_ffn_bias, L0_ffn_a, L0_ffn_b)
    return x

_drawn_inputs = setup_inputs


def setup_inputs(seed=0):
    import zlib

    import numpy as np

    out = dict(_drawn_inputs(seed))
    spreads = {'L0_xattn_bq': (0.0, 0.322),
     'L0_xattn_bk': (0.0, 0.8),
     'L0_xattn_bv': (0.0, 0.1),
     'L0_xattn_bo': (0.0, 0.1),
     'L0_attn_rms_w': (1.0, 0.2),
     'L0_attn_in_proj_b': (0.0, 0.1),
     'L0_attn_conv_b': (0.0, 0.1)}
    factors = {'L0_attn_log_dt_scale': 5.562, 'L0_ffn_a': 8.0, 'L0_ffn_b': 8.0}
    for name, (base, spread) in spreads.items():
        noise = np.random.default_rng([zlib.crc32(name.encode()), seed]).standard_normal(out[name].shape)
        drawn = base * np.exp(spread * noise) if base else spread * noise
        out[name] = jnp.asarray(drawn.astype(out[name].dtype))
    for name, factor in factors.items():
        out[name] = (out[name] * factor).astype(out[name].dtype)
    return out
```

```python
from contextlib import ExitStack

import concourse.bass as bass
from concourse import mybir

ALU = mybir.AluOpType
ACT = mybir.ActivationFunctionType
F32 = mybir.dt.float32
BF16 = mybir.dt.bfloat16
U8 = mybir.dt.uint8
U16 = mybir.dt.uint16
I32 = mybir.dt.int32
AX = mybir.AxisListType

P = 128
NB = 4
S = 128
DM = 128
NK = 2048
H = 16
DH = DM // H
BLK = 512
KT = BLK // P
TOK = NB * S
DI = 256
HD = DI // H
BIG = 1.0e30
SCALE = float(DH) ** -0.5
EPS_LN = 1e-5
EPS_RMS = 1e-6
GN = 16
LN2 = 0.6931471805599453
ONES_PAIR = 1.0 + 0x3F80 / 2.0 ** 23

NBLK = NK // BLK
UNITS = 2 * KT
ALL_MASKED = NB * (NK - BLK) // 2 * 0x0101
K_LEVEL = [0, 1, 2, 0, 1, 0]
Q_LEVEL = [0, 0, 0, 1, 1, 2]
NTERM = len(K_LEVEL)
MROW = NTERM * DH

VEC = {n: i for i, n in enumerate(
    ["bq", "bk", "rms", "xg_b0", "xg_b1", "k_b0", "k_b1", "z_b0", "z_b1", "v_b"]
    + [f"cw{i}{j}" for i in range(2) for j in range(4)]
    + ["cb0", "cb1", "gn_w0", "gn_w1", "gn_b0", "gn_b1", "d0", "d1", "gate_b", "log_dt", "freq", "sgn",
       "eps_ln", "eps_rms", "root_shift", "one"])}
NVEC = len(VEC)


def perceiver_kernel(nc, x, ctx_t, mask, wq, wk, wv, wo, vec, rows, ident, avg, w_in, w_gate, w_q, w_read,
                     w_out, ffn_w, ffn_at, ffn_b, out):
    ctx = ExitStack()
    with ctx:
        def sb(name, shape, dt=F32):
            return ctx.enter_context(nc.sbuf_tensor(name, shape, dt))

        def pb(name, shape, dt=F32):
            return ctx.enter_context(nc.psum_tensor(name, shape, dt))

        def sem(name):
            return ctx.enter_context(nc.semaphore(name))

        scratch = nc.dram_tensor("scratch", [2 * DI + 2 * H + 7 * H, TOK], F32, kind="Internal").ap()
        ROW_K, ROW_Q, ROW_V, ROW_G = 0, DI, 2 * DI, 2 * DI + 2 * H

        x_sb = sb("x_sb", [P, NB, DM])
        ctx_sb = sb("ctx_sb", [P, NB, BLK])
        mask_sb = sb("mask_sb", [P, NB, NK], U8)
        mask_bf = sb("mask_bf", [P, NB, BLK], BF16)
        mask_neg = sb("mask_neg", [P, NB, BLK])
        vec_sb = sb("vec_sb", [P, NVEC])
        rows_sb = sb("rows_sb", [P, 3, DM])
        id_sb = sb("id_sb", [P, P])
        id_bf = sb("id_bf", [P, P], BF16)
        neg_id4 = sb("neg_id4", [P, 4, P], BF16)
        avg_sb = sb("avg_sb", [P, P])
        wq_sb, wk_sb, wv_sb, wo_sb = (sb(n, [P, DM]) for n in ("wq_sb", "wk_sb", "wv_sb", "wo_sb"))
        w_in_sb = sb("w_in_sb", [P, 3 * DI + 2 * H])
        w_gate_sb = sb("w_gate_sb", [P, 2, 7 * H])
        w_q_sb = sb("w_q_sb", [P, 2, DI])
        w_rd = sb("w_rd", [P, NB, DI])
        w_rs = sb("w_rs", [P, NB, DI])
        w_out_sb = sb("w_out_sb", [P, 2, DM])
        fw_sb = sb("fw_sb", [P, DM])
        fat_sb = sb("fat_sb", [16, DM])
        fb_sb = sb("fb_sb", [16, DM])
        w_eff = sb("w_eff", [P, DM])
        stats = sb("stats", [P, NB, 6])
        mv = sb("mv", [P, NB, 2])
        lnv = sb("lnv", [P, NB])
        rstd = sb("rstd", [P, NB])
        xn = sb("xn", [P, NB, DM])
        xn_t = sb("xn_t", [P, TOK])
        xb = sb("xb", [P, NB, DM])
        q_f = sb("q_f", [P, TOK])
        q_r = sb("q_r", [P, TOK])
        q_split = sb("q_split", [P, 3, TOK], BF16)
        k_f = sb("k_f", [P, NB, BLK])
        k_r = sb("k_r", [P, BLK])
        k_split = sb("k_split", [P, NB, 3, BLK], BF16)
        q_stack = sb("q_stack", [P, H, TOK], BF16)
        k_stack = [sb(f"k_stack{b}", [P, H, BLK], BF16) for b in range(NB)]
        v_ones = sb("v_ones", [P, NB, KT, H, DH + 1])
        junk = sb("junk", [P, 2, BLK], BF16)
        mx = sb("mx", [P, NB, H])
        mflag = sb("mflag", [P, H])
        mneg = sb("mneg", [P, H])
        mrest = sb("mrest", [P, H])
        m_split = sb("m_split", [P, NB, 3 * H], BF16)
        m_t = sb("m_t", [3 * H, NB, S], BF16)
        probs = sb("probs", [P, 3, 8, S])
        probs_flat = probs[:, :, :, :].rearrange("p a h s -> p (a h s)")
        o_sb = sb("o_sb", [P, 2, 4 * S])
        rden = sb("rden", [P, H])
        attn = sb("attn", [P, 2, DM])
        attn_t = sb("attn_t", [P, 2, S])
        x1 = sb("x1", [P, NB, DM])

        def chain_view(stack, half):
            flat = stack[:, :, :].rearrange("p h k -> p (h k)").bitcast(F32)
            return flat[:, 2048 * half:2048 * (half + 1)]

        k_ch, q_ch = chain_view(k_stack[0], 0), chain_view(k_stack[0], 1)
        kc_ch, w_ch = chain_view(k_stack[1], 0), chain_view(k_stack[1], 1)
        y_ch, prod = chain_view(k_stack[2], 0), chain_view(k_stack[2], 1)
        sq = chain_view(k_stack[3], 0)
        by_t = lambda v: v.rearrange("p (d t) -> p d t", d=HD)
        xr = xn
        xr_t = xn_t
        ks_flat = k_split[:, :, :, :].rearrange("p b l k -> p (b l k)").bitcast(F32)
        ms = sb("ms", [P, NB])
        rms_r = sb("rms_r", [P, NB])
        rq2 = sb("rq2", [P, NB])
        x1h = ks_flat[:, 1024:1536].rearrange("p (b d) -> p b d", b=NB)
        hn = ks_flat[:, 1536:2048].rearrange("p (b d) -> p b d", b=NB)
        mask_flat = mask_sb[:, :, :].rearrange("p b k -> p (b k)").bitcast(F32)
        v_flat = v_ones[:, :, :, :, :].rearrange("p b t h e -> p (b t h e)")
        n_xg = 2 * NB * (S + 3)
        xg = mask_flat[:, 0:n_xg].rearrange("p (i b t) -> p i b t", i=2, b=NB)
        g_ch = mask_flat[:, n_xg:n_xg + 7 * S].rearrange("p (g t) -> p g t", g=7)
        pair = lambda flat, n: flat[:, 2 * S * n:2 * S * (n + 1)].rearrange("p (a t) -> p a t", a=2)
        two = lambda v: v.rearrange("p (i t) -> p i t", i=2)
        spare = chain_view(k_stack[3], 1)
        conv, sigc = two(spare[:, 0:2 * TOK]), two(spare[:, 2 * TOK:4 * TOK])
        ctx_flat = ctx_sb[:, :, :].rearrange("p b k -> p (b k)")
        xc, zs = two(ctx_flat[:, 0:2 * TOK]), two(ctx_flat[:, 2 * TOK:4 * TOK])
        neg_flat = mask_neg[:, :, :].rearrange("p b k -> p (b k)")
        sigz = two(neg_flat[:, 0:2 * TOK])
        kq_rows = k_f[:, :, :]
        v_rows = q_f[0:2 * H, :]
        g_rows = q_r[0:7 * H, :]
        v_own, v_swap = v_flat[:, 0:S], v_flat[:, S:2 * S]
        sig_bc, sig_br = pair(v_flat, 1), pair(v_flat, 2)
        sig_om = sb("sig_om", [P, S])
        names = ["nk", "lnk", "nrm", "rk", "nq", "lnq", "nrq", "rq", "dt", "ah", "ww", "w2", "s2", "p1", "n1", "den",
                 "num", "rdn", "ratio", "lr", "ell", "mm", "m2", "n1s", "nsq", "flag", "lnsq", "yy", "t1", "t2", "t3",
                 "c1", "l1", "rt", "vp", "vr1", "vr2", "vr3", "brk", "wt", "ct", "gq", "rr", "r2", "cc", "dd", "t4",
                 "t5", "t6", "t7", "t8"]
        q_flat = q_stack[:, :, :].rearrange("p h k -> p (h k)").bitcast(F32)
        room = [q_flat[:, S * i:S * (i + 1)] for i in range(32)] + [probs_flat[:, S * i:S * (i + 1)] for i in range(24)]
        T = dict(zip(names, room))
        ab, ee, uu, lnu, corr, sp = (pair(v_flat, 3 + i) for i in range(6))
        elds = sb("elds", [P, 1])
        ph = [pair(ks_flat, i) for i in range(2)]
        pa, pbb = pair(ks_flat, 2), pair(ks_flat, 3)
        grow = sb("grow", [P, 2, HD])
        gjunk = sb("gjunk", [P, 2, HD])
        pred = sb("pred", [P, 2])
        gst = sb("gst", [P, 8, 6])
        gmv = sb("gmv", [P, 8, 2])
        gmean = sb("gmean", [P, 8])
        gdm = sb("gdm", [P, 8])
        gdv = sb("gdv", [P, 8])
        gln = sb("gln", [P, 8])
        grs = sb("grs", [P, 8])
        gsc = sb("gsc", [P, 8])
        gbi = sb("gbi", [P, 8])
        yn = sigc
        y2 = conv
        x2 = xb
        x2b = x1h
        am = sb("am", [P, 1])
        amx = sb("amx", [P, 1])
        fsc = sb("fsc", [P, 1])
        finv = sb("finv", [P, 1])
        fq = sb("fq", [P, DM])
        res = ks_flat[:, 2048:2560].rearrange("p (b d) -> p b d", b=NB)

        mask_sum = sb("mask_sum", [P, 1])
        some_open = sb("some_open", [P, 1])
        go_general = sb("go_general", [1, 1], I32)
        q_cur = k_stack[1][:, :, 0:S]
        q_raw = k_stack[2][:, :, 0:S]
        m_blk = sb("m_blk", [P, H])
        m_run = sb("m_run", [P, H])
        m_new = sb("m_new", [P, H])
        fade_arg = sb("fade_arg", [P, H])
        fade = sb("fade", [P, H])
        o_run = sb("o_run", [P, H, DH + 1])

        SA = [pb(f"SA{i}", [P, BLK]) for i in range(2)]
        SB = [pb(f"SB{i}", [P, 2, BLK]) for i in range(2)]
        MI = pb("MI", [P, BLK])
        OT = pb("OT", [P, BLK])

        s_x, s_vec, s_id, s_wq, s_wk, s_wv, s_wo, s_rows = (sem(n) for n in (
            "s_x", "s_vec", "s_id", "s_wq", "s_wk", "s_wv", "s_wo", "s_rows"))
        s_ctx = [sem(f"s_ctx{b}") for b in range(NB)]
        s_mask = sem("s_mask")
        s_late = sem("s_late")
        dve_early = sem("dve_early")
        kst0_filled = sem("kst0_filled")
        kst_filled = sem("kst_filled")
        qst_filled = sem("qst_filled")
        ot_zeroed = sem("ot_zeroed")
        consts_ready = sem("consts_ready")
        mask_ready = sem("mask_ready")
        v_ones_set = sem("v_ones_set")
        ln_var = sem("ln_var")
        ln_rstd = sem("ln_rstd")
        xn_ready = sem("xn_ready")
        xnT_done = sem("xnT_done")
        xnT_copied = sem("xnT_copied")
        q_done = sem("q_done")
        q_copied = sem("q_copied")
        q_split_done = sem("q_split_done")
        q_stacked = sem("q_stacked")
        k_done = sem("k_done")
        k_copied = sem("k_copied")
        k_split_done = sem("k_split_done")
        k_stacked = [sem(f"k_stacked{b}") for b in range(NB)]
        v_done = sem("v_done")
        v_copied = sem("v_copied")
        score_done = sem("score_done")
        max_done = sem("max_done")
        mneg_done = sem("mneg_done")
        mT_done = sem("mT_done")
        mT_copied = sem("mT_copied")
        m_stacked = sem("m_stacked")
        unit_scored = sem("unit_scored")
        unit_exp = sem("unit_exp")
        unit_pv = sem("unit_pv")
        o_copied = sem("o_copied")
        oT_done = sem("oT_done")
        attn_done = sem("attn_done")
        aT_done = sem("aT_done")
        aT_copied = sem("aT_copied")
        wo_done = sem("wo_done")
        x1_done = sem("x1_done")
        stored = sem("stored")
        act_done = sem("act_done")
        xb_done = sem("xb_done")

        ms_done = sem("ms_done")
        rms_done = sem("rms_done")
        xg_done = sem("xg_done")
        xg_copied = sem("xg_copied")
        kp_done = sem("kp_done")
        kp_copied = sem("kp_copied")
        vp_done = sem("vp_done")
        vp_copied = sem("vp_copied")
        z_done = sem("z_done")
        conv_done = sem("conv_done")
        sigc_done = sem("sigc_done")
        xc_done = sem("xc_done")
        sigz_done = sem("sigz_done")
        gate_done = sem("gate_done")
        gate_copied = sem("gate_copied")
        qp_done = sem("qp_done")
        qp_copied = sem("qp_copied")
        pad_zeroed = sem("pad_zeroed")
        k_stored = sem("k_stored")
        v_stored = sem("v_stored")
        g_stored = sem("g_stored")
        q_stored = sem("q_stored")
        k_loaded = sem("k_loaded")
        v_loaded = sem("v_loaded")
        g_loaded = sem("g_loaded")
        q_loaded = sem("q_loaded")
        ksq_done = sem("ksq_done")
        qsq_done = sem("qsq_done")
        nk_done = sem("nk_done")
        nq_done = sem("nq_done")
        knorm_done = sem("knorm_done")
        qnorm_done = sem("qnorm_done")
        abs_done = sem("abs_done")
        u_done = sem("u_done")
        ratio_done = sem("ratio_done")
        nsq_done = sem("nsq_done")
        ell_done = sem("ell_done")
        c1_done = sem("c1_done")
        parts_done = sem("parts_done")
        y_done = sem("y_done")
        gst_done = sem("gst_done")
        gm_done = sem("gm_done")
        gdv_done = sem("gdv_done")
        gv_done = sem("gv_done")
        grs_done = sem("grs_done")
        gbi_done = sem("gbi_done")
        yn_done = sem("yn_done")
        y2_done = sem("y2_done")
        o2_done = sem("o2_done")
        x2_done = sem("x2_done")
        ffn_done = sem("ffn_done")
        res_done = sem("res_done")
        am_done = sem("am_done")
        amx_done = sem("amx_done")
        ab_mm_done = sem("ab_mm_done")
        wrs_done = sem("wrs_done")
        h2_done = sem("h2_done")
        x1h_done = sem("x1h_done")
        sig_g = sem("sig_g")
        exp_g = sem("exp_g")
        ln_g = sem("ln_g")
        mm_g = sem("mm_g")
        sum_done = sem("sum_done")
        open_done = sem("open_done")
        count_done = sem("count_done")
        flag_done = sem("flag_done")
        g_ctx = sem("g_ctx")
        g_mask = sem("g_mask")
        g_kproj = sem("g_kproj")
        g_kcopied = sem("g_kcopied")
        g_ksplit = sem("g_ksplit")
        g_kstacked = sem("g_kstacked")
        g_vproj = sem("g_vproj")
        g_vcopied = sem("g_vcopied")
        g_maskset = sem("g_maskset")
        g_q = sem("g_q")
        g_masked = sem("g_masked")
        g_fade_arg = sem("g_fade_arg")
        g_fade = sem("g_fade")
        g_merged = sem("g_merged")
        g_step = sem("g_step")
        dve_post = sem("dve_post")

        def col(name, n=P):
            return vec_sb[0:n, VEC[name]:VEC[name] + 1]

        block = ctx.enter_context(nc.Block())

        @block.sync
        def _(sp):
            sp.dma_start(x_sb[:, :, :], x.rearrange("b s d -> s b d")).then_inc(s_x, 16)
            sp.dma_start(wk_sb[:, :], wk).then_inc(s_wk, 16)
            sp.dma_start(ctx_sb[:, 0, :], ctx_t[0, :, NK - BLK:NK]).then_inc(s_ctx[0], 16)
            sp.dma_start(wq_sb[:, :], wq).then_inc(s_wq, 16)
            for b in range(1, NB):
                sp.dma_start(ctx_sb[:, b, :], ctx_t[b, :, NK - BLK:NK]).then_inc(s_ctx[b], 16)
            sp.dma_start(wv_sb[:, :], wv).then_inc(s_wv, 16)
            for b in range(NB):
                sp.wait_ge(k_split_done, b + 1)
                sp.wait_ge(kst_filled if b else kst0_filled, max(b, 1))
                for t in range(NTERM):
                    sp.dma_start(k_stack[b][DH * t:DH * (t + 1), :, :], k_split[:, b, K_LEVEL[t], :])\
                      .then_inc(k_stacked[b], 16)
            for dst, src in ((w_in_sb[:, :], w_in), (w_gate_sb[:, :, :], w_gate), (w_q_sb[:, :, :], w_q),
                             (w_rd[:, :, :], w_read[0]), (w_rs[:, :, :], w_read[1]), (w_out_sb[:, :, :], w_out),
                             (fw_sb[:, :], ffn_w), (fat_sb[:, :], ffn_at), (fb_sb[:, :], ffn_b), (avg_sb[:, :], avg)):
                sp.dma_start(dst, src).then_inc(s_late, 16)
            sp.wait_ge(flag_done, 1)
            with sp.If(sp.value_load(go_general[0:1, 0:1]) != 0):
                for b in range(NB):
                    sp.wait_ge(k_stacked[b], 16 * NTERM)
                sp.wait_ge(mask_ready, NB)
                with sp.Fori(0, NB) as b:
                    with sp.Fori(0, NBLK) as k:
                        n = b * NBLK + k
                        sp.wait_ge(g_merged, n + 1)
                        sp.dma_start(ctx_sb[:, 0, :], ctx_t[bass.ds(b, 1), :, bass.ds(k * BLK, BLK)]
                                     .rearrange("o d k -> d (o k)")).then_inc(g_ctx, 16)
                        sp.dma_start(mask_sb[:, 0, 0:BLK], mask[bass.ds(b, 1), :, bass.ds(k * BLK, BLK)]
                                     .rearrange("o q k -> q (o k)")).then_inc(g_mask, 16)
                        sp.wait_ge(g_ksplit, n + 1)
                        for t in range(NTERM):
                            sp.dma_start(k_stack[0][DH * t:DH * (t + 1), :, :], k_split[:, 0, K_LEVEL[t], :])\
                              .then_inc(g_kstacked, 16)
                        sp.wait_ge(mT_copied, n + 1)
                        sp.dma_start(q_cur[MROW:MROW + 3, :, :], m_t[:, 0, :]).then_inc(m_stacked, 16)
            with sp.Else():
                sp.nop()
            sp.nop()
            sp.wait_ge(kp_copied, 2)
            sp.dma_start(scratch[ROW_K:ROW_K + DI, :].rearrange("(i p) t -> p i t", i=2), kq_rows[:, 0:2, :])\
                .then_inc(k_stored, 16)
            sp.wait_ge(vp_copied, 1)
            sp.dma_start(scratch[ROW_V:ROW_V + 2 * H, :], v_rows).then_inc(v_stored, 16)
            sp.wait_ge(k_stored, 16)
            for s in range(2):
                sp.dma_start(k_ch[64 * s:64 * (s + 1), :],
                             scratch[ROW_K:ROW_K + DI, :].rearrange("(h d) (b t) -> b h d t", d=HD, b=NB))\
                    .then_inc(k_loaded, 16)
            sp.wait_ge(gate_copied, 1)
            sp.dma_start(scratch[ROW_G:ROW_G + 7 * H, :], g_rows).then_inc(g_stored, 16)
            sp.wait_ge(v_stored, 16)
            v_src = scratch[ROW_V:ROW_V + 2 * H, :].rearrange("(h s) (b t) -> s b h t", s=2, b=NB)
            for s in range(2):
                sp.dma_start(v_own[64 * s:64 * (s + 1), :], v_src[s]).then_inc(v_loaded, 16)
                sp.dma_start(v_swap[64 * s:64 * (s + 1), :], v_src[1 - s]).then_inc(v_loaded, 16)
            sp.wait_ge(g_stored, 16)
            for s in range(2):
                sp.dma_start(g_ch[64 * s:64 * (s + 1), :, :],
                             scratch[ROW_G:ROW_G + 7 * H, :].rearrange("(h g) (b t) -> b h g t", g=7, b=NB))\
                    .then_inc(g_loaded, 16)
            sp.wait_ge(qp_copied, 2)
            sp.dma_start(scratch[ROW_Q:ROW_Q + DI, :].rearrange("(i p) t -> p i t", i=2), kq_rows[:, 2:4, :])\
                .then_inc(q_stored, 16)
            sp.wait_ge(q_stored, 16)
            for s in range(2):
                sp.dma_start(q_ch[64 * s:64 * (s + 1), :],
                             scratch[ROW_Q:ROW_Q + DI, :].rearrange("(h d) (b t) -> b h d t", d=HD, b=NB))\
                    .then_inc(q_loaded, 16)
            sp.wait_ge(res_done, 1)
            sp.dma_start(out.rearrange("b s d -> s b d"), res[:, :, :]).then_inc(stored, 16)
            sp.wait_ge(stored, 16)

        @block.gpsimd
        def _(pool):
            pool.memset(q_stack[:, :, :].bitcast(F32), 0.0).then_inc(qst_filled, 1)
            pool.memset(v_ones[:, :, :, :, DH:DH + 1], 1.0).then_inc(v_ones_set, 1)
            pool.memset(k_stack[1][:, :, :].bitcast(F32), ONES_PAIR).then_inc(kst_filled, 1)
            pool.wait_ge(q_split_done, 1)
            pool.wait_ge(qst_filled, 1)
            for t in range(NTERM):
                pool.dma_start(q_stack[DH * t:DH * (t + 1), :, :], q_split[:, Q_LEVEL[t], :])\
                    .then_inc(q_stacked, 16)
            for b in range(NB):
                pool.wait_ge(s_mask, 16 * NB)
                last = NK - BLK
                pool.tensor_scalar(mask_neg[:, b, :], mask_sb[:, b, last:NK], -BIG, 1.0, ALU.mult, ALU.mult)
                pool.tensor_scalar(mask_bf[:, b, :], mask_sb[:, b, last:NK], 1.0, 1.0, ALU.mult, ALU.mult)\
                    .then_inc(mask_ready, 1)
            for b in (2, 3):
                pool.memset(k_stack[b][:, :, :].bitcast(F32), ONES_PAIR).then_inc(kst_filled, 1)
            pool.wait_ge(s_x, 16)
            pool.wait_ge(s_rows, 16)
            for b in range(NB):
                pool.tensor_tensor(xb[:, b, :], x_sb[:, b, :], rows_sb[:, 1, :], ALU.add).then_inc(xb_done, 1)
            pool.wait_ge(flag_done, 1)
            with pool.If(pool.value_load(go_general[0:1, 0:1]) != 0):
                pool.nop()
            with pool.Else():
                for b in range(NB):
                    pool.wait_ge(mT_copied, b + 1)
                    pool.dma_start(q_stack[MROW:MROW + 3, :, S * b:S * (b + 1)], m_t[:, b, :]).then_inc(m_stacked, 16)

            pool.nop()
            pool.wait_ge(x1_done, NB)
            pool.memset(xg[:, :, :, 0:3], 0.0).then_inc(pad_zeroed, 1)
            pool.wait_ge(s_late, 160)
            pool.tensor_scalar(w_rs[:, :, :], w_rs[:, :, :], col("sgn"), 1.0, ALU.mult, ALU.mult).then_inc(wrs_done, 1)
            pool.wait_ge(am_done, 1)
            pool.partition_all_reduce(amx[:, :], am[:, :], P, bass.bass_isa.ReduceOp.max).then_inc(amx_done, 1)
            pool.wait_ge(h2_done, NB)
            pool.tensor_tensor(x1h[:, :, :], x1[:, :, :], hn[:, :, :], ALU.add).then_inc(x1h_done, 1)

        @block.scalar
        def _(act):
            act.dma_start(vec_sb[:, :], vec).then_inc(s_vec, 16)
            act.dma_start(id_sb[:, :], ident).then_inc(s_id, 16)
            for b in range(NB):
                act.dma_start(mask_sb[:, b, :], mask[b]).then_inc(s_mask, 16)
            act.dma_start(rows_sb[:, :, :], rows).then_inc(s_rows, 16)
            act.dma_start(wo_sb[:, :], wo).then_inc(s_wo, 16)

            act.preload_act_table_set("natural_log_exp_and_others")
            act.wait_ge(s_vec, 16)
            act.wait_ge(ln_var, 1)
            nc.scalar.activation(lnv[:, :], mv[:, :, 1], ACT.Ln, bias=col("eps_ln")).then_inc(act_done, 1)
            act.wait_ge(act_done, 1)
            nc.scalar.activation(rstd[:, :], lnv[:, :], ACT.Exp, scale=-0.5).then_inc(ln_rstd, 1)

            def k_evac(b):
                act.wait_ge(k_done, b + 1)
                src = SB[b // 2][:, b % 2, :]
                nc.scalar.activation(k_f[:, b, :], src, ACT.Identity, bias=col("bk")).then_inc(k_copied, 1)
                nc.scalar.activation(k_split[:, b, 0, :], src, ACT.Identity, bias=col("bk")).then_inc(k_copied, 1)

            k_evac(0)
            act.wait_ge(xnT_done, 1)
            nc.scalar.activation(xn_t[:, :], MI[:, :], ACT.Copy).then_inc(xnT_copied, 1)
            k_evac(1)
            act.wait_ge(q_done, 1)
            nc.scalar.activation(q_f[:, :], SA[0][:, :], ACT.Identity, bias=col("bq")).then_inc(q_copied, 1)
            nc.scalar.activation(q_split[:, 0, :], SA[0][:, :], ACT.Identity, bias=col("bq")).then_inc(q_copied, 1)
            k_evac(2)
            k_evac(3)
            act.wait_ge(s_mask, 16 * NB)
            nc.scalar.activation(probs_flat.bitcast(BF16)[:, 0:NB * (NK - BLK) // 2].rearrange("p (b k) -> p b k", b=NB),
                                 mask_sb[:, :, 0:NK - BLK].bitcast(U16), ACT.Copy, accum_out=mask_sum[:, :])\
                .then_inc(sum_done, 1)

            def m_evac(b):
                act.wait_ge(mT_done, b + 1)
                nc.scalar.activation(m_t[:, b, :], MI[0:3 * H, 0:S // 2].bitcast(BF16), ACT.Copy).then_inc(mT_copied, 1)

            def general_block(n):
                act.wait_ge(g_kproj, n + 1)
                for dst in (k_f[:, 0, :], k_split[:, 0, 0, :]):
                    nc.scalar.activation(dst, SB[0][:, 0, :], ACT.Identity, bias=col("bk")).then_inc(g_kcopied, 1)
                act.wait_ge(g_fade_arg, n + 1)
                nc.scalar.activation(fade[:, :], fade_arg[:, :], ACT.Exp, scale=SCALE).then_inc(g_fade, 1)
                act.wait_ge(mT_done, n + 1)
                nc.scalar.activation(m_t[:, 0, :], MI[0:3 * H, 0:S], ACT.Copy).then_inc(mT_copied, 1)
                for u in range(UNITS):
                    act.wait_ge(unit_scored, n * UNITS + u + 1)
                    if u >= 2:
                        act.wait_ge(unit_pv, n * UNITS + u - 1)
                    nc.scalar.activation(probs[:, u % 2, :, :],
                                         SB[u % 2][:, :, :].rearrange("p a (c s) -> p (a c) s", c=4),
                                         ACT.Exp, scale=SCALE).then_inc(unit_exp, 1)
                act.wait_ge(unit_pv, n * UNITS + UNITS)
                nc.scalar.activation(o_sb[:, 0, :], OT[:, :], ACT.Copy).then_inc(o_copied, 1)

            act.wait_ge(flag_done, 1)
            with act.If(act.value_load(go_general[0:1, 0:1]) != 0):
                with act.Fori(0, NB) as b:
                    with act.Fori(0, NBLK) as k:
                        general_block(b * NBLK + k)
                    act.wait_ge(aT_done, b + 1)
                    nc.scalar.activation(attn_t[:, 0, :], MI[:, 0:S], ACT.Copy).then_inc(aT_copied, 1)
            with act.Else():
                m_evac(0)
                for b in range(NB):
                    for u in range(8):
                        n = 8 * b + u
                        act.wait_ge(unit_scored, n + 1)
                        if n >= 3:
                            act.wait_ge(unit_pv, n - 2)
                        nc.scalar.activation(probs[:, n % 3, :, :], SB[n % 2][:, :, :].rearrange("p a (c s) -> p (a c) s", c=4),
                                             ACT.Exp, scale=SCALE).then_inc(unit_exp, 1)
                        if u == 3 and b >= 1:
                            act.wait_ge(aT_done, b)
                            nc.scalar.activation(attn_t[:, (b - 1) % 2, :], MI[:, 0:S], ACT.Copy).then_inc(aT_copied, 1)
                        if u == 6 and b + 1 < NB:
                            m_evac(b + 1)
                    act.wait_ge(unit_pv, 8 * b + 8)
                    nc.scalar.activation(o_sb[:, b % 2, :], OT[:, :], ACT.Copy).then_inc(o_copied, 1)
                act.wait_ge(aT_done, NB)
                nc.scalar.activation(attn_t[:, (NB - 1) % 2, :], MI[:, 0:S], ACT.Copy).then_inc(aT_copied, 1)

            act.nop()

            def root_recip(dst, tmp, src, eps, ready, value, done):
                act.wait_ge(ready, value)
                n = act_n[0] = act_n[0] + 1
                nc.scalar.activation(tmp, src, ACT.Ln, bias=eps).then_inc(act_done, 1)
                act.wait_ge(act_done, n)
                nc.scalar.activation(dst, tmp, ACT.Exp, scale=-0.5).then_inc(done, 1)

            act_n = [1]
            root_recip(rstd[:, :], lnv[:, :], mv[:, :, 1], col("eps_ln"), ln_var, 2, ln_rstd)
            root_recip(rms_r[:, :], lnv[:, :], ms[:, :], col("eps_rms"), ms_done, 1, rms_done)
            act.wait_ge(xnT_done, 2)
            nc.scalar.activation(xr_t[:, :], MI[:, :], ACT.Copy, scale=col("rms")).then_inc(xnT_copied, 1)
            act.wait_ge(pad_zeroed, 1)
            for i in range(2):
                act.wait_ge(xg_done, i + 1)
                nc.scalar.activation(xg[:, i, :, 3:], SB[0][:, i, :].rearrange("p (b t) -> p b t", b=NB), ACT.Identity,
                                     bias=col(f"xg_b{i}")).then_inc(xg_copied, 1)
            for i in range(2):
                act.wait_ge(conv_done, i + 1)
                nc.scalar.activation(sigc[:, i, :], conv[:, i, :], ACT.Sigmoid).then_inc(sigc_done, 1)
            for i in range(2):
                act.wait_ge(z_done, i + 1)
                nc.scalar.activation(sigz[:, i, :], (SA[1], OT)[i][:, :], ACT.Sigmoid, bias=col(f"z_b{i}"))\
                    .then_inc(sigz_done, 1)
            act.wait_ge(gate_done, 1)
            nc.scalar.activation(g_rows, MI[0:7 * H, :], ACT.Identity, bias=col("gate_b", 7 * H)).then_inc(gate_copied, 1)
            act.wait_ge(qp_done, 2)
            nc.scalar.activation(kq_rows[:, 3, :], SB[0][:, 1, :], ACT.Copy).then_inc(qp_copied, 1)
            act.wait_ge(k_loaded, 32)
            nc.scalar.activation(sq, k_ch, ACT.Square).then_inc(ksq_done, 1)
            act.wait_ge(g_loaded, 32)
            nc.scalar.activation(sig_om[:, :], g_ch[:, 1, :], ACT.Sigmoid, scale=2.0).then_inc(sig_g, 1)
            nc.scalar.activation(sig_bc[:, :, :], g_ch[:, 2:4, :], ACT.Sigmoid).then_inc(sig_g, 1)
            nc.scalar.activation(sig_br[:, :, :], g_ch[:, 5:7, :], ACT.Sigmoid).then_inc(sig_g, 1)
            nc.scalar.activation(ab[:, :, :], g_ch[:, 0:5:4, :], ACT.Abs).then_inc(abs_done, 1)
            act.wait_ge(abs_done, 1)
            nc.scalar.activation(ee[:, :, :], ab[:, :, :], ACT.Exp, scale=-1.0).then_inc(exp_g, 1)
            nc.scalar.activation(elds[:, :], col("log_dt"), ACT.Exp).then_inc(exp_g, 1)
            act.wait_ge(u_done, 1)
            nc.scalar.activation(lnu[:, :, :], uu[:, :, :], ACT.Ln).then_inc(ln_g, 1)

            def root(dst, tmp, src, ready, done):
                act.wait_ge(ready, 1)
                n = act_n[0] = act_n[0] + 1
                nc.scalar.activation(tmp, src, ACT.Ln, scale=2.0 ** 30).then_inc(act_done, 1)
                act.wait_ge(act_done, n)
                nc.scalar.activation(dst, tmp, ACT.Exp, scale=0.5, bias=col("root_shift")).then_inc(done, 1)

            root(T["nrm"][:, :], T["lnk"][:, :], T["nk"][:, :], nk_done, knorm_done)
            act.wait_ge(ratio_done, 1)
            nc.scalar.activation(T["lr"][:, :], T["ratio"][:, :], ACT.Ln).then_inc(ln_g, 1)
            act.wait_ge(nsq_done, 1)
            n = act_n[0] = act_n[0] + 1
            nc.scalar.activation(T["lnsq"][:, :], T["nsq"][:, :], ACT.Ln).then_inc(act_done, 1)
            act.wait_ge(act_done, n)
            nc.scalar.activation(T["yy"][:, :], T["lnsq"][:, :], ACT.Exp, scale=-0.5).then_inc(mm_g, 1)
            act.wait_ge(ell_done, 1)
            nc.scalar.activation(T["mm"][:, :], T["ell"][:, :], ACT.Exp).then_inc(mm_g, 1)
            nc.scalar.activation(T["m2"][:, :], T["ell"][:, :], ACT.Exp, scale=2.0).then_inc(mm_g, 1)
            act.wait_ge(c1_done, 1)
            n = act_n[0] = act_n[0] + 1
            nc.scalar.activation(T["l1"][:, :], T["c1"][:, :], ACT.Ln).then_inc(act_done, 1)
            act.wait_ge(act_done, n)
            nc.scalar.activation(T["rt"][:, :], T["l1"][:, :], ACT.Exp, scale=0.5).then_inc(mm_g, 1)
            act.wait_ge(q_loaded, 32)
            act.wait_ge(nk_done, 1)
            nc.scalar.activation(sq, q_ch, ACT.Square).then_inc(qsq_done, 1)
            root(T["nrq"][:, :], T["lnq"][:, :], T["nq"][:, :], nq_done, qnorm_done)
            root_recip(grs[:, :], gln[:, :], MI[:, 8:16], col("eps_ln"), gv_done, 1, grs_done)
            for i in range(2):
                act.wait_ge(gbi_done, i + 1)
                for b in range(NB):
                    j = NB * i + b
                    nc.scalar.activation(yn[:, i, S * b:S * (b + 1)], SB[0][:, i, S * b:S * (b + 1)], ACT.Identity,
                                         scale=gsc[:, j:j + 1], bias=gbi[:, j:j + 1]).then_inc(yn_done, 1)
            root_recip(rstd[:, :], lnv[:, :], mv[:, :, 1], col("eps_ln"), ln_var, 3, ln_rstd)
            act.wait_ge(xnT_done, 3)
            nc.scalar.activation(xn_t[:, :], MI[:, :], ACT.Copy).then_inc(xnT_copied, 1)

        @block.vector
        def _(dve):
            count = [0]
            dve_done = dve_early

            def step(ins):
                count[0] += 1
                ins.then_inc(dve_done, 1)

            def link(ins):
                step(ins)
                dve.wait_ge(dve_done, count[0])

            nc.vector.memset(OT[:, :], 0.0).then_inc(ot_zeroed, 1)
            nc.vector.memset(k_stack[0][:, :, :].bitcast(F32), ONES_PAIR).then_inc(kst0_filled, 1)
            dve.wait_ge(s_x, 16)
            for b in range(NB):
                step(nc.vector.bn_stats(stats[:, b, :], x_sb[:, b, :]))
            dve.wait_ge(dve_done, count[0])
            for b in range(NB):
                last = nc.vector.bn_aggr(mv[:, b, :], stats[:, b, :])
                if b < NB - 1:
                    step(last)
            last.then_inc(ln_var, 1)
            dve.wait_ge(dve_done, count[0])
            dve.wait_ge(s_id, 16)
            link(nc.vector.tensor_copy(id_bf[:, :], id_sb[:, :]))
            for j in range(4):
                nc.vector.tensor_scalar(neg_id4[:, j, :], id_sb[:, :], -BIG, None, ALU.mult).then_inc(consts_ready, 1)
            dve.wait_ge(ln_rstd, 1)
            for b in range(NB):
                nc.vector.tensor_scalar(xn[:, b, :], x_sb[:, b, :], mv[:, b, 0:1], rstd[:, b:b + 1],
                                        ALU.subtract, ALU.mult).then_inc(xn_ready, 1)

            def k_levels(b):
                dve.wait_ge(k_copied, 2 * b + 2)
                link(nc.vector.tensor_tensor(k_r[:, :], k_f[:, b, :], k_split[:, b, 0, :], ALU.subtract))
                link(nc.vector.tensor_copy(k_split[:, b, 1, :], k_r[:, :]))
                nc.vector.tensor_tensor(k_split[:, b, 2, :], k_r[:, :], k_split[:, b, 1, :], ALU.subtract)\
                    .then_inc(k_split_done, 1)
                dve.wait_ge(k_split_done, b + 1)

            def v_evac(b, src):
                dve.wait_ge(v_done, b + 1)
                nc.vector.tensor_tensor(
                    v_ones[:, b, :, :, 0:DH], src.rearrange("p (t h d) -> p t h d", t=KT, h=H),
                    rows_sb[:, 0, :].rearrange("p (o h d) -> p o h d", o=1, h=H).to_broadcast([P, KT, H, DH]),
                    ALU.add).then_inc(v_copied, 1)

            k_levels(0)
            dve.wait_ge(q_copied, 2)
            link(nc.vector.tensor_tensor(q_r[:, :], q_f[:, :], q_split[:, 0, :], ALU.subtract))
            link(nc.vector.tensor_copy(q_split[:, 1, :], q_r[:, :]))
            nc.vector.tensor_tensor(q_split[:, 2, :], q_r[:, :], q_split[:, 1, :], ALU.subtract).then_inc(q_split_done, 1)
            dve.wait_ge(s_rows, 16)
            dve.wait_ge(v_ones_set, 1)
            k_levels(1)
            v_evac(0, SA[0][:, :])
            v_evac(1, SA[1][:, :])
            k_levels(2)
            v_evac(2, MI[:, :])
            k_levels(3)
            v_evac(3, SA[0][:, :])

            dve.wait_ge(sum_done, 1)
            nc.vector.tensor_scalar(some_open[:, :], mask_sum[:, :], float(ALL_MASKED), None, ALU.is_lt).then_inc(open_done, 1)
            dve.wait_ge(count_done, 1)
            nc.vector.tensor_copy(go_general[:, :], SA[1][0:1, 0:1]).then_inc(flag_done, 1)

            def head_max(n):
                b, h = divmod(n, H)
                dve.wait_ge(score_done, n + 1)
                if h == 0:
                    dve.wait_ge(mask_ready, b + 1)
                if n >= 2:
                    dve.wait_ge(max_done, n - 1)
                nc.vector.tensor_tensor_reduce(junk[:, n % 2, :], SA[n % 2][:, :], mask_neg[:, b, :], 1.0, -3.0e38,
                                               ALU.add, ALU.max, mx[:, b, h:h + 1]).then_inc(max_done, 1)

            def negate_max(b):
                dve.wait_ge(max_done, H * (b + 1))
                link(nc.vector.tensor_scalar(mflag[:, :], mx[:, b, :], -0.5 * BIG, 2.0 * BIG, ALU.is_lt, ALU.mult))
                link(nc.vector.scalar_tensor_tensor(mneg[:, :], mx[:, b, :], -1.0, mflag[:, :], ALU.mult, ALU.subtract))
                link(nc.vector.tensor_copy(m_split[:, b, 0:H], mneg[:, :]))
                link(nc.vector.tensor_tensor(mrest[:, :], mneg[:, :], m_split[:, b, 0:H], ALU.subtract))
                link(nc.vector.tensor_copy(m_split[:, b, H:2 * H], mrest[:, :]))
                nc.vector.tensor_tensor(m_split[:, b, 2 * H:3 * H], mrest[:, :], m_split[:, b, H:2 * H], ALU.subtract)\
                    .then_inc(mneg_done, 1)
                dve.wait_ge(mneg_done, b + 1)

            def normalise(b):
                dve.wait_ge(oT_done, b + 1)
                o_v = MI[:, :].rearrange("p (h e) -> p h e", h=H)
                link(nc.vector.reciprocal(rden[:, :].rearrange("p (h e) -> p h e", e=1), o_v[:, :, DH:DH + 1]))
                nc.vector.tensor_tensor(attn[:, b % 2, :].rearrange("p (h d) -> p h d", h=H), o_v[:, :, 0:DH],
                                        rden[:, :].rearrange("p (h e) -> p h e", e=1).to_broadcast([P, H, DH]),
                                        ALU.mult).then_inc(attn_done, 1)

            def residual(b):
                dve.wait_ge(wo_done, b + 1)
                dve.wait_ge(xb_done, NB)
                nc.vector.tensor_tensor(x1[:, b, :], MI[:, 0:DM], xb[:, b, :], ALU.add).then_inc(x1_done, 1)

            dve.wait_ge(flag_done, 1)
            V = nc.vector

            def general_block(n):
                dve.wait_ge(g_merged, n + 1)
                dve.wait_ge(g_kcopied, 2 * n + 2)
                g_n = n * 15
                V.tensor_tensor(k_r[:, :], k_f[:, 0, :], k_split[:, 0, 0, :], ALU.subtract).then_inc(g_step, 1)
                dve.wait_ge(g_step, g_n + 1)
                V.tensor_copy(k_split[:, 0, 1, :], k_r[:, :]).then_inc(g_step, 1)
                dve.wait_ge(g_step, g_n + 2)
                V.tensor_tensor(k_split[:, 0, 2, :], k_r[:, :], k_split[:, 0, 1, :], ALU.subtract).then_inc(g_ksplit, 1)
                dve.wait_ge(g_vproj, n + 1)
                V.tensor_tensor(v_ones[:, 0, :, :, 0:DH], MI[:, :].rearrange("p (t h d) -> p t h d", t=KT, h=H),
                                rows_sb[:, 0, :].rearrange("p (o h d) -> p o h d", o=1, h=H).to_broadcast([P, KT, H, DH]),
                                ALU.add).then_inc(g_vcopied, 1)
                dve.wait_ge(g_mask, 16 * n + 16)
                V.tensor_scalar(mask_neg[:, 0, :], mask_sb[:, 0, 0:BLK], -BIG, None, ALU.mult).then_inc(g_step, 1)
                V.tensor_scalar(mask_bf[:, 0, :], mask_sb[:, 0, 0:BLK], 1.0, None, ALU.mult).then_inc(g_maskset, 1)
                dve.wait_ge(g_step, g_n + 3)
                for h in range(H):
                    dve.wait_ge(score_done, n * H + h + 1)
                    if h >= 2:
                        dve.wait_ge(max_done, n * H + h - 1)
                    masked = probs_flat[:, BLK * (h % 2):BLK * (h % 2) + BLK]
                    V.tensor_tensor(masked, SA[h % 2][:, :], mask_neg[:, 0, :], ALU.add).then_inc(g_masked, 1)
                    dve.wait_ge(g_masked, n * H + h + 1)
                    V.tensor_reduce(m_blk[:, h:h + 1], masked, AX.X, ALU.max).then_inc(max_done, 1)
                dve.wait_ge(max_done, n * H + H)
                V.tensor_tensor(m_new[:, :], m_blk[:, :], m_run[:, :], ALU.max).then_inc(g_step, 1)
                dve.wait_ge(g_step, g_n + 4)
                V.tensor_tensor(fade_arg[:, :], m_run[:, :], m_new[:, :], ALU.subtract).then_inc(g_fade_arg, 1)
                dve.wait_ge(g_fade_arg, n + 1)
                V.tensor_copy(m_run[:, :], m_new[:, :]).then_inc(g_step, 1)
                V.tensor_scalar(mflag[:, :], m_new[:, :], -0.5 * BIG, 2.0 * BIG, ALU.is_lt, ALU.mult).then_inc(g_step, 1)
                dve.wait_ge(g_step, g_n + 6)
                V.scalar_tensor_tensor(mneg[:, :], m_new[:, :], -1.0, mflag[:, :], ALU.mult, ALU.subtract).then_inc(g_step, 1)
                dve.wait_ge(g_step, g_n + 7)
                V.tensor_copy(m_split[:, 0, 0:H], mneg[:, :]).then_inc(g_step, 1)
                dve.wait_ge(g_step, g_n + 8)
                V.tensor_tensor(mrest[:, :], mneg[:, :], m_split[:, 0, 0:H], ALU.subtract).then_inc(g_step, 1)
                dve.wait_ge(g_step, g_n + 9)
                V.tensor_copy(m_split[:, 0, H:2 * H], mrest[:, :]).then_inc(g_step, 1)
                dve.wait_ge(g_step, g_n + 10)
                V.tensor_tensor(m_split[:, 0, 2 * H:3 * H], mrest[:, :], m_split[:, 0, H:2 * H], ALU.subtract).then_inc(mneg_done, 1)
                dve.wait_ge(g_fade, n + 1)
                V.tensor_tensor(o_run[:, :, :], o_run[:, :, :], fade[:, :].rearrange("p (h e) -> p h e", e=1)
                                .to_broadcast([P, H, DH + 1]), ALU.mult).then_inc(g_step, 1)
                dve.wait_ge(g_step, g_n + 11)
                dve.wait_ge(oT_done, n + 1)
                V.tensor_tensor(o_run[:, :, :], o_run[:, :, :], MI[:, :].rearrange("p (h e) -> p h e", h=H)[:, :, 0:DH + 1],
                                ALU.add).then_inc(g_step, 4)
                dve.wait_ge(g_step, g_n + 15)
                V.tensor_copy(m_blk[:, :], m_new[:, :]).then_inc(g_merged, 1)

            with dve.If(dve.value_load(go_general[0:1, 0:1]) != 0):
                dve.wait_ge(q_stacked, 16 * NTERM)
                dve.wait_ge(k_stacked[1], 16 * NTERM)
                dve.wait_ge(k_stacked[2], 16 * NTERM)
                dve.wait_ge(mask_ready, NB)
                dve.wait_ge(xb_done, NB)
                V.memset(m_blk[:, :], 0.0).then_inc(g_merged, 1)
                V.memset(m_run[:, :], -3.0e38).then_inc(g_q, 1)
                V.memset(o_run[:, :, :], 0.0).then_inc(g_q, 1)
                with dve.Fori(0, NB) as b:
                    V.tensor_copy(q_cur, q_stack[:, :, bass.ds(b * S, S)]).then_inc(g_q, 1)
                    V.tensor_copy(q_raw, q_stack[:, :, bass.ds(b * S, S)]).then_inc(g_q, 1)
                    with dve.Fori(0, NBLK) as k:
                        dve.wait_ge(g_q, 4 * b + 4)
                        general_block(b * NBLK + k)
                    dve.wait_ge(g_merged, b * NBLK + NBLK + 1)
                    V.reciprocal(rden[:, :].rearrange("p (h e) -> p h e", e=1), o_run[:, :, DH:DH + 1]).then_inc(attn_done, 1)
                    dve.wait_ge(attn_done, 2 * b + 1)
                    V.tensor_tensor(attn[:, 0, :].rearrange("p (h d) -> p h d", h=H), o_run[:, :, 0:DH],
                                    rden[:, :].rearrange("p (h e) -> p h e", e=1).to_broadcast([P, H, DH]),
                                    ALU.mult).then_inc(attn_done, 1)
                    dve.wait_ge(wo_done, b + 1)
                    V.tensor_tensor(x1[:, bass.ds(b, 1), :].rearrange("p o d -> p (o d)"), MI[:, 0:DM],
                                    xb[:, bass.ds(b, 1), :].rearrange("p o d -> p (o d)"), ALU.add).then_inc(x1_done, 1)
                    dve.wait_ge(x1_done, b + 1)
                    V.memset(m_run[:, :], -3.0e38).then_inc(g_q, 1)
                    V.memset(o_run[:, :, :], 0.0).then_inc(g_q, 1)
            with dve.Else():
                for h in range(H):
                    head_max(h)
                negate_max(0)
                for b in range(NB):
                    for u in range(8):
                        if b + 1 < NB:
                            for h in range(3 * u, min(3 * u + 3, H)):
                                head_max(H * (b + 1) + h)
                            if u == 5:
                                negate_max(b + 1)
                        if u == 2 and b >= 1:
                            normalise(b - 1)
                        if u == 4 and b >= 1:
                            residual(b - 1)
                normalise(NB - 1)
                residual(NB - 1)

            dve.nop()
            count[0] = 0
            dve_done = dve_post

            def need(n):
                dve.wait_ge(dve_done, n)

            def run(ins):
                step(ins)
                return count[0]

            def moments(nth):
                for b in range(NB):
                    a = run(V.bn_stats(stats[:, b, :], x_src[:, b, :]))
                need(a)
                for b in range(NB):
                    a = V.bn_aggr(mv[:, b, :], stats[:, b, :])
                    if b < NB - 1:
                        step(a)
                a.then_inc(ln_var, 1)
                dve.wait_ge(ln_var, nth)

            dve.wait_ge(x1_done, NB)
            x_src = x1
            moments(2)
            dve.wait_ge(ln_rstd, 2)
            need(count[0])
            a = run(V.tensor_tensor(ms[:, :], mv[:, :, 1], rstd[:, :], ALU.mult))
            need(a)
            V.tensor_tensor(ms[:, :], ms[:, :], rstd[:, :], ALU.mult).then_inc(ms_done, 1)
            dve.wait_ge(rms_done, 1)
            link(V.tensor_tensor(rq2[:, :], rstd[:, :], rms_r[:, :], ALU.mult))
            for b in range(NB):
                V.tensor_scalar(xr[:, b, :], x1[:, b, :], mv[:, b, 0:1], rq2[:, b:b + 1], ALU.subtract, ALU.mult)\
                    .then_inc(xn_ready, 1)
            for b in range(NB):
                V.tensor_scalar(hn[:, b, :], x1[:, b, :], mv[:, b, 0:1], rstd[:, b:b + 1], ALU.subtract, ALU.mult)\
                    .then_inc(h2_done, 1)
            dve.wait_ge(s_late, 160)
            V.tensor_reduce(am[:, :], fw_sb[:, :], AX.X, ALU.max, apply_absolute_value=True).then_inc(am_done, 1)

            dve.wait_ge(xg_copied, 1)
            for i in range(2):
                dve.wait_ge(xg_copied, i + 1)
                acc = conv[:, i, :].rearrange("p (b t) -> p b t", b=NB)
                link(V.tensor_scalar(acc, xg[:, i, :, 0:S], col(f"cw{i}0"), col(f"cb{i}"), ALU.mult, ALU.add))
                for j in range(1, 4):
                    last = V.scalar_tensor_tensor(acc, xg[:, i, :, j:j + S], col(f"cw{i}{j}"), acc, ALU.mult, ALU.add)
                    if j < 3:
                        link(last)
                last.then_inc(conv_done, 1)
                dve.wait_ge(kp_done, i + 1)
                V.tensor_scalar(kq_rows[:, i, :], SB[1][:, i, :], col(f"k_b{i}"), None, ALU.add).then_inc(kp_copied, 1)
            dve.wait_ge(vp_done, 1)
            V.tensor_scalar(v_rows, SA[0][0:2 * H, :], col("v_b", 2 * H), None, ALU.add).then_inc(vp_copied, 1)
            for i in range(2):
                dve.wait_ge(sigc_done, i + 1)
                V.tensor_tensor(xc[:, i, :], conv[:, i, :], sigc[:, i, :], ALU.mult).then_inc(xc_done, 1)
            for i in range(2):
                dve.wait_ge(sigz_done, i + 1)
                run(V.scalar_tensor_tensor(zs[:, i, :], (SA[1], OT)[i][:, :], col(f"z_b{i}"), sigz[:, i, :],
                                           ALU.add, ALU.mult))
            dve.wait_ge(qp_done, 1)
            V.tensor_copy(kq_rows[:, 2, :], SB[0][:, 0, :]).then_inc(qp_copied, 1)

            dve.wait_ge(amx_done, 1)
            link(V.tensor_scalar(fsc[:, :], amx[:, :], 1.0 / 7.0, None, ALU.mult))
            link(V.reciprocal(finv[:, :], fsc[:, :]))
            link(V.tensor_scalar(fq[:, :], fw_sb[:, :], finv[:, 0:1], None, ALU.mult))
            link(V.tensor_scalar(fq[:, :], fq[:, :], 12582912.0, -12582912.0, ALU.add, ALU.add))
            link(V.tensor_scalar(fq[:, :], fq[:, :], -8.0, 7.0, ALU.max, ALU.min))
            dve.wait_ge(ab_mm_done, 1)
            w_eff_at = run(V.scalar_tensor_tensor(w_eff[:, :], fq[:, :], fsc[:, 0:1], SB[1][:, 1, 0:DM], ALU.mult, ALU.add))

            t = lambda n: T[n][:, :]

            def tt(o, x0, x1_, op):
                return run(V.tensor_tensor(o, x0, x1_, op))

            dve.wait_ge(ksq_done, 1)
            a = run(V.tensor_reduce(t("nk"), sq.rearrange("p (d t) -> p t d", d=HD), AX.X, ALU.add))
            need(a)
            V.tensor_scalar(t("nk"), t("nk"), 1.0e-28, None, ALU.max).then_inc(nk_done, 1)
            dve.wait_ge(exp_g, 2)
            V.tensor_scalar(uu[:, :, :], ee[:, :, :], 1.0, None, ALU.add).then_inc(u_done, 1)
            dve.wait_ge(u_done, 1)
            a = run(V.scalar_tensor_tensor(corr[:, :, :], uu[:, :, :], -1.0, ee[:, :, :], ALU.add, ALU.subtract))
            need(a)
            a = run(V.scalar_tensor_tensor(corr[:, :, :], g_ch[:, 0:5:4, :], 0.0, corr[:, :, :], ALU.max, ALU.subtract))
            need(a)
            dve.wait_ge(ln_g, 1)
            a = tt(sp[:, :, :], lnu[:, :, :], corr[:, :, :], ALU.add)
            need(a)
            a = run(V.tensor_scalar(t("dt"), sp[:, 1, :], elds[:, 0:1], 1.0e-4, ALU.mult, ALU.add))
            need(a)
            dve.wait_ge(sig_g, 3)
            run(V.scalar_tensor_tensor(t("ah"), t("dt"), 0.5, sp[:, 0, :], ALU.mult, ALU.mult))
            a = run(V.scalar_tensor_tensor(t("ww"), sig_om[:, :], col("freq"), t("dt"), ALU.mult, ALU.mult))
            need(a)
            tt(t("s2"), t("ah"), t("ah"), ALU.mult)
            a = tt(t("w2"), t("ww"), t("ww"), ALU.mult)
            need(a)
            a = tt(t("t1"), t("s2"), t("w2"), ALU.add)
            need(a)
            run(V.tensor_scalar(t("p1"), t("t1"), 1.0, None, ALU.add))
            a = run(V.tensor_scalar(t("n1"), t("t1"), -1.0, 1.0, ALU.mult, ALU.add))
            need(a)
            run(V.scalar_tensor_tensor(t("den"), t("ah"), 2.0, t("p1"), ALU.mult, ALU.add))
            run(V.scalar_tensor_tensor(t("num"), t("ah"), -2.0, t("p1"), ALU.mult, ALU.add))
            a = tt(t("n1s"), t("n1"), t("n1"), ALU.mult)
            need(a)
            a = run(V.reciprocal(t("rdn"), t("den")))
            b_ = run(V.scalar_tensor_tensor(t("t2"), t("w2"), 4.0, t("n1s"), ALU.mult, ALU.add))
            need(a)
            a = tt(t("t3"), t("num"), t("rdn"), ALU.mult)
            need(b_)
            b_ = run(V.tensor_scalar(t("flag"), t("t2"), 0.0, None, ALU.is_equal))
            need(a)
            V.tensor_scalar(t("ratio"), t("t3"), 1.0e-16, 1.0, ALU.max, ALU.min).then_inc(ratio_done, 1)
            need(b_)
            V.tensor_tensor(t("nsq"), t("t2"), t("flag"), ALU.add).then_inc(nsq_done, 1)
            a = tt(t("t4"), t("n1"), t("flag"), ALU.add)
            dve.wait_ge(ln_g, 2)
            V.scalar_tensor_tensor(t("ell"), t("lr"), 4.0, sig_br[:, 1, :], ALU.mult, ALU.mult).then_inc(ell_done, 1)
            dve.wait_ge(mm_g, 1)
            dve.wait_ge(nsq_done, 1)
            a = tt(t("t5"), t("yy"), t("yy"), ALU.mult)
            need(a)
            a = tt(t("t6"), t("t5"), t("nsq"), ALU.mult)
            need(a)
            a = run(V.tensor_scalar(t("t7"), t("t6"), -0.5, 1.5, ALU.mult, ALU.add))
            need(a)
            a = tt(t("t8"), t("yy"), t("t7"), ALU.mult)
            need(a)
            tt(ph[0][:, 0, :], t("t4"), t("t8"), ALU.mult)
            a = run(V.scalar_tensor_tensor(ph[0][:, 1, :], t("ww"), 2.0, t("t8"), ALU.mult, ALU.mult))
            off = 1
            cur = 0
            while off < S:
                need(count[0])
                X, Y, n_ = ph[cur], ph[1 - cur], S - off
                run(V.tensor_tensor(pa[:, :, 0:n_], X[:, :, off:S], X[:, 0:1, 0:n_].to_broadcast([P, 2, n_]), ALU.mult))
                run(V.tensor_tensor(pbb[:, :, 0:n_], X[:, :, off:S], X[:, 1:2, 0:n_].to_broadcast([P, 2, n_]), ALU.mult))
                a = run(V.tensor_copy(Y[:, :, 0:off], X[:, :, 0:off]))
                need(a)
                run(V.tensor_tensor(Y[:, 0, off:S], pa[:, 0, 0:n_], pbb[:, 1, 0:n_], ALU.subtract))
                run(V.tensor_tensor(Y[:, 1, off:S], pa[:, 1, 0:n_], pbb[:, 0, 0:n_], ALU.add))
                off *= 2
                cur = 1 - cur
            cosp, sinp = ph[cur][:, 0, :], ph[cur][:, 1, :]
            dve.wait_ge(mm_g, 3)
            a = run(V.tensor_scalar(t("t1"), t("m2"), -1.0, 1.0, ALU.mult, ALU.add))
            need(a)
            V.tensor_scalar(t("c1"), t("t1"), 0.0, 1.0e-6, ALU.max, ALU.add).then_inc(c1_done, 1)
            dve.wait_ge(knorm_done, 1)
            a = run(V.tensor_scalar(t("t2"), t("nrm"), 1.0e-6, None, ALU.add))
            need(a)
            a = run(V.reciprocal(t("rk"), t("t2")))
            need(a)
            a = tt(t("brk"), sig_br[:, 0, :], t("rk"), ALU.mult)
            dve.wait_ge(v_loaded, 64)
            run(V.tensor_tensor(t("vr1"), v_own[:, :], cosp, ALU.mult))
            a = run(V.scalar_tensor_tensor(t("vr2"), v_swap[:, :], col("sgn"), sinp, ALU.mult, ALU.mult))
            need(a)
            run(V.scalar_tensor_tensor(t("t3"), t("brk"), -1.0, t("mm"), ALU.mult, ALU.mult))
            a = tt(t("vr3"), t("vr1"), t("vr2"), ALU.add)
            dve.wait_ge(mm_g, 4)
            b_ = tt(t("vp"), sig_bc[:, 0, :], t("rt"), ALU.mult)
            need(b_)
            tt(t("ct"), t("t3"), t("rk"), ALU.mult)
            a = tt(t("t4"), t("vr3"), t("vp"), ALU.mult)
            need(a)
            a = tt(t("wt"), t("t4"), t("brk"), ALU.mult)
            need(a)
            bc = lambda v: v.rearrange("p (o t) -> p o t", o=1).to_broadcast([P, HD, S])
            run(V.tensor_tensor(by_t(w_ch), by_t(k_ch), bc(t("wt")), ALU.mult))
            a = run(V.tensor_tensor(by_t(kc_ch), by_t(k_ch), bc(t("ct")), ALU.mult))
            need(a)
            Yt, Kt_, Wt, Ct = by_t(y_ch), by_t(k_ch), by_t(w_ch), by_t(kc_ch)
            run(V.tensor_copy(Yt[:, :, 0], Wt[:, :, 0]))
            for n_ in range(1, S):
                need(count[0])
                p_ = n_ % 2
                run(V.tensor_tensor_reduce(gjunk[:, p_, :], Yt[:, :, n_ - 1], Kt_[:, :, n_], 1.0, 0.0, ALU.mult, ALU.add,
                                           pred[:, p_:p_ + 1]))
                run(V.scalar_tensor_tensor(grow[:, p_, :], Yt[:, :, n_ - 1], T["mm"][:, n_:n_ + 1], Wt[:, :, n_],
                                           ALU.mult, ALU.add))
                need(count[0])
                run(V.scalar_tensor_tensor(Yt[:, :, n_], Ct[:, :, n_], pred[:, p_:p_ + 1], grow[:, p_, :],
                                           ALU.mult, ALU.add))
            dve.wait_ge(qsq_done, 1)
            a = run(V.tensor_reduce(t("nq"), sq.rearrange("p (d t) -> p t d", d=HD), AX.X, ALU.add))
            need(a)
            V.tensor_scalar(t("nq"), t("nq"), 1.0e-28, None, ALU.max).then_inc(nq_done, 1)
            need(count[0])
            a = run(V.tensor_tensor(prod, y_ch, q_ch, ALU.mult))
            need(a)
            a = run(V.tensor_reduce(t("rr"), prod.rearrange("p (d t) -> p t d", d=HD), AX.X, ALU.add))
            dve.wait_ge(qnorm_done, 1)
            a = run(V.tensor_scalar(t("t5"), t("nrq"), 1.0e-6, None, ALU.add))
            need(a)
            a = run(V.reciprocal(t("rq"), t("t5")))
            need(a)
            a = tt(t("gq"), t("rq"), sig_bc[:, 1, :], ALU.mult)
            need(a)
            a = tt(t("r2"), t("rr"), t("gq"), ALU.mult)
            need(a)
            V.tensor_tensor(t("cc"), t("r2"), cosp, ALU.mult).then_inc(parts_done, 1)
            V.tensor_tensor(t("dd"), t("r2"), sinp, ALU.mult).then_inc(parts_done, 1)
            for i in range(2):
                dve.wait_ge(y_done, i + 1)
                for b in range(NB):
                    a = run(V.bn_stats(gst[:, NB * i + b, :], SB[0][:, i, S * b:S * (b + 1)]))
            need(a)
            for j in range(8):
                V.bn_aggr(gmv[:, j, :], gst[:, j, :]).then_inc(gst_done, 1)
            dve.wait_ge(gm_done, 1)
            a = run(V.tensor_copy(gmean[:, :], MI[:, 0:8]))
            need(a)
            a = run(V.tensor_tensor(gdm[:, :], gmv[:, :, 0], gmean[:, :], ALU.subtract))
            need(a)
            a = run(V.tensor_tensor(gdm[:, :], gdm[:, :], gdm[:, :], ALU.mult))
            need(a)
            V.tensor_tensor(gdv[:, :], gdm[:, :], gmv[:, :, 1], ALU.add).then_inc(gdv_done, 1)
            dve.wait_ge(grs_done, 1)
            for i in range(2):
                a = run(V.tensor_scalar(gsc[:, NB * i:NB * (i + 1)], grs[:, NB * i:NB * (i + 1)], col(f"gn_w{i}"), None, ALU.mult))
            need(a)
            a = run(V.tensor_tensor(gdm[:, :], gmean[:, :], gsc[:, :], ALU.mult))
            need(a)
            for i in range(2):
                V.tensor_scalar(gbi[:, NB * i:NB * (i + 1)], gdm[:, NB * i:NB * (i + 1)], -1.0, col(f"gn_b{i}"),
                                ALU.mult, ALU.add).then_inc(gbi_done, 1)
            for i in range(2):
                dve.wait_ge(yn_done, NB * (i + 1))
                a = run(V.tensor_tensor(yn[:, i, :], yn[:, i, :], zs[:, i, :], ALU.mult))
                need(a)
                V.scalar_tensor_tensor(y2[:, i, :], xc[:, i, :], col(f"d{i}"), yn[:, i, :], ALU.mult, ALU.add)\
                    .then_inc(y2_done, 1)
            dve.wait_ge(o2_done, 1)
            dve.wait_ge(x1h_done, 1)
            V.tensor_tensor(x2[:, :, :], SB[1][:, 0, :].rearrange("p (b d) -> p b d", b=NB), x1h[:, :, :], ALU.add)\
                .then_inc(x2_done, 1)
            dve.wait_ge(x2_done, 1)
            x_src = x2
            moments(3)
            a = run(V.tensor_tensor(res[:, :, :], x2[:, :, :],
                                    rows_sb[:, 2:3, :].to_broadcast([P, NB, DM]), ALU.add))
            dve.wait_ge(ln_rstd, 3)
            need(count[0])
            for b in range(NB):
                V.tensor_scalar(xn[:, b, :], x2[:, b, :], mv[:, b, 0:1], rstd[:, b:b + 1], ALU.subtract, ALU.mult)\
                    .then_inc(xn_ready, 1)
            dve.wait_ge(ffn_done, 1)
            V.tensor_tensor(res[:, :, :], res[:, :, :], SA[0][:, :].rearrange("p (b d) -> p b d", b=NB), ALU.add)\
                .then_inc(res_done, 1)

        @block.tensor
        def _(pe):
            def k_project(b):
                pe.wait_ge(s_ctx[b], 16)
                nc.tensor.matmul(SB[b // 2][:, b % 2, :], wk_sb[:, :], ctx_sb[:, b, :], start=True, stop=True)\
                    .then_inc(k_done, 1)

            def v_project(b, dst):
                for t in range(KT):
                    last = nc.tensor.matmul(dst[:, P * t:P * (t + 1)], ctx_sb[:, b, P * t:P * (t + 1)], wv_sb[:, :],
                                            start=True, stop=True)
                last.then_inc(v_done, 1)

            pe.wait_ge(s_wk, 16)
            k_project(0)
            k_project(1)
            pe.wait_ge(s_id, 16)
            for b in range(NB):
                pe.wait_ge(xn_ready, b + 1)
                last = nc.tensor.transpose(MI[:, P * b:P * (b + 1)], xn[:, b, :], id_sb[:, :])
            last.then_inc(xnT_done, 1)
            pe.wait_ge(s_wq, 16)
            pe.wait_ge(xnT_copied, 1)
            nc.tensor.matmul(SA[0][:, :], wq_sb[:, :], xn_t[:, :], start=True, stop=True).then_inc(q_done, 1)
            k_project(2)
            k_project(3)
            pe.wait_ge(s_wv, 16)
            pe.wait_ge(q_copied, 2)
            v_project(0, SA[0][:, :])
            v_project(1, SA[1][:, :])
            v_project(2, MI[:, :])
            pe.wait_ge(v_copied, 1)
            v_project(3, SA[0][:, :])

            def score(n):
                b, h = divmod(n, H)
                if h == 0:
                    pe.wait_ge(k_stacked[b], 16 * NTERM)
                if n == 0:
                    pe.wait_ge(q_stacked, 16 * NTERM)
                    pe.wait_ge(v_copied, NB)
                if n >= 2:
                    pe.wait_ge(max_done, n - 1)
                nc.tensor.matmul(SA[n % 2][:, :], q_stack[:, h, S * b:S * (b + 1)], k_stack[b][:, h, :],
                                 start=True, stop=True).then_inc(score_done, 1)

            def turn_max(b):
                pe.wait_ge(mneg_done, b + 1)
                if b >= 2:
                    pe.wait_ge(x1_done, b - 1)
                nc.tensor.transpose(MI[0:3 * H, 0:S // 2].bitcast(BF16), m_split[:, b, :], id_bf[:, :]).then_inc(mT_done, 1)

            def unit_scores(n):
                b, u = divmod(n, 8)
                t, half = divmod(u, 2)
                if u == 0:
                    pe.wait_ge(m_stacked, 16 * b + 16)
                    pe.wait_ge(mask_ready, b + 1)
                    pe.wait_ge(consts_ready, 4)
                if n >= 2:
                    pe.wait_ge(unit_exp, n - 1)
                for g in range(2):
                    for j in range(4):
                        h = 8 * half + 4 * g + j
                        nc.tensor.matmul(SB[n % 2][:, g, S * j:S * (j + 1)], k_stack[b][:, h, P * t:P * (t + 1)],
                                         q_stack[:, h, S * b:S * (b + 1)], start=(j == 0), stop=False,
                                         skip_group_check=True)
                    last = nc.tensor.matmul(SB[n % 2][:, g, :], mask_bf[:, b, P * t:P * (t + 1)],
                                            neg_id4[:, :, :].rearrange("p a s -> p (a s)"), start=False, stop=True,
                                            skip_group_check=True)
                last.then_inc(unit_scored, 1)

            def unit_values(n):
                b, u = divmod(n, 8)
                t, half = divmod(u, 2)
                pe.wait_ge(unit_exp, n + 1)
                if u == 0:
                    if b == 0:
                        pe.wait_ge(ot_zeroed, 1)
                    else:
                        pe.wait_ge(o_copied, b)
                for i in range(8):
                    h = 8 * half + i
                    g, j = divmod(h, 4)
                    last = nc.tensor.matmul(OT[32 * j:32 * j + DH + 1, S * g:S * (g + 1)], v_ones[:, b, t, h, :],
                                            probs[:, n % 3, i, :], start=(t == 0 and g == 0), stop=(t == KT - 1),
                                            skip_group_check=True)
                last.then_inc(unit_pv, 1)

            def turn_out(b):
                pe.wait_ge(o_copied, b + 1)
                if b >= 1:
                    pe.wait_ge(x1_done, b)
                pe.wait_ge(mT_copied, min(b + 2, NB))
                for g in range(4):
                    last = nc.tensor.transpose(MI[:, S * g:S * (g + 1)], o_sb[:, b % 2, S * g:S * (g + 1)], id_sb[:, :])
                last.then_inc(oT_done, 1)

            def turn_attn(b):
                pe.wait_ge(attn_done, b + 1)
                nc.tensor.transpose(MI[:, 0:S], attn[:, b % 2, :], id_sb[:, :]).then_inc(aT_done, 1)

            def project_out(b):
                pe.wait_ge(aT_copied, b + 1)
                pe.wait_ge(s_wo, 16)
                nc.tensor.matmul(MI[:, 0:DM], attn_t[:, b % 2, :], wo_sb[:, :], start=True, stop=True).then_inc(wo_done, 1)

            MM = nc.tensor.matmul
            pe.wait_ge(open_done, 1)
            pe.wait_ge(v_copied, 2)
            MM(SA[1][0:1, 0:1], some_open[:, :], col("one"), start=True, stop=True).then_inc(count_done, 1)

            def general_block(n):
                pe.wait_ge(g_ctx, 16 * n + 16)
                MM(SB[0][:, 0, :], wk_sb[:, :], ctx_sb[:, 0, :], start=True, stop=True).then_inc(g_kproj, 1)
                for t in range(KT):
                    last = MM(MI[:, P * t:P * (t + 1)], ctx_sb[:, 0, P * t:P * (t + 1)], wv_sb[:, :], start=True, stop=True)
                last.then_inc(g_vproj, 1)
                pe.wait_ge(g_kstacked, n * (16 * NTERM) + 16 * NTERM)
                for h in range(H):
                    if h >= 2:
                        pe.wait_ge(max_done, n * H + h - 1)
                    MM(SA[h % 2][:, :], q_raw[:, h, :], k_stack[0][:, h, :], start=True, stop=True).then_inc(score_done, 1)
                pe.wait_ge(mneg_done, n + 1)
                pe.wait_ge(g_vcopied, n + 1)
                MM(MI[0:3 * H, 0:S], m_split[:, 0, :], id_bf[:, :], start=True, stop=True).then_inc(mT_done, 1)
                pe.wait_ge(m_stacked, 16 * n + 16)
                pe.wait_ge(g_maskset, n + 1)

                def values(u):
                    t, half = divmod(u, 2)
                    pe.wait_ge(unit_exp, n * UNITS + u + 1)
                    for i in range(8):
                        g, j = divmod(8 * half + i, 4)
                        last = MM(OT[32 * j:32 * j + DH + 1, S * g:S * (g + 1)], v_ones[:, 0, t, 8 * half + i, :],
                                  probs[:, u % 2, i, :], start=(t == 0 and g == 0), stop=(t == KT - 1),
                                  skip_group_check=True)
                    last.then_inc(unit_pv, 1)

                for u in range(UNITS):
                    t, half = divmod(u, 2)
                    if u >= 2:
                        pe.wait_ge(unit_exp, n * UNITS + u - 1)
                    for g in range(2):
                        for j in range(4):
                            h = 8 * half + 4 * g + j
                            MM(SB[u % 2][:, g, S * j:S * (j + 1)], k_stack[0][:, h, P * t:P * (t + 1)], q_cur[:, h, :],
                               start=(j == 0), stop=False, skip_group_check=True)
                        last = MM(SB[u % 2][:, g, :], mask_bf[:, 0, P * t:P * (t + 1)],
                                  neg_id4[:, :, :].rearrange("p a s -> p (a s)"), start=False, stop=True,
                                  skip_group_check=True)
                    last.then_inc(unit_scored, 1)
                    if u >= 1:
                        values(u - 1)
                values(UNITS - 1)
                pe.wait_ge(o_copied, n + 1)
                for g in range(4):
                    last = nc.tensor.transpose(MI[:, S * g:S * (g + 1)], o_sb[:, 0, S * g:S * (g + 1)], id_sb[:, :])
                last.then_inc(oT_done, 1)

            pe.wait_ge(flag_done, 1)
            with pe.If(pe.value_load(go_general[0:1, 0:1]) != 0):
                pe.wait_ge(v_copied, NB)
                pe.wait_ge(ot_zeroed, 1)
                pe.wait_ge(consts_ready, 4)
                pe.wait_ge(s_wo, 16)
                with pe.Fori(0, NB) as b:
                    with pe.Fori(0, NBLK) as k:
                        pe.wait_ge(g_q, 4 * b + 4)
                        general_block(b * NBLK + k)
                    pe.wait_ge(attn_done, 2 * b + 2)
                    nc.tensor.transpose(MI[:, 0:S], attn[:, 0, :], id_sb[:, :]).then_inc(aT_done, 1)
                    pe.wait_ge(aT_copied, b + 1)
                    MM(MI[:, 0:DM], attn_t[:, 0, :], wo_sb[:, :], start=True, stop=True).then_inc(wo_done, 1)
            with pe.Else():
                for h in range(H):
                    score(h)
                turn_max(0)
                for b in range(NB):
                    for u in range(8):
                        n = 8 * b + u
                        unit_scores(n)
                        if b + 1 < NB:
                            for h in range(3 * u, min(3 * u + 3, H)):
                                score(H * (b + 1) + h)
                            if u == 6:
                                turn_max(b + 1)
                        if n >= 1:
                            unit_values(n - 1)
                        if b >= 1:
                            if u == 1:
                                turn_out(b - 1)
                            if u == 3:
                                turn_attn(b - 1)
                            if u == 4:
                                project_out(b - 1)
                unit_values(8 * NB - 1)
                turn_out(NB - 1)
                turn_attn(NB - 1)
                project_out(NB - 1)

            pe.nop()
            pe.wait_ge(x1_done, NB)
            for b in range(NB):
                pe.wait_ge(xn_ready, NB + b + 1)
                last = nc.tensor.transpose(MI[:, S * b:S * (b + 1)], xr[:, b, :], id_sb[:, :])
            last.then_inc(xnT_done, 1)
            pe.wait_ge(s_late, 160)
            pe.wait_ge(xnT_copied, 2)
            for i in range(2):
                MM(SB[0][:, i, :], w_in_sb[:, DI + P * i:DI + P * (i + 1)], xr_t[:, :], start=True, stop=True).then_inc(xg_done, 1)
            for i in range(2):
                MM(SB[1][:, i, :], w_in_sb[:, 2 * DI + P * i:2 * DI + P * (i + 1)], xr_t[:, :], start=True, stop=True)\
                    .then_inc(kp_done, 1)
            MM(SA[0][0:2 * H, :], w_in_sb[:, 3 * DI:3 * DI + 2 * H], xr_t[:, :], start=True, stop=True).then_inc(vp_done, 1)
            MM(SA[1][:, :], w_in_sb[:, 0:P], xr_t[:, :], start=True, stop=True).then_inc(z_done, 1)
            MM(OT[:, :], w_in_sb[:, P:2 * P], xr_t[:, :], start=True, stop=True).then_inc(z_done, 1)
            for i in range(2):
                pe.wait_ge(xc_done, i + 1)
                last = MM(MI[0:7 * H, :], w_gate_sb[:, i, :], xc[:, i, :], start=(i == 0), stop=(i == 1))
            last.then_inc(gate_done, 1)
            pe.wait_ge(xg_copied, 2)
            for o in range(2):
                for i in range(2):
                    last = MM(SB[0][:, o, :], w_q_sb[:, i, P * o:P * (o + 1)], xc[:, i, :], start=(i == 0), stop=(i == 1))
                last.then_inc(qp_done, 1)
            pe.wait_ge(kp_copied, 2)
            MM(SB[1][:, 1, 0:DM], fat_sb[:, :], fb_sb[:, :], start=True, stop=True).then_inc(ab_mm_done, 1)
            pe.wait_ge(parts_done, 2)
            pe.wait_ge(wrs_done, 1)
            pe.wait_ge(qp_copied, 2)
            for i in range(2):
                for b in range(NB):
                    MM(SB[0][:, i, S * b:S * (b + 1)], w_rd[:, b, P * i:P * (i + 1)], T["cc"][:, :], start=True, stop=False)
                    last = MM(SB[0][:, i, S * b:S * (b + 1)], w_rs[:, b, P * i:P * (i + 1)], T["dd"][:, :], start=False, stop=True)
                last.then_inc(y_done, 1)
            pe.wait_ge(gst_done, 8)
            pe.wait_ge(gate_copied, 1)
            MM(MI[:, 0:8], avg_sb[:, :], gmv[:, :, 0], start=True, stop=True).then_inc(gm_done, 1)
            pe.wait_ge(gdv_done, 1)
            MM(MI[:, 8:16], avg_sb[:, :], gdv[:, :], start=True, stop=True).then_inc(gv_done, 1)
            pe.wait_ge(y2_done, 2)
            for b in range(NB):
                for i in range(2):
                    last = MM(SB[1][:, 0, S * b:S * (b + 1)], y2[:, i, S * b:S * (b + 1)], w_out_sb[:, i, :], start=(i == 0),
                              stop=(i == 1))
            last.then_inc(o2_done, 1)
            for b in range(NB):
                pe.wait_ge(xn_ready, 2 * NB + b + 1)
                last = nc.tensor.transpose(MI[:, S * b:S * (b + 1)], xn[:, b, :], id_sb[:, :])
            last.then_inc(xnT_done, 1)
            pe.wait_ge(xnT_copied, 3)
            for b in range(NB):
                last = MM(SA[0][:, S * b:S * (b + 1)], xn_t[:, S * b:S * (b + 1)], w_eff[:, :], start=True, stop=True)
            last.then_inc(ffn_done, 1)


INPUTS = ["x", "ctx_t", "mask", "wq", "wk", "wv", "wo", "vec", "rows", "ident", "avg", "w_in", "w_gate", "w_q",
          "w_read", "w_out", "ffn_w", "ffn_at", "ffn_b"]


def kernel(**inputs):
    import numpy as np
    import concourse.bacc as bacc
    from concourse.bass_utils import run_bass_kernel_spmd

    a = {k: np.asarray(v) for k, v in inputs.items()}
    f32 = np.float32

    cols = {n: np.zeros((P, 1), f32) for n in VEC}

    def put(name, v):
        cols[name][:v.shape[0], 0] = v

    by_dim = lambda w: w.reshape(H, DH, DM).transpose(1, 0, 2).reshape(DM, DM)
    put("bq", a["L0_xattn_bq"].reshape(H, DH).T.reshape(-1))
    put("bk", a["L0_xattn_bk"].reshape(H, DH).T.reshape(-1))
    put("rms", a["L0_attn_rms_w"])
    b_in = a["L0_attn_in_proj_b"]
    for i in range(2):
        put(f"z_b{i}", b_in[P * i:P * (i + 1)])
        put(f"xg_b{i}", b_in[DI + P * i:DI + P * (i + 1)])
        put(f"k_b{i}", b_in[2 * DI + P * i:2 * DI + P * (i + 1)])
        put(f"cb{i}", a["L0_attn_conv_b"][P * i:P * (i + 1)])
        put(f"gn_w{i}", a["L0_attn_gn_w"][P * i:P * (i + 1)])
        put(f"gn_b{i}", a["L0_attn_gn_b"][P * i:P * (i + 1)])
        put(f"d{i}", a["L0_attn_D_param"][P * i:P * (i + 1)])
        for j in range(4):
            put(f"cw{i}{j}", a["L0_attn_conv_w"][P * i:P * (i + 1), j])
    put("v_b", b_in[3 * DI:])
    put("gate_b", a["L0_attn_gate_b"].reshape(7, H).T.reshape(-1))
    put("log_dt", np.tile(a["L0_attn_log_dt_scale"], 8))
    put("freq", np.tile((f32(1.0) / f32(10000.0) ** (np.arange(H, dtype=f32) / f32(H))).astype(f32), 8))
    put("sgn", np.repeat(np.array([-1.0, 1.0], f32), 64))
    put("eps_ln", np.full(P, EPS_LN, f32))
    put("eps_rms", np.full(P, EPS_RMS, f32))
    put("one", np.ones(P, f32))
    put("root_shift", np.full(P, -15 * LN2, f32))
    rows = np.stack([a["L0_xattn_bv"], a["L0_xattn_bo"], a["L0_ffn_bias"]])
    rd = a["L0_attn_readout_w"].reshape(H, 2, DI)
    w_read = np.zeros((2, 2, NB, H, NB, DI), f32)
    for s in range(2):
        for b in range(NB):
            w_read[0, s, b, :, b, :] = rd[:, s]
            w_read[1, s, b, :, b, :] = rd[:, 1 - s]
    arrays = {
        "x": a["x"],
        "ctx_t": a["ctx_1024"].transpose(0, 2, 1),
        "mask": a["mask_BxSxS2_bk1"],
        "wq": by_dim(a["L0_xattn_Wq"]).T, "wk": by_dim(a["L0_xattn_Wk"]).T,
        "wv": a["L0_xattn_Wv"].T, "wo": a["L0_xattn_Wo"].T,
        "vec": np.concatenate([cols[n] for n in VEC], axis=1),
        "rows": np.broadcast_to(rows[None], (P, 3, DM)),
        "ident": np.eye(P, dtype=f32),
        "avg": np.kron(np.eye(P // GN, dtype=f32), np.full((GN, GN), 1.0 / GN, f32)),
        "w_in": a["L0_attn_in_proj_w"],
        "w_gate": a["L0_attn_gate_w"].reshape(2, P, 7, H).transpose(1, 0, 3, 2).reshape(P, 2, 7 * H),
        "w_q": a["L0_attn_Q_w"].reshape(2, P, DI).transpose(1, 0, 2),
        "w_read": w_read.reshape(2, P, NB, DI),
        "w_out": a["L0_attn_out_w"].reshape(2, P, DM).transpose(1, 0, 2),
        "ffn_w": a["L0_ffn_kernel"], "ffn_at": a["L0_ffn_a"].T, "ffn_b": a["L0_ffn_b"],
    }
    arrays = {k: np.ascontiguousarray(arrays[k]) for k in INPUTS}
    nc = bacc.Bacc("TRN2", target_bir_lowering=False, num_devices=1)
    aps = [nc.dram_tensor(f"in_{k}", v.shape, mybir.dt.from_np(v.dtype), kind="ExternalInput").ap()
           for k, v in arrays.items()]
    out = nc.dram_tensor("out", (NB, S, DM), F32, kind="ExternalOutput").ap()
    perceiver_kernel(nc, *aps, out)
    r = run_bass_kernel_spmd(nc, [{f"in_{k}": v for k, v in arrays.items()}], core_ids=[0])
    return r.results[0]["out"]
```

```python
from contextlib import ExitStack

import concourse.bass as bass
from concourse import mybir

ALU = mybir.AluOpType
ACT = mybir.ActivationFunctionType
F32 = mybir.dt.float32
BF16 = mybir.dt.bfloat16
U8 = mybir.dt.uint8
U16 = mybir.dt.uint16
I32 = mybir.dt.int32
AX = mybir.AxisListType

P = 128
NB = 4
S = 128
DM = 128
NK = 2048
H = 16
DH = DM // H
BLK = 512
KT = BLK // P
TOK = NB * S
DI = 256
HD = DI // H
C = 4
NC = S // C
NPAIR = C * (C - 1) // 2
BIG = 1.0e30
SCALE = float(DH) ** -0.5
EPS_LN = 1e-5
EPS_RMS = 1e-6
GN = 16
LN2 = 0.6931471805599453
ONES_PAIR = 1.0 + 0x3F80 / 2.0 ** 23

NBLK = NK // BLK
UNITS = 2 * KT
ALL_MASKED = NB * (NK - BLK) // 2 * 0x0101
K_LEVEL = [0, 1, 2, 0, 1, 0]
Q_LEVEL = [0, 0, 0, 1, 1, 2]
NTERM = len(K_LEVEL)
MROW = NTERM * DH

VEC = {n: i for i, n in enumerate(
    ["bq", "bk", "rms", "xg_b0", "xg_b1", "k_b0", "k_b1", "z_b0", "z_b1", "v_b"]
    + [f"cw{i}{j}" for i in range(2) for j in range(4)]
    + ["cb0", "cb1", "gn_w0", "gn_w1", "gn_b0", "gn_b1", "d0", "d1", "gate_b", "log_dt", "freq", "sgn",
       "eps_ln", "eps_rms", "root_shift", "one"])}
NVEC = len(VEC)


def perceiver_kernel(nc, x, ctx_t, mask, wq, wk, wv, wo, vec, rows, ident, avg, w_in, w_gate, w_q, w_read,
                     w_out, ffn_w, ffn_at, ffn_b, out):
    ctx = ExitStack()
    with ctx:
        def sb(name, shape, dt=F32):
            return ctx.enter_context(nc.sbuf_tensor(name, shape, dt))

        def pb(name, shape, dt=F32):
            return ctx.enter_context(nc.psum_tensor(name, shape, dt))

        def sem(name):
            return ctx.enter_context(nc.semaphore(name))

        scratch = nc.dram_tensor("scratch", [2 * DI + 2 * H + 7 * H, TOK], F32, kind="Internal").ap()
        ROW_K, ROW_Q, ROW_V, ROW_G = 0, DI, 2 * DI, 2 * DI + 2 * H

        x_sb = sb("x_sb", [P, NB, DM])
        ctx_sb = sb("ctx_sb", [P, NB, BLK])
        mask_sb = sb("mask_sb", [P, NB, NK], U8)
        mask_bf = sb("mask_bf", [P, NB, BLK], BF16)
        mask_neg = sb("mask_neg", [P, NB, BLK])
        vec_sb = sb("vec_sb", [P, NVEC])
        rows_sb = sb("rows_sb", [P, 3, DM])
        id_sb = sb("id_sb", [P, P])
        id_bf = sb("id_bf", [P, P], BF16)
        neg_id4 = sb("neg_id4", [P, 4, P], BF16)
        avg_sb = sb("avg_sb", [P, P])
        wq_sb, wk_sb, wv_sb, wo_sb = (sb(n, [P, DM]) for n in ("wq_sb", "wk_sb", "wv_sb", "wo_sb"))
        w_in_sb = sb("w_in_sb", [P, 3 * DI + 2 * H])
        w_gate_sb = sb("w_gate_sb", [P, 2, 7 * H])
        w_q_sb = sb("w_q_sb", [P, 2, DI])
        w_rd = sb("w_rd", [P, NB, DI])
        w_rs = sb("w_rs", [P, NB, DI])
        w_out_sb = sb("w_out_sb", [P, 2, DM])
        fw_sb = sb("fw_sb", [P, DM])
        fat_sb = sb("fat_sb", [16, DM])
        fb_sb = sb("fb_sb", [16, DM])
        w_eff = sb("w_eff", [P, DM])
        stats = sb("stats", [P, NB, 6])
        mv = sb("mv", [P, NB, 2])
        lnv = sb("lnv", [P, NB])
        rstd = sb("rstd", [P, NB])
        xn = sb("xn", [P, NB, DM])
        xn_t = sb("xn_t", [P, TOK])
        xb = sb("xb", [P, NB, DM])
        q_f = sb("q_f", [P, TOK])
        q_r = sb("q_r", [P, TOK])
        q_split = sb("q_split", [P, 3, TOK], BF16)
        k_f = sb("k_f", [P, NB, BLK])
        k_r = sb("k_r", [P, BLK])
        k_split = sb("k_split", [P, NB, 3, BLK], BF16)
        q_stack = sb("q_stack", [P, H, TOK], BF16)
        k_stack = [sb(f"k_stack{b}", [P, H, BLK], BF16) for b in range(NB)]
        v_ones = sb("v_ones", [P, NB, KT, H, DH + 1])
        junk = sb("junk", [P, 2, BLK], BF16)
        mx = sb("mx", [P, NB, H])
        mflag = sb("mflag", [P, H])
        mneg = sb("mneg", [P, H])
        mrest = sb("mrest", [P, H])
        m_split = sb("m_split", [P, NB, 3 * H], BF16)
        m_t = sb("m_t", [3 * H, NB, S], BF16)
        probs = sb("probs", [P, 3, 8, S])
        probs_flat = probs[:, :, :, :].rearrange("p a h s -> p (a h s)")
        o_sb = sb("o_sb", [P, 2, 4 * S])
        rden = sb("rden", [P, H])
        attn = sb("attn", [P, 2, DM])
        attn_t = sb("attn_t", [P, 2, S])
        x1 = sb("x1", [P, NB, DM])

        def chain_view(stack, half):
            flat = stack[:, :, :].rearrange("p h k -> p (h k)").bitcast(F32)
            return flat[:, 2048 * half:2048 * (half + 1)]

        k_ch, q_ch = chain_view(k_stack[0], 0), chain_view(k_stack[0], 1)
        chunked = lambda v, n: v.rearrange("p (d c j) -> p d c j", c=NC, j=n)
        flat1 = k_stack[1][:, :, :].rearrange("p h k -> p (h k)").bitcast(F32)
        flat2 = k_stack[2][:, :, :].rearrange("p h k -> p (h k)").bitcast(F32)
        kappa = flat1[:, 0:(HD + 1) * S]
        kap_t = kappa.rearrange("p (d t) -> p d t", d=HD + 1)
        kap_c = chunked(kappa, C)
        pair_tmp = flat1[:, (HD + 1) * S:(HD + 1) * S + (HD + 1) * NC * 3]
        SLOT = C + 1
        NS = (NC + 1) * SLOT
        bank = flat2[:, 0:(HD + 1) * NS].rearrange("p (d n) -> p d n", d=HD + 1)
        bank_c = bank.rearrange("p d (c j) -> p d c j", j=SLOT)
        at = [(HD + 1) * NS]

        def carve(n):
            at[0] += n
            return flat2[:, at[0] - n:at[0]]

        gram, dcoef = (carve(NPAIR * NC) for _ in range(2))
        coef = carve(NC * SLOT)
        coef_c = coef.rearrange("p (c j) -> p c j", j=SLOT)
        m_pair = carve(3 * NC).rearrange("p (c j) -> p c j", j=3)
        m_three = carve(2 * NC).rearrange("p (c j) -> p c j", j=2)
        bcoef = carve(S).rearrange("p (c j) -> p c j", j=C)
        m_scan = carve(S)
        uk, y_ch = flat1[:, 0:2048], flat1[:, 2048:4096]
        prod = flat2[:, 0:2048]
        sq = chain_view(k_stack[3], 0)
        by_t = lambda v: v.rearrange("p (d t) -> p d t", d=HD)
        xr = xn
        xr_t = xn_t
        ks_flat = k_split[:, :, :, :].rearrange("p b l k -> p (b l k)").bitcast(F32)
        ms = sb("ms", [P, NB])
        rms_r = sb("rms_r", [P, NB])
        rq2 = sb("rq2", [P, NB])
        x1h = ks_flat[:, 1024:1536].rearrange("p (b d) -> p b d", b=NB)
        hn = ks_flat[:, 1536:2048].rearrange("p (b d) -> p b d", b=NB)
        mask_flat = mask_sb[:, :, :].rearrange("p b k -> p (b k)").bitcast(F32)
        v_flat = v_ones[:, :, :, :, :].rearrange("p b t h e -> p (b t h e)")
        n_xg = 2 * NB * (S + 3)
        xg = mask_flat[:, 0:n_xg].rearrange("p (i b t) -> p i b t", i=2, b=NB)
        g_ch = mask_flat[:, n_xg:n_xg + 7 * S].rearrange("p (g t) -> p g t", g=7)
        pair = lambda flat, n: flat[:, 2 * S * n:2 * S * (n + 1)].rearrange("p (a t) -> p a t", a=2)
        two = lambda v: v.rearrange("p (i t) -> p i t", i=2)
        spare = chain_view(k_stack[3], 1)
        conv, sigc = two(spare[:, 0:2 * TOK]), two(spare[:, 2 * TOK:4 * TOK])
        ctx_flat = ctx_sb[:, :, :].rearrange("p b k -> p (b k)")
        xc, zs = two(ctx_flat[:, 0:2 * TOK]), two(ctx_flat[:, 2 * TOK:4 * TOK])
        neg_flat = mask_neg[:, :, :].rearrange("p b k -> p (b k)")
        m_full = spare
        sigz = two(neg_flat[:, 0:2 * TOK])
        kq_rows = k_f[:, :, :]
        v_rows = q_f[0:2 * H, :]
        g_rows = q_r[0:7 * H, :]
        v_own, v_swap = v_flat[:, 0:S], v_flat[:, S:2 * S]
        sig_bc, sig_br = pair(v_flat, 1), pair(v_flat, 2)
        sig_om = sb("sig_om", [P, S])
        names = ["nk", "lnk", "nrm", "rk", "nq", "lnq", "nrq", "rq", "dt", "ah", "ww", "w2", "s2", "p1", "n1", "den",
                 "num", "rdn", "ratio", "lr", "ell", "mm", "m2", "n1s", "nsq", "flag", "lnsq", "yy", "t1", "t2", "t3",
                 "c1", "l1", "rt", "vp", "vr1", "vr2", "vr3", "brk", "wt", "ct", "gq", "rr", "r2", "cc", "dd", "t4",
                 "t5", "t6", "t7", "t8"]
        q_flat = q_stack[:, :, :].rearrange("p h k -> p (h k)").bitcast(F32)
        room = [q_flat[:, S * i:S * (i + 1)] for i in range(32)] + [probs_flat[:, S * i:S * (i + 1)] for i in range(24)]
        T = dict(zip(names, room))
        ab, ee, uu, lnu, corr, sp = (pair(v_flat, 3 + i) for i in range(6))
        elds = sb("elds", [P, 1])
        ph = [pair(ks_flat, i) for i in range(2)]
        pa, pbb = pair(ks_flat, 2), pair(ks_flat, 3)
        dot_junk = sb("dot_junk", [P, C, HD + 1])
        terms = sb("terms", [P, HD, SLOT])
        gst = sb("gst", [P, 8, 6])
        gmv = sb("gmv", [P, 8, 2])
        gmean = sb("gmean", [P, 8])
        gdm = sb("gdm", [P, 8])
        gdv = sb("gdv", [P, 8])
        gln = sb("gln", [P, 8])
        grs = sb("grs", [P, 8])
        gsc = sb("gsc", [P, 8])
        gbi = sb("gbi", [P, 8])
        yn = sigc
        y2 = conv
        x2 = xb
        x2b = x1h
        am = sb("am", [P, 1])
        amx = sb("amx", [P, 1])
        fsc = sb("fsc", [P, 1])
        finv = sb("finv", [P, 1])
        fq = sb("fq", [P, DM])
        res = ks_flat[:, 2048:2560].rearrange("p (b d) -> p b d", b=NB)

        mask_sum = sb("mask_sum", [P, 1])
        some_open = sb("some_open", [P, 1])
        go_general = sb("go_general", [1, 1], I32)
        q_cur = k_stack[1][:, :, 0:S]
        q_raw = k_stack[2][:, :, 0:S]
        m_blk = sb("m_blk", [P, H])
        m_run = sb("m_run", [P, H])
        m_new = sb("m_new", [P, H])
        fade_arg = sb("fade_arg", [P, H])
        fade = sb("fade", [P, H])
        o_run = sb("o_run", [P, H, DH + 1])

        SA = [pb(f"SA{i}", [P, BLK]) for i in range(2)]
        SB = [pb(f"SB{i}", [P, 2, BLK]) for i in range(2)]
        MI = pb("MI", [P, BLK])
        OT = pb("OT", [P, BLK])

        s_x, s_vec, s_id, s_wq, s_wk, s_wv, s_wo, s_rows = (sem(n) for n in (
            "s_x", "s_vec", "s_id", "s_wq", "s_wk", "s_wv", "s_wo", "s_rows"))
        s_ctx = [sem(f"s_ctx{i}") for i in range(2)]
        s_mask = sem("s_mask")
        s_mask_rest = sem("s_mask_rest")
        s_late = sem("s_late")
        dve_early = sem("dve_early")
        kst0_filled = sem("kst0_filled")
        kst_filled = sem("kst_filled")
        qst_filled = sem("qst_filled")
        ot_zeroed = sem("ot_zeroed")
        consts_ready = sem("consts_ready")
        mask_ready = sem("mask_ready")
        v_ones_set = sem("v_ones_set")
        ln_var = sem("ln_var")
        ln_rstd = sem("ln_rstd")
        xn_ready = sem("xn_ready")
        xnT_done = sem("xnT_done")
        xnT_copied = sem("xnT_copied")
        q_done = sem("q_done")
        q_copied = sem("q_copied")
        q_split_done = sem("q_split_done")
        q_stacked = sem("q_stacked")
        q_stacked_lo = sem("q_stacked_lo")
        k_done = sem("k_done")
        k_copied = sem("k_copied")
        k_split_done = sem("k_split_done")
        k_stacked = [sem(f"k_stacked{b}") for b in range(NB)]
        v_done = sem("v_done")
        v_copied = sem("v_copied")
        score_done = sem("score_done")
        max_done = sem("max_done")
        mneg_done = sem("mneg_done")
        mT_done = sem("mT_done")
        mT_copied = sem("mT_copied")
        m_stacked = sem("m_stacked")
        unit_scored = sem("unit_scored")
        unit_exp = sem("unit_exp")
        unit_pv = sem("unit_pv")
        o_copied = sem("o_copied")
        oT_done = sem("oT_done")
        attn_done = sem("attn_done")
        aT_done = sem("aT_done")
        aT_copied = sem("aT_copied")
        wo_done = sem("wo_done")
        x1_done = sem("x1_done")
        stored = sem("stored")
        act_done = sem("act_done")
        xb_done = sem("xb_done")

        ms_done = sem("ms_done")
        rms_done = sem("rms_done")
        xg_done = sem("xg_done")
        xg_copied = sem("xg_copied")
        kp_done = sem("kp_done")
        kp_copied = sem("kp_copied")
        vp_done = sem("vp_done")
        vp_copied = sem("vp_copied")
        z_done = sem("z_done")
        conv_done = sem("conv_done")
        sigc_done = sem("sigc_done")
        xc_done = sem("xc_done")
        sigz_done = sem("sigz_done")
        gate_done = sem("gate_done")
        gate_copied = sem("gate_copied")
        qp_done = sem("qp_done")
        qp_copied = sem("qp_copied")
        pad_zeroed = sem("pad_zeroed")
        k_stored = sem("k_stored")
        v_stored = sem("v_stored")
        g_stored = sem("g_stored")
        q_stored = sem("q_stored")
        k_loaded = sem("k_loaded")
        v_loaded = sem("v_loaded")
        g_loaded = sem("g_loaded")
        q_loaded = sem("q_loaded")
        ksq_done = sem("ksq_done")
        qsq_done = sem("qsq_done")
        nk_done = sem("nk_done")
        nq_done = sem("nq_done")
        knorm_done = sem("knorm_done")
        qnorm_done = sem("qnorm_done")
        abs_done = sem("abs_done")
        u_done = sem("u_done")
        ratio_done = sem("ratio_done")
        nsq_done = sem("nsq_done")
        ell_done = sem("ell_done")
        c1_done = sem("c1_done")
        parts_done = sem("parts_done")
        y_done = sem("y_done")
        gst_done = sem("gst_done")
        gm_done = sem("gm_done")
        gdv_done = sem("gdv_done")
        gv_done = sem("gv_done")
        grs_done = sem("grs_done")
        gbi_done = sem("gbi_done")
        yn_done = sem("yn_done")
        y2_done = sem("y2_done")
        o2_done = sem("o2_done")
        x2_done = sem("x2_done")
        ffn_done = sem("ffn_done")
        res_done = sem("res_done")
        am_done = sem("am_done")
        amx_done = sem("amx_done")
        ab_mm_done = sem("ab_mm_done")
        wrs_done = sem("wrs_done")
        h2_done = sem("h2_done")
        x1h_done = sem("x1h_done")
        sig_g = sem("sig_g")
        exp_g = sem("exp_g")
        ln_g = sem("ln_g")
        mm_g = sem("mm_g")
        sum_done = sem("sum_done")
        open_done = sem("open_done")
        count_done = sem("count_done")
        flag_done = sem("flag_done")
        g_ctx = sem("g_ctx")
        g_mask = sem("g_mask")
        g_kproj = sem("g_kproj")
        g_kcopied = sem("g_kcopied")
        g_ksplit = sem("g_ksplit")
        g_kstacked = sem("g_kstacked")
        g_vproj = sem("g_vproj")
        g_vcopied = sem("g_vcopied")
        g_maskset = sem("g_maskset")
        g_q = sem("g_q")
        bank_set = sem("bank_set")
        m_scan_done = sem("m_scan_done")
        m_spread = sem("m_spread")
        g_masked = sem("g_masked")
        g_fade_arg = sem("g_fade_arg")
        g_fade = sem("g_fade")
        g_merged = sem("g_merged")
        g_step = sem("g_step")
        dve_post = sem("dve_post")

        def col(name, n=P):
            return vec_sb[0:n, VEC[name]:VEC[name] + 1]

        block = ctx.enter_context(nc.Block())

        @block.sync
        def _(sp):
            sp.dma_start(x_sb[:, :, :], x.rearrange("b s d -> s b d")).then_inc(s_x, 16)
            sp.dma_start(wk_sb[:, :], wk).then_inc(s_wk, 16)
            sp.dma_start(ctx_sb[:, 0, :], ctx_t[0, :, NK - BLK:NK]).then_inc(s_ctx[0], 16)
            sp.dma_start(wq_sb[:, :], wq).then_inc(s_wq, 16)
            sp.dma_start(ctx_sb[:, 1:NB, :], ctx_t[1:NB, :, NK - BLK:NK].rearrange("b d k -> d b k")).then_inc(s_ctx[1], 16)
            sp.dma_start(wv_sb[:, :], wv).then_inc(s_wv, 16)
            sp.dma_start(rows_sb[:, :, :], rows).then_inc(s_rows, 16)
            sp.dma_start(wo_sb[:, :], wo).then_inc(s_wo, 16)
            for b in range(NB):
                sp.wait_ge(k_split_done, b + 1)
                sp.wait_ge(kst_filled if b else kst0_filled, b or 3)
                for t in range(NTERM):
                    sp.dma_start(k_stack[b][DH * t:DH * (t + 1), :, :], k_split[:, b, K_LEVEL[t], :])\
                      .then_inc(k_stacked[b], 16)
            sp.wait_ge(flag_done, 1)
            with sp.If(sp.value_load(go_general[0:1, 0:1]) != 0):
                for b in range(NB):
                    sp.wait_ge(k_stacked[b], 16 * NTERM)
                sp.wait_ge(mask_ready, NB)
                with sp.Fori(0, NB) as b:
                    with sp.Fori(0, NBLK) as k:
                        n = b * NBLK + k
                        sp.wait_ge(g_merged, n + 1)
                        sp.dma_start(ctx_sb[:, 0, :], ctx_t[bass.ds(b, 1), :, bass.ds(k * BLK, BLK)]
                                     .rearrange("o d k -> d (o k)")).then_inc(g_ctx, 16)
                        sp.dma_start(mask_sb[:, 0, 0:BLK], mask[bass.ds(b, 1), :, bass.ds(k * BLK, BLK)]
                                     .rearrange("o q k -> q (o k)")).then_inc(g_mask, 16)
                        sp.wait_ge(g_ksplit, n + 1)
                        for t in range(NTERM):
                            sp.dma_start(k_stack[0][DH * t:DH * (t + 1), :, :], k_split[:, 0, K_LEVEL[t], :])\
                              .then_inc(g_kstacked, 16)
                        sp.wait_ge(mT_copied, n + 2)
                        sp.dma_start(q_cur[MROW:MROW + 3, :, :], m_t[:, 0, :]).then_inc(m_stacked, 16)
            with sp.Else():
                sp.nop()
            sp.nop()
            sp.wait_ge(x1_done, 1)
            for dst, src in ((w_in_sb[:, :], w_in), (w_gate_sb[:, :, :], w_gate), (w_q_sb[:, :, :], w_q),
                             (w_rd[:, :, :], w_read[0]), (w_rs[:, :, :], w_read[1]), (w_out_sb[:, :, :], w_out),
                             (fw_sb[:, :], ffn_w), (fat_sb[:, :], ffn_at), (fb_sb[:, :], ffn_b), (avg_sb[:, :], avg)):
                sp.dma_start(dst, src).then_inc(s_late, 16)
            sp.wait_ge(kp_copied, 2)
            sp.dma_start(scratch[ROW_K:ROW_K + DI, :].rearrange("(i p) t -> p i t", i=2), kq_rows[:, 0:2, :])\
                .then_inc(k_stored, 16)
            sp.wait_ge(vp_copied, 1)
            sp.dma_start(scratch[ROW_V:ROW_V + 2 * H, :], v_rows).then_inc(v_stored, 16)
            sp.wait_ge(k_stored, 16)
            for s in range(2):
                sp.dma_start(k_ch[64 * s:64 * (s + 1), :],
                             scratch[ROW_K:ROW_K + DI, :].rearrange("(h d) (b t) -> b h d t", d=HD, b=NB))\
                    .then_inc(k_loaded, 16)
            sp.wait_ge(gate_copied, 1)
            sp.dma_start(scratch[ROW_G:ROW_G + 7 * H, :], g_rows).then_inc(g_stored, 16)
            sp.wait_ge(v_stored, 16)
            v_src = scratch[ROW_V:ROW_V + 2 * H, :].rearrange("(h s) (b t) -> s b h t", s=2, b=NB)
            for s in range(2):
                sp.dma_start(v_own[64 * s:64 * (s + 1), :], v_src[s]).then_inc(v_loaded, 16)
                sp.dma_start(v_swap[64 * s:64 * (s + 1), :], v_src[1 - s]).then_inc(v_loaded, 16)
            sp.wait_ge(g_stored, 16)
            for s in range(2):
                sp.dma_start(g_ch[64 * s:64 * (s + 1), :, :],
                             scratch[ROW_G:ROW_G + 7 * H, :].rearrange("(h g) (b t) -> b h g t", g=7, b=NB))\
                    .then_inc(g_loaded, 16)
            sp.wait_ge(qp_copied, 2)
            sp.dma_start(scratch[ROW_Q:ROW_Q + DI, :].rearrange("(i p) t -> p i t", i=2), kq_rows[:, 2:4, :])\
                .then_inc(q_stored, 16)
            sp.wait_ge(q_stored, 16)
            for s in range(2):
                sp.dma_start(q_ch[64 * s:64 * (s + 1), :],
                             scratch[ROW_Q:ROW_Q + DI, :].rearrange("(h d) (b t) -> b h d t", d=HD, b=NB))\
                    .then_inc(q_loaded, 16)
            sp.wait_ge(res_done, 1)
            sp.dma_start(out.rearrange("b s d -> s b d"), res[:, :, :]).then_inc(stored, 16)
            sp.wait_ge(stored, 16)

        @block.gpsimd
        def _(pool):
            pool.memset(q_stack[:, :, :].bitcast(F32), 0.0).then_inc(qst_filled, 1)
            pool.memset(v_ones[:, :, :, :, DH:DH + 1], 1.0).then_inc(v_ones_set, 1)
            pool.memset(k_stack[1][:, :, :].bitcast(F32), ONES_PAIR).then_inc(kst_filled, 1)
            pool.wait_ge(q_split_done, 1)
            pool.wait_ge(qst_filled, 1)
            for t in range(NTERM // 2, NTERM):
                pool.dma_start(q_stack[DH * t:DH * (t + 1), :, :], q_split[:, Q_LEVEL[t], :])\
                    .then_inc(q_stacked, 16)
            for b in range(NB):
                pool.wait_ge(s_mask, 16)
                last = NK - BLK
                pool.tensor_scalar(mask_neg[:, b, :], mask_sb[:, b, last:NK], -BIG, 1.0, ALU.mult, ALU.mult)
                pool.tensor_scalar(mask_bf[:, b, :], mask_sb[:, b, last:NK], 1.0, 1.0, ALU.mult, ALU.mult)\
                    .then_inc(mask_ready, 1)
                if b == 0:
                    for later in (2, 3):
                        pool.memset(k_stack[later][:, :, :].bitcast(F32), ONES_PAIR).then_inc(kst_filled, 1)
            pool.wait_ge(s_x, 16)
            pool.wait_ge(s_rows, 16)
            for b in range(NB):
                pool.tensor_tensor(xb[:, b, :], x_sb[:, b, :], rows_sb[:, 1, :], ALU.add).then_inc(xb_done, 1)
            pool.nop()
            pool.wait_ge(x1_done, NB)
            pool.memset(xg[:, :, :, 0:3], 0.0).then_inc(pad_zeroed, 1)
            pool.memset(bank[:, HD, :], 1.0).then_inc(bank_set, 1)
            pool.memset(bank[:, 0:HD, 0:1], 0.0).then_inc(bank_set, 1)
            pool.wait_ge(s_late, 160)
            pool.tensor_scalar(w_rs[:, :, :], w_rs[:, :, :], col("sgn"), 1.0, ALU.mult, ALU.mult).then_inc(wrs_done, 1)
            pool.wait_ge(k_loaded, 32)
            pool.tensor_copy(bank_c[:, 0:HD, 0:NC, C:C + 1], chunked(k_ch, C)[:, :, :, C - 1:C]).then_inc(bank_set, 1)
            pool.wait_ge(am_done, 1)
            pool.partition_all_reduce(amx[:, :], am[:, :], P, bass.bass_isa.ReduceOp.max).then_inc(amx_done, 1)
            pool.wait_ge(h2_done, NB)
            pool.tensor_tensor(x1h[:, :, :], x1[:, :, :], hn[:, :, :], ALU.add).then_inc(x1h_done, 1)

        @block.scalar
        def _(act):
            act.dma_start(vec_sb[:, :], vec).then_inc(s_vec, 16)
            act.dma_start(id_sb[:, :], ident).then_inc(s_id, 16)
            act.preload_act_table_set("natural_log_exp_and_others")
            act.wait_ge(s_vec, 16)
            act.wait_ge(ln_var, 1)
            nc.scalar.activation(lnv[:, :], mv[:, :, 1], ACT.Ln, bias=col("eps_ln")).then_inc(act_done, 1)
            act.wait_ge(act_done, 1)
            nc.scalar.activation(rstd[:, :], lnv[:, :], ACT.Exp, scale=-0.5).then_inc(ln_rstd, 1)

            def k_evac(b):
                act.wait_ge(k_done, b + 1)
                src = SB[b // 2][:, b % 2, :]
                nc.scalar.activation(k_f[:, b, :], src, ACT.Identity, bias=col("bk")).then_inc(k_copied, 1)
                nc.scalar.activation(k_split[:, b, 0, :], src, ACT.Identity, bias=col("bk")).then_inc(k_copied, 1)

            k_evac(0)
            act.wait_ge(xnT_done, 1)
            nc.scalar.activation(xn_t[:, :], MI[:, :], ACT.Copy).then_inc(xnT_copied, 1)
            act.wait_ge(q_done, 1)
            nc.scalar.activation(q_f[:, :], SA[0][:, :], ACT.Identity, bias=col("bq")).then_inc(q_copied, 1)
            nc.scalar.activation(q_split[:, 0, :], SA[0][:, :], ACT.Identity, bias=col("bq")).then_inc(q_copied, 1)
            k_evac(1)
            mask_q = mask.rearrange("b q k -> q b k")
            act.dma_start(mask_sb[:, :, NK - BLK:NK], mask_q[:, :, NK - BLK:NK]).then_inc(s_mask, 16)
            act.dma_start(mask_sb[:, :, 0:NK - BLK], mask_q[:, :, 0:NK - BLK]).then_inc(s_mask_rest, 16)
            act.wait_ge(q_split_done, 1)
            act.wait_ge(qst_filled, 1)
            for t in range(NTERM // 2):
                act.dma_start(q_stack[DH * t:DH * (t + 1), :, :], q_split[:, Q_LEVEL[t], :]).then_inc(q_stacked_lo, 16)
            k_evac(2)
            k_evac(3)

            def v_evac(b):
                act.wait_ge(v_done, b + 1)
                nc.scalar.activation(v_ones[:, b, :, :, 0:DH],
                                     SB[b // 2][:, b % 2, :].rearrange("p (t h d) -> p t h d", t=KT, h=H), ACT.Copy)\
                    .then_inc(v_copied, 1)

            act.wait_ge(v_ones_set, 1)
            for b in range(NB):
                v_evac(b)
            def m_evac(b):
                act.wait_ge(mT_done, b + 1)
                nc.scalar.activation(m_t[:, b, :], MI[0:3 * H, 0:S // 2].bitcast(BF16), ACT.Copy).then_inc(mT_copied, 1)

            def m_stack(b):
                act.wait_ge(mT_copied, b + 1)
                act.dma_start(q_stack[MROW:MROW + 3, :, S * b:S * (b + 1)], m_t[:, b, :]).then_inc(m_stacked, 16)

            act.wait_ge(s_mask_rest, 16)
            nc.scalar.activation(probs_flat.bitcast(BF16)[:, 0:NB * (NK - BLK) // 2].rearrange("p (b k) -> p b k", b=NB),
                                 mask_sb[:, :, 0:NK - BLK].bitcast(U16), ACT.Copy, accum_out=mask_sum[:, :])\
                .then_inc(sum_done, 1)

            def general_block(n):
                act.wait_ge(g_kproj, n + 1)
                for dst in (k_f[:, 0, :], k_split[:, 0, 0, :]):
                    nc.scalar.activation(dst, SB[0][:, 0, :], ACT.Identity, bias=col("bk")).then_inc(g_kcopied, 1)
                act.wait_ge(g_fade_arg, n + 1)
                nc.scalar.activation(fade[:, :], fade_arg[:, :], ACT.Exp, scale=SCALE).then_inc(g_fade, 1)
                act.wait_ge(mT_done, n + 2)
                nc.scalar.activation(m_t[:, 0, :], MI[0:3 * H, 0:S], ACT.Copy).then_inc(mT_copied, 1)
                for u in range(UNITS):
                    act.wait_ge(unit_scored, n * UNITS + u + 1)
                    if u >= 2:
                        act.wait_ge(unit_pv, n * UNITS + u - 1)
                    nc.scalar.activation(probs[:, u % 2, :, :],
                                         SB[u % 2][:, :, :].rearrange("p a (c s) -> p (a c) s", c=4),
                                         ACT.Exp, scale=SCALE).then_inc(unit_exp, 1)
                act.wait_ge(unit_pv, n * UNITS + UNITS)
                nc.scalar.activation(o_sb[:, 0, :], OT[:, :], ACT.Copy).then_inc(o_copied, 1)

            m_evac(0)
            act.wait_ge(flag_done, 1)
            with act.If(act.value_load(go_general[0:1, 0:1]) != 0):
                with act.Fori(0, NB) as b:
                    with act.Fori(0, NBLK) as k:
                        general_block(b * NBLK + k)
                    act.wait_ge(aT_done, b + 1)
                    nc.scalar.activation(attn_t[:, 0, :], MI[:, 0:S], ACT.Copy).then_inc(aT_copied, 1)
            with act.Else():
                m_stack(0)
                for b in range(NB):
                    for u in range(8):
                        n = 8 * b + u
                        act.wait_ge(unit_scored, n + 1)
                        if n >= 3:
                            act.wait_ge(unit_pv, n - 2)
                        nc.scalar.activation(probs[:, n % 3, :, :], SB[n % 2][:, :, :].rearrange("p a (c s) -> p (a c) s", c=4),
                                             ACT.Exp, scale=SCALE).then_inc(unit_exp, 1)
                        if u == 2 and b >= 1:
                            act.wait_ge(aT_done, b)
                            nc.scalar.activation(attn_t[:, (b - 1) % 2, :], MI[:, 0:S], ACT.Copy).then_inc(aT_copied, 1)
                        if u == 4 and b + 1 < NB:
                            m_evac(b + 1)
                            m_stack(b + 1)
                    act.wait_ge(unit_pv, 8 * b + 8)
                    nc.scalar.activation(o_sb[:, b % 2, :], OT[:, :], ACT.Copy).then_inc(o_copied, 1)
                act.wait_ge(aT_done, NB)
                nc.scalar.activation(attn_t[:, (NB - 1) % 2, :], MI[:, 0:S], ACT.Copy).then_inc(aT_copied, 1)

            act.nop()

            def root_recip(dst, tmp, src, eps, ready, value, done):
                act.wait_ge(ready, value)
                n = act_n[0] = act_n[0] + 1
                nc.scalar.activation(tmp, src, ACT.Ln, bias=eps).then_inc(act_done, 1)
                act.wait_ge(act_done, n)
                nc.scalar.activation(dst, tmp, ACT.Exp, scale=-0.5).then_inc(done, 1)

            act_n = [1]
            root_recip(rstd[:, :], lnv[:, :], mv[:, :, 1], col("eps_ln"), ln_var, 2, ln_rstd)
            root_recip(rms_r[:, :], lnv[:, :], ms[:, :], col("eps_rms"), ms_done, 1, rms_done)
            act.wait_ge(xnT_done, 2)
            nc.scalar.activation(xr_t[:, :], MI[:, :], ACT.Copy, scale=col("rms")).then_inc(xnT_copied, 1)
            act.wait_ge(pad_zeroed, 1)
            for i in range(2):
                act.wait_ge(xg_done, i + 1)
                nc.scalar.activation(xg[:, i, :, 3:], SB[0][:, i, :].rearrange("p (b t) -> p b t", b=NB), ACT.Identity,
                                     bias=col(f"xg_b{i}")).then_inc(xg_copied, 1)
            for i in range(2):
                act.wait_ge(conv_done, i + 1)
                nc.scalar.activation(sigc[:, i, :], conv[:, i, :], ACT.Sigmoid).then_inc(sigc_done, 1)
            for i in range(2):
                act.wait_ge(z_done, i + 1)
                nc.scalar.activation(sigz[:, i, :], (SA[1], OT)[i][:, :], ACT.Sigmoid, bias=col(f"z_b{i}"))\
                    .then_inc(sigz_done, 1)
            act.wait_ge(gate_done, 1)
            nc.scalar.activation(g_rows, MI[0:7 * H, :], ACT.Identity, bias=col("gate_b", 7 * H)).then_inc(gate_copied, 1)
            act.wait_ge(qp_done, 2)
            nc.scalar.activation(kq_rows[:, 3, :], SB[0][:, 1, :], ACT.Copy).then_inc(qp_copied, 1)
            act.wait_ge(k_loaded, 32)
            nc.scalar.activation(sq, k_ch, ACT.Square).then_inc(ksq_done, 1)
            act.wait_ge(g_loaded, 32)
            nc.scalar.activation(sig_om[:, :], g_ch[:, 1, :], ACT.Sigmoid, scale=2.0).then_inc(sig_g, 1)
            nc.scalar.activation(sig_bc[:, :, :], g_ch[:, 2:4, :], ACT.Sigmoid).then_inc(sig_g, 1)
            nc.scalar.activation(sig_br[:, :, :], g_ch[:, 5:7, :], ACT.Sigmoid).then_inc(sig_g, 1)
            nc.scalar.activation(ab[:, :, :], g_ch[:, 0:5:4, :], ACT.Abs).then_inc(abs_done, 1)
            act.wait_ge(abs_done, 1)
            nc.scalar.activation(ee[:, :, :], ab[:, :, :], ACT.Exp, scale=-1.0).then_inc(exp_g, 1)
            nc.scalar.activation(elds[:, :], col("log_dt"), ACT.Exp).then_inc(exp_g, 1)
            act.wait_ge(u_done, 1)
            nc.scalar.activation(lnu[:, :, :], uu[:, :, :], ACT.Ln).then_inc(ln_g, 1)

            def root(dst, tmp, src, ready, done):
                act.wait_ge(ready, 1)
                n = act_n[0] = act_n[0] + 1
                nc.scalar.activation(tmp, src, ACT.Ln, scale=2.0 ** 30).then_inc(act_done, 1)
                act.wait_ge(act_done, n)
                nc.scalar.activation(dst, tmp, ACT.Exp, scale=0.5, bias=col("root_shift")).then_inc(done, 1)

            root(T["nrm"][:, :], T["lnk"][:, :], T["nk"][:, :], nk_done, knorm_done)
            act.wait_ge(ratio_done, 1)
            nc.scalar.activation(T["lr"][:, :], T["ratio"][:, :], ACT.Ln).then_inc(ln_g, 1)
            act.wait_ge(nsq_done, 1)
            n = act_n[0] = act_n[0] + 1
            nc.scalar.activation(T["lnsq"][:, :], T["nsq"][:, :], ACT.Ln).then_inc(act_done, 1)
            act.wait_ge(act_done, n)
            nc.scalar.activation(T["yy"][:, :], T["lnsq"][:, :], ACT.Exp, scale=-0.5).then_inc(mm_g, 1)
            act.wait_ge(ell_done, 1)
            nc.scalar.activation(T["mm"][:, :], T["ell"][:, :], ACT.Exp).then_inc(mm_g, 1)
            nc.scalar.activation(T["m2"][:, :], T["ell"][:, :], ACT.Exp, scale=2.0).then_inc(mm_g, 1)
            act.wait_ge(c1_done, 1)
            n = act_n[0] = act_n[0] + 1
            nc.scalar.activation(T["l1"][:, :], T["c1"][:, :], ACT.Ln).then_inc(act_done, 1)
            act.wait_ge(act_done, n)
            nc.scalar.activation(T["rt"][:, :], T["l1"][:, :], ACT.Exp, scale=0.5).then_inc(mm_g, 1)
            act.wait_ge(m_scan_done, 1)
            nc.scalar.activation(by_t(m_full), m_scan.rearrange("p (o t) -> p o t", o=1).to_broadcast([P, HD, S]), ACT.Copy)\
                .then_inc(m_spread, 1)
            act.wait_ge(q_loaded, 32)
            act.wait_ge(nk_done, 1)
            nc.scalar.activation(sq, q_ch, ACT.Square).then_inc(qsq_done, 1)
            root(T["nrq"][:, :], T["lnq"][:, :], T["nq"][:, :], nq_done, qnorm_done)
            root_recip(grs[:, :], gln[:, :], MI[:, 8:16], col("eps_ln"), gv_done, 1, grs_done)
            for i in range(2):
                act.wait_ge(gbi_done, i + 1)
                for b in range(NB):
                    j = NB * i + b
                    nc.scalar.activation(yn[:, i, S * b:S * (b + 1)], SB[0][:, i, S * b:S * (b + 1)], ACT.Identity,
                                         scale=gsc[:, j:j + 1], bias=gbi[:, j:j + 1]).then_inc(yn_done, 1)
            root_recip(rstd[:, :], lnv[:, :], mv[:, :, 1], col("eps_ln"), ln_var, 3, ln_rstd)
            act.wait_ge(xnT_done, 3)
            nc.scalar.activation(xn_t[:, :], MI[:, :], ACT.Copy).then_inc(xnT_copied, 1)

        @block.vector
        def _(dve):
            count = [0]
            dve_done = dve_early

            def step(ins):
                count[0] += 1
                ins.then_inc(dve_done, 1)

            def link(ins):
                step(ins)
                dve.wait_ge(dve_done, count[0])

            nc.vector.memset(OT[:, :], 0.0).then_inc(ot_zeroed, 1)
            k0_filler = k_stack[0][:, :, :].rearrange("p h k -> p (h k)").bitcast(F32)
            nc.vector.memset(k0_filler[:, 0:1024], ONES_PAIR).then_inc(kst0_filled, 1)
            dve.wait_ge(s_x, 16)
            for b in range(NB):
                step(nc.vector.bn_stats(stats[:, b, :], x_sb[:, b, :]))
            dve.wait_ge(dve_done, count[0])
            for b in range(NB):
                last = nc.vector.bn_aggr(mv[:, b, :], stats[:, b, :])
                if b < NB - 1:
                    step(last)
            last.then_inc(ln_var, 1)
            dve.wait_ge(dve_done, count[0])
            nc.vector.memset(k0_filler[:, 1024:2048], ONES_PAIR).then_inc(kst0_filled, 1)
            dve.wait_ge(ln_rstd, 1)
            for b in range(NB):
                nc.vector.tensor_scalar(xn[:, b, :], x_sb[:, b, :], mv[:, b, 0:1], rstd[:, b:b + 1],
                                        ALU.subtract, ALU.mult).then_inc(xn_ready, 1)

            nc.vector.memset(k0_filler[:, 2048:4096], ONES_PAIR).then_inc(kst0_filled, 1)

            def k_levels(b):
                dve.wait_ge(k_copied, 2 * b + 2)
                link(nc.vector.tensor_tensor(k_r[:, :], k_f[:, b, :], k_split[:, b, 0, :], ALU.subtract))
                link(nc.vector.tensor_copy(k_split[:, b, 1, :], k_r[:, :]))
                nc.vector.tensor_tensor(k_split[:, b, 2, :], k_r[:, :], k_split[:, b, 1, :], ALU.subtract)\
                    .then_inc(k_split_done, 1)
                dve.wait_ge(k_split_done, b + 1)

            k_levels(0)
            dve.wait_ge(q_copied, 2)
            link(nc.vector.tensor_tensor(q_r[:, :], q_f[:, :], q_split[:, 0, :], ALU.subtract))
            link(nc.vector.tensor_copy(q_split[:, 1, :], q_r[:, :]))
            nc.vector.tensor_tensor(q_split[:, 2, :], q_r[:, :], q_split[:, 1, :], ALU.subtract).then_inc(q_split_done, 1)
            dve.wait_ge(s_id, 16)
            link(nc.vector.tensor_copy(id_bf[:, :], id_sb[:, :]))
            for j in range(4):
                nc.vector.tensor_scalar(neg_id4[:, j, :], id_sb[:, :], -BIG, None, ALU.mult).then_inc(consts_ready, 1)
            k_levels(1)

            def head_max(n):
                b, h = divmod(n, H)
                dve.wait_ge(score_done, n + 1)
                if h == 0:
                    dve.wait_ge(mask_ready, b + 1)
                if n >= 2:
                    dve.wait_ge(max_done, n - 1)
                nc.vector.tensor_tensor_reduce(junk[:, n % 2, :], SA[n % 2][:, :], mask_neg[:, b, :], 1.0, -3.0e38,
                                               ALU.add, ALU.max, mx[:, b, h:h + 1]).then_inc(max_done, 1)

            def negate_max(b):
                dve.wait_ge(max_done, H * (b + 1))
                link(nc.vector.tensor_scalar(mflag[:, :], mx[:, b, :], -0.5 * BIG, 2.0 * BIG, ALU.is_lt, ALU.mult))
                link(nc.vector.scalar_tensor_tensor(mneg[:, :], mx[:, b, :], -1.0, mflag[:, :], ALU.mult, ALU.subtract))
                link(nc.vector.tensor_copy(m_split[:, b, 0:H], mneg[:, :]))
                link(nc.vector.tensor_tensor(mrest[:, :], mneg[:, :], m_split[:, b, 0:H], ALU.subtract))
                link(nc.vector.tensor_copy(m_split[:, b, H:2 * H], mrest[:, :]))
                nc.vector.tensor_tensor(m_split[:, b, 2 * H:3 * H], mrest[:, :], m_split[:, b, H:2 * H], ALU.subtract)\
                    .then_inc(mneg_done, 1)
                dve.wait_ge(mneg_done, b + 1)

            def normalise(b):
                dve.wait_ge(oT_done, b + 1)
                o_v = MI[:, :].rearrange("p (h e) -> p h e", h=H)
                link(nc.vector.reciprocal(rden[:, :].rearrange("p (h e) -> p h e", e=1), o_v[:, :, DH:DH + 1]))
                link(nc.vector.tensor_tensor(attn[:, b % 2, :].rearrange("p (h d) -> p h d", h=H), o_v[:, :, 0:DH],
                                             rden[:, :].rearrange("p (h e) -> p h e", e=1).to_broadcast([P, H, DH]),
                                             ALU.mult))
                nc.vector.tensor_tensor(attn[:, b % 2, :], attn[:, b % 2, :], rows_sb[:, 0, :], ALU.add).then_inc(attn_done, 1)

            def residual(b):
                dve.wait_ge(wo_done, b + 1)
                dve.wait_ge(xb_done, NB)
                nc.vector.tensor_tensor(x1[:, b, :], MI[:, 0:DM], xb[:, b, :], ALU.add).then_inc(x1_done, 1)

            for h in range(10):
                head_max(h)
            dve.wait_ge(sum_done, 1)
            nc.vector.tensor_scalar(some_open[:, :], mask_sum[:, :], float(ALL_MASKED), None, ALU.is_lt).then_inc(open_done, 1)
            for h in range(10, 14):
                head_max(h)
            dve.wait_ge(count_done, 1)
            nc.vector.tensor_copy(go_general[:, :], MI[0:1, 0:1]).then_inc(flag_done, 1)
            for h in range(14, H):
                head_max(h)
            negate_max(0)
            k_levels(2)
            k_levels(3)
            dve.wait_ge(s_rows, 16)
            V = nc.vector

            def general_block(n):
                dve.wait_ge(g_merged, n + 1)
                dve.wait_ge(g_kcopied, 2 * n + 2)
                g_n = n * 15
                V.tensor_tensor(k_r[:, :], k_f[:, 0, :], k_split[:, 0, 0, :], ALU.subtract).then_inc(g_step, 1)
                dve.wait_ge(g_step, g_n + 1)
                V.tensor_copy(k_split[:, 0, 1, :], k_r[:, :]).then_inc(g_step, 1)
                dve.wait_ge(g_step, g_n + 2)
                V.tensor_tensor(k_split[:, 0, 2, :], k_r[:, :], k_split[:, 0, 1, :], ALU.subtract).then_inc(g_ksplit, 1)
                dve.wait_ge(g_vproj, n + 1)
                V.tensor_tensor(v_ones[:, 0, :, :, 0:DH], MI[:, :].rearrange("p (t h d) -> p t h d", t=KT, h=H),
                                rows_sb[:, 0, :].rearrange("p (o h d) -> p o h d", o=1, h=H).to_broadcast([P, KT, H, DH]),
                                ALU.add).then_inc(g_vcopied, 1)
                dve.wait_ge(g_mask, 16 * n + 16)
                V.tensor_scalar(mask_neg[:, 0, :], mask_sb[:, 0, 0:BLK], -BIG, None, ALU.mult).then_inc(g_step, 1)
                V.tensor_scalar(mask_bf[:, 0, :], mask_sb[:, 0, 0:BLK], 1.0, None, ALU.mult).then_inc(g_maskset, 1)
                dve.wait_ge(g_step, g_n + 3)
                for h in range(H):
                    dve.wait_ge(score_done, n * H + (H + h + 1))
                    if h >= 2:
                        dve.wait_ge(max_done, n * H + (H + h - 1))
                    masked = probs_flat[:, BLK * (h % 2):BLK * (h % 2) + BLK]
                    V.tensor_tensor(masked, SA[h % 2][:, :], mask_neg[:, 0, :], ALU.add).then_inc(g_masked, 1)
                    dve.wait_ge(g_masked, n * H + h + 1)
                    V.tensor_reduce(m_blk[:, h:h + 1], masked, AX.X, ALU.max).then_inc(max_done, 1)
                dve.wait_ge(max_done, n * H + 2 * H)
                V.tensor_tensor(m_new[:, :], m_blk[:, :], m_run[:, :], ALU.max).then_inc(g_step, 1)
                dve.wait_ge(g_step, g_n + 4)
                V.tensor_tensor(fade_arg[:, :], m_run[:, :], m_new[:, :], ALU.subtract).then_inc(g_fade_arg, 1)
                dve.wait_ge(g_fade_arg, n + 1)
                V.tensor_copy(m_run[:, :], m_new[:, :]).then_inc(g_step, 1)
                V.tensor_scalar(mflag[:, :], m_new[:, :], -0.5 * BIG, 2.0 * BIG, ALU.is_lt, ALU.mult).then_inc(g_step, 1)
                dve.wait_ge(g_step, g_n + 6)
                V.scalar_tensor_tensor(mneg[:, :], m_new[:, :], -1.0, mflag[:, :], ALU.mult, ALU.subtract).then_inc(g_step, 1)
                dve.wait_ge(g_step, g_n + 7)
                V.tensor_copy(m_split[:, 0, 0:H], mneg[:, :]).then_inc(g_step, 1)
                dve.wait_ge(g_step, g_n + 8)
                V.tensor_tensor(mrest[:, :], mneg[:, :], m_split[:, 0, 0:H], ALU.subtract).then_inc(g_step, 1)
                dve.wait_ge(g_step, g_n + 9)
                V.tensor_copy(m_split[:, 0, H:2 * H], mrest[:, :]).then_inc(g_step, 1)
                dve.wait_ge(g_step, g_n + 10)
                V.tensor_tensor(m_split[:, 0, 2 * H:3 * H], mrest[:, :], m_split[:, 0, H:2 * H], ALU.subtract).then_inc(mneg_done, 1)
                dve.wait_ge(g_fade, n + 1)
                V.tensor_tensor(o_run[:, :, :], o_run[:, :, :], fade[:, :].rearrange("p (h e) -> p h e", e=1)
                                .to_broadcast([P, H, DH + 1]), ALU.mult).then_inc(g_step, 1)
                dve.wait_ge(g_step, g_n + 11)
                dve.wait_ge(oT_done, n + 1)
                V.tensor_tensor(o_run[:, :, :], o_run[:, :, :], MI[:, :].rearrange("p (h e) -> p h e", h=H)[:, :, 0:DH + 1],
                                ALU.add).then_inc(g_step, 4)
                dve.wait_ge(g_step, g_n + 15)
                V.tensor_copy(m_blk[:, :], m_new[:, :]).then_inc(g_merged, 1)

            with dve.If(dve.value_load(go_general[0:1, 0:1]) != 0):
                dve.wait_ge(q_stacked, 16 * (NTERM // 2))
                dve.wait_ge(q_stacked_lo, 16 * (NTERM // 2))
                dve.wait_ge(k_stacked[1], 16 * NTERM)
                dve.wait_ge(k_stacked[2], 16 * NTERM)
                dve.wait_ge(mask_ready, NB)
                dve.wait_ge(xb_done, NB)
                V.memset(m_blk[:, :], 0.0).then_inc(g_merged, 1)
                V.memset(m_run[:, :], -3.0e38).then_inc(g_q, 1)
                V.memset(o_run[:, :, :], 0.0).then_inc(g_q, 1)
                with dve.Fori(0, NB) as b:
                    V.tensor_copy(q_cur, q_stack[:, :, bass.ds(b * S, S)]).then_inc(g_q, 1)
                    V.tensor_copy(q_raw, q_stack[:, :, bass.ds(b * S, S)]).then_inc(g_q, 1)
                    with dve.Fori(0, NBLK) as k:
                        dve.wait_ge(g_q, 4 * b + 4)
                        general_block(b * NBLK + k)
                    dve.wait_ge(g_merged, b * NBLK + NBLK + 1)
                    V.reciprocal(rden[:, :].rearrange("p (h e) -> p h e", e=1), o_run[:, :, DH:DH + 1]).then_inc(attn_done, 1)
                    dve.wait_ge(attn_done, 2 * b + 1)
                    V.tensor_tensor(attn[:, 0, :].rearrange("p (h d) -> p h d", h=H), o_run[:, :, 0:DH],
                                    rden[:, :].rearrange("p (h e) -> p h e", e=1).to_broadcast([P, H, DH]),
                                    ALU.mult).then_inc(attn_done, 1)
                    dve.wait_ge(wo_done, b + 1)
                    V.tensor_tensor(x1[:, bass.ds(b, 1), :].rearrange("p o d -> p (o d)"), MI[:, 0:DM],
                                    xb[:, bass.ds(b, 1), :].rearrange("p o d -> p (o d)"), ALU.add).then_inc(x1_done, 1)
                    dve.wait_ge(x1_done, b + 1)
                    V.memset(m_run[:, :], -3.0e38).then_inc(g_q, 1)
                    V.memset(o_run[:, :, :], 0.0).then_inc(g_q, 1)
            with dve.Else():
                for b in range(NB):
                    for u in range(8):
                        if b + 1 < NB and u < 4:
                            for h in range(4 * u, 4 * u + 4):
                                head_max(H * (b + 1) + h)
                        if u == 1 and b >= 1:
                            normalise(b - 1)
                        if u == 3 and b >= 1:
                            residual(b - 1)
                        if b + 1 < NB and u == 3:
                            negate_max(b + 1)
                normalise(NB - 1)
                residual(NB - 1)

            dve.nop()
            count[0] = 0
            dve_done = dve_post

            def need(n):
                dve.wait_ge(dve_done, n)

            def run(ins):
                step(ins)
                return count[0]

            def moments(nth):
                for b in range(NB):
                    a = run(V.bn_stats(stats[:, b, :], x_src[:, b, :]))
                need(a)
                for b in range(NB):
                    a = V.bn_aggr(mv[:, b, :], stats[:, b, :])
                    if b < NB - 1:
                        step(a)
                a.then_inc(ln_var, 1)
                dve.wait_ge(ln_var, nth)

            dve.wait_ge(x1_done, NB)
            x_src = x1
            moments(2)
            dve.wait_ge(ln_rstd, 2)
            need(count[0])
            a = run(V.tensor_tensor(ms[:, :], mv[:, :, 1], rstd[:, :], ALU.mult))
            need(a)
            V.tensor_tensor(ms[:, :], ms[:, :], rstd[:, :], ALU.mult).then_inc(ms_done, 1)
            dve.wait_ge(rms_done, 1)
            link(V.tensor_tensor(rq2[:, :], rstd[:, :], rms_r[:, :], ALU.mult))
            for b in range(NB):
                V.tensor_scalar(xr[:, b, :], x1[:, b, :], mv[:, b, 0:1], rq2[:, b:b + 1], ALU.subtract, ALU.mult)\
                    .then_inc(xn_ready, 1)
            for b in range(NB):
                V.tensor_scalar(hn[:, b, :], x1[:, b, :], mv[:, b, 0:1], rstd[:, b:b + 1], ALU.subtract, ALU.mult)\
                    .then_inc(h2_done, 1)
            dve.wait_ge(s_late, 160)
            V.tensor_reduce(am[:, :], fw_sb[:, :], AX.X, ALU.max, apply_absolute_value=True).then_inc(am_done, 1)

            dve.wait_ge(xg_copied, 1)
            for i in range(2):
                dve.wait_ge(xg_copied, i + 1)
                acc = conv[:, i, :].rearrange("p (b t) -> p b t", b=NB)
                link(V.tensor_scalar(acc, xg[:, i, :, 0:S], col(f"cw{i}0"), col(f"cb{i}"), ALU.mult, ALU.add))
                for j in range(1, 4):
                    last = V.scalar_tensor_tensor(acc, xg[:, i, :, j:j + S], col(f"cw{i}{j}"), acc, ALU.mult, ALU.add)
                    if j < 3:
                        link(last)
                last.then_inc(conv_done, 1)
                dve.wait_ge(kp_done, i + 1)
                V.tensor_scalar(kq_rows[:, i, :], SB[1][:, i, :], col(f"k_b{i}"), None, ALU.add).then_inc(kp_copied, 1)
            dve.wait_ge(vp_done, 1)
            V.tensor_scalar(v_rows, SA[0][0:2 * H, :], col("v_b", 2 * H), None, ALU.add).then_inc(vp_copied, 1)
            for i in range(2):
                dve.wait_ge(sigc_done, i + 1)
                V.tensor_tensor(xc[:, i, :], conv[:, i, :], sigc[:, i, :], ALU.mult).then_inc(xc_done, 1)
            for i in range(2):
                dve.wait_ge(sigz_done, i + 1)
                run(V.scalar_tensor_tensor(zs[:, i, :], (SA[1], OT)[i][:, :], col(f"z_b{i}"), sigz[:, i, :],
                                           ALU.add, ALU.mult))
            dve.wait_ge(qp_done, 1)
            V.tensor_copy(kq_rows[:, 2, :], SB[0][:, 0, :]).then_inc(qp_copied, 1)

            dve.wait_ge(amx_done, 1)
            link(V.tensor_scalar(fsc[:, :], amx[:, :], 1.0 / 7.0, None, ALU.mult))
            link(V.reciprocal(finv[:, :], fsc[:, :]))
            link(V.tensor_scalar(fq[:, :], fw_sb[:, :], finv[:, 0:1], None, ALU.mult))
            link(V.tensor_scalar(fq[:, :], fq[:, :], 12582912.0, -12582912.0, ALU.add, ALU.add))
            link(V.tensor_scalar(fq[:, :], fq[:, :], -8.0, 7.0, ALU.max, ALU.min))
            dve.wait_ge(ab_mm_done, 1)
            w_eff_at = run(V.scalar_tensor_tensor(w_eff[:, :], fq[:, :], fsc[:, 0:1], SB[1][:, 1, 0:DM], ALU.mult, ALU.add))

            t = lambda n: T[n][:, :]

            def tt(o, x0, x1_, op):
                return run(V.tensor_tensor(o, x0, x1_, op))

            dve.wait_ge(k_loaded, 32)
            need(count[0])
            kc = chunked(k_ch, C)
            g0 = spare[:, 0:HD * NC * 3].rearrange("p (d c j) -> p d c j", d=HD, j=3)
            g1 = pair_tmp[:, 0:HD * NC * 3].rearrange("p (d c j) -> p d c j", d=HD, j=3)
            gv = gram.rearrange("p (g c j) -> p g c j", g=2, j=3)
            dv = dcoef.rearrange("p (g c j) -> p g c j", g=2, j=3)
            run(V.tensor_tensor(g0, kc[:, :, :, 1:4], kc[:, :, :, 0:1].to_broadcast([P, HD, NC, 3]), ALU.mult))
            run(V.tensor_tensor(g1[:, :, :, 0:2], kc[:, :, :, 2:4], kc[:, :, :, 1:2].to_broadcast([P, HD, NC, 2]), ALU.mult))
            a = run(V.tensor_tensor(g1[:, :, :, 2:3], kc[:, :, :, 3:4], kc[:, :, :, 2:3], ALU.mult))
            need(a)
            for g, products in enumerate((g0, g1)):
                run(V.tensor_reduce(gv[:, g, :, :].rearrange("p c j -> p (c j)"),
                                    products.rearrange("p d c j -> p (c j) d"), AX.X, ALU.add))

            dve.wait_ge(ksq_done, 1)
            a = run(V.tensor_reduce(t("nk"), sq.rearrange("p (d t) -> p t d", d=HD), AX.X, ALU.add))
            need(a)
            V.tensor_scalar(t("nk"), t("nk"), 1.0e-28, None, ALU.max).then_inc(nk_done, 1)
            dve.wait_ge(exp_g, 2)
            V.tensor_scalar(uu[:, :, :], ee[:, :, :], 1.0, None, ALU.add).then_inc(u_done, 1)
            dve.wait_ge(u_done, 1)
            a = run(V.scalar_tensor_tensor(corr[:, :, :], uu[:, :, :], -1.0, ee[:, :, :], ALU.add, ALU.subtract))
            need(a)
            a = run(V.scalar_tensor_tensor(corr[:, :, :], g_ch[:, 0:5:4, :], 0.0, corr[:, :, :], ALU.max, ALU.subtract))
            need(a)
            dve.wait_ge(ln_g, 1)
            a = tt(sp[:, :, :], lnu[:, :, :], corr[:, :, :], ALU.add)
            need(a)
            a = run(V.tensor_scalar(t("dt"), sp[:, 1, :], elds[:, 0:1], 1.0e-4, ALU.mult, ALU.add))
            need(a)
            dve.wait_ge(sig_g, 3)
            run(V.scalar_tensor_tensor(t("ah"), t("dt"), 0.5, sp[:, 0, :], ALU.mult, ALU.mult))
            a = run(V.scalar_tensor_tensor(t("ww"), sig_om[:, :], col("freq"), t("dt"), ALU.mult, ALU.mult))
            need(a)
            tt(t("s2"), t("ah"), t("ah"), ALU.mult)
            a = tt(t("w2"), t("ww"), t("ww"), ALU.mult)
            need(a)
            a = tt(t("t1"), t("s2"), t("w2"), ALU.add)
            need(a)
            run(V.tensor_scalar(t("p1"), t("t1"), 1.0, None, ALU.add))
            a = run(V.tensor_scalar(t("n1"), t("t1"), -1.0, 1.0, ALU.mult, ALU.add))
            need(a)
            run(V.scalar_tensor_tensor(t("den"), t("ah"), 2.0, t("p1"), ALU.mult, ALU.add))
            run(V.scalar_tensor_tensor(t("num"), t("ah"), -2.0, t("p1"), ALU.mult, ALU.add))
            a = tt(t("n1s"), t("n1"), t("n1"), ALU.mult)
            need(a)
            a = run(V.reciprocal(t("rdn"), t("den")))
            b_ = run(V.scalar_tensor_tensor(t("t2"), t("w2"), 4.0, t("n1s"), ALU.mult, ALU.add))
            need(a)
            a = tt(t("t3"), t("num"), t("rdn"), ALU.mult)
            need(b_)
            b_ = run(V.tensor_scalar(t("flag"), t("t2"), 0.0, None, ALU.is_equal))
            need(a)
            V.tensor_scalar(t("ratio"), t("t3"), 1.0e-16, 1.0, ALU.max, ALU.min).then_inc(ratio_done, 1)
            need(b_)
            V.tensor_tensor(t("nsq"), t("t2"), t("flag"), ALU.add).then_inc(nsq_done, 1)
            a = tt(t("t4"), t("n1"), t("flag"), ALU.add)
            dve.wait_ge(ln_g, 2)
            V.scalar_tensor_tensor(t("ell"), t("lr"), 4.0, sig_br[:, 1, :], ALU.mult, ALU.mult).then_inc(ell_done, 1)
            dve.wait_ge(mm_g, 1)
            dve.wait_ge(nsq_done, 1)
            a = tt(t("t5"), t("yy"), t("yy"), ALU.mult)
            need(a)
            a = tt(t("t6"), t("t5"), t("nsq"), ALU.mult)
            need(a)
            a = run(V.tensor_scalar(t("t7"), t("t6"), -0.5, 1.5, ALU.mult, ALU.add))
            need(a)
            a = tt(t("t8"), t("yy"), t("t7"), ALU.mult)
            need(a)
            tt(ph[0][:, 0, :], t("t4"), t("t8"), ALU.mult)
            a = run(V.scalar_tensor_tensor(ph[0][:, 1, :], t("ww"), 2.0, t("t8"), ALU.mult, ALU.mult))
            off = 1
            cur = 0
            while off < S:
                need(count[0])
                X, Y, n_ = ph[cur], ph[1 - cur], S - off
                run(V.tensor_tensor(pa[:, :, 0:n_], X[:, :, off:S], X[:, 0:1, 0:n_].to_broadcast([P, 2, n_]), ALU.mult))
                run(V.tensor_tensor(pbb[:, :, 0:n_], X[:, :, off:S], X[:, 1:2, 0:n_].to_broadcast([P, 2, n_]), ALU.mult))
                a = run(V.tensor_copy(Y[:, :, 0:off], X[:, :, 0:off]))
                need(a)
                run(V.tensor_tensor(Y[:, 0, off:S], pa[:, 0, 0:n_], pbb[:, 1, 0:n_], ALU.subtract))
                run(V.tensor_tensor(Y[:, 1, off:S], pa[:, 1, 0:n_], pbb[:, 0, 0:n_], ALU.add))
                off *= 2
                cur = 1 - cur
            cosp, sinp = ph[cur][:, 0, :], ph[cur][:, 1, :]
            dve.wait_ge(mm_g, 3)
            a = run(V.tensor_scalar(t("t1"), t("m2"), -1.0, 1.0, ALU.mult, ALU.add))
            need(a)
            V.tensor_scalar(t("c1"), t("t1"), 0.0, 1.0e-6, ALU.max, ALU.add).then_inc(c1_done, 1)
            dve.wait_ge(knorm_done, 1)
            a = run(V.tensor_scalar(t("t2"), t("nrm"), 1.0e-6, None, ALU.add))
            need(a)
            a = run(V.reciprocal(t("rk"), t("t2")))
            need(a)
            a = tt(t("brk"), sig_br[:, 0, :], t("rk"), ALU.mult)
            dve.wait_ge(v_loaded, 64)
            run(V.tensor_tensor(t("vr1"), v_own[:, :], cosp, ALU.mult))
            a = run(V.scalar_tensor_tensor(t("vr2"), v_swap[:, :], col("sgn"), sinp, ALU.mult, ALU.mult))
            need(a)
            run(V.scalar_tensor_tensor(t("t3"), t("brk"), -1.0, t("mm"), ALU.mult, ALU.mult))
            a = tt(t("vr3"), t("vr1"), t("vr2"), ALU.add)
            dve.wait_ge(mm_g, 4)
            b_ = tt(t("vp"), sig_bc[:, 0, :], t("rt"), ALU.mult)
            need(b_)
            tt(t("ct"), t("t3"), t("rk"), ALU.mult)
            a = tt(t("t4"), t("vr3"), t("vp"), ALU.mult)
            need(a)
            a = tt(t("wt"), t("t4"), t("brk"), ALU.mult)
            need(a)
            mc = t("mm").rearrange("p (c j) -> p c j", j=C)
            ctc = t("ct").rearrange("p (c j) -> p c j", j=C)
            run(V.tensor_tensor(m_pair, mc[:, :, 0:3], mc[:, :, 1:4], ALU.mult))
            run(V.tensor_copy(kap_c[:, HD, :, :], t("wt").rearrange("p (c j) -> p c j", j=C)))
            run(V.tensor_copy(bcoef[:, :, 0:1], ctc[:, :, 0:1]))
            run(V.tensor_tensor(bcoef[:, :, 1:2], ctc[:, :, 1:2], mc[:, :, 0:1], ALU.mult))
            run(V.tensor_tensor(dv[:, 0, :, :], gv[:, 0, :, :], ctc[:, :, 1:4], ALU.mult))
            run(V.tensor_tensor(dv[:, 1, :, 0:2], gv[:, 1, :, 0:2], ctc[:, :, 2:4], ALU.mult))
            run(V.tensor_tensor(dv[:, 1, :, 2:3], gv[:, 1, :, 2:3], ctc[:, :, 3:4], ALU.mult))
            run(V.tensor_copy(m_scan, t("mm")))
            need(count[0])
            run(V.tensor_tensor(m_three, m_pair[:, :, 0:2], mc[:, :, 2:4], ALU.mult))
            run(V.tensor_tensor(coef_c[:, :, 0:1], m_pair[:, :, 0:1], m_pair[:, :, 2:3], ALU.mult))
            run(V.tensor_tensor(bcoef[:, :, 2:3], ctc[:, :, 2:3], m_pair[:, :, 0:1], ALU.mult))
            run(V.tensor_tensor(dv[:, 0, :, 1:2], dv[:, 0, :, 1:2], mc[:, :, 1:2], ALU.mult))
            run(V.tensor_tensor(dv[:, 0, :, 2:3], dv[:, 0, :, 2:3], m_pair[:, :, 1:2], ALU.mult))
            run(V.tensor_tensor(dv[:, 1, :, 1:2], dv[:, 1, :, 1:2], mc[:, :, 2:3], ALU.mult))
            V.memset(m_scan[:, 0:1], 0.0).then_inc(m_scan_done, 1)
            need(count[0])
            a = run(V.tensor_tensor(bcoef[:, :, 3:4], ctc[:, :, 3:4], m_three[:, :, 0:1], ALU.mult))
            dve.wait_ge(bank_set, 3)
            for j, fade_to_end in enumerate((m_three[:, :, 1:2], m_pair[:, :, 2:3], mc[:, :, 3:4])):
                run(V.tensor_tensor(bank_c[:, 0:HD, 0:NC, 1 + j], kc[:, :, :, j],
                                    fade_to_end.rearrange("p c o -> p o c").to_broadcast([P, HD, NC]), ALU.mult))
            need(a)
            wide = lambda v, rows, n: v.rearrange("p c j -> p (c j)").rearrange("p (o x) -> p o x", o=1)\
                .to_broadcast([P, rows, NC * n])
            a = run(V.tensor_tensor(kap_t[:, 0:HD, :], by_t(k_ch), wide(bcoef, HD, C), ALU.mult))
            need(a)
            for i in range(C - 1):
                n = C - 1 - i
                src = kap_c[:, :, :, i:i + 1].to_broadcast([P, HD + 1, NC, n])
                dst = kap_c[:, :, :, i + 1:C]
                weight = dv[:, min(i, 1), :, 0:n] if i < 2 else dv[:, 1, :, 2:3]
                tmp = pair_tmp[:, 0:(HD + 1) * NC * n].rearrange("p (d c j) -> p d c j", d=HD + 1, j=n)
                for j in range(n):
                    run(V.tensor_tensor(tmp[:, :, :, j], kap_c[:, :, :, i],
                                        weight[:, :, j:j + 1].rearrange("p c o -> p o c").to_broadcast([P, HD + 1, NC]),
                                        ALU.mult))
                need(count[0])
                run(V.tensor_tensor(dst, dst, tmp, ALU.add))
                need(count[0])
            for c in range(NC):
                need(count[0])
                for j in range(C):
                    run(V.tensor_tensor_reduce(dot_junk[:, j, :], bank[:, :, SLOT * c], kap_t[:, :, C * c + j], 1.0, 0.0,
                                               ALU.mult, ALU.add, coef[:, SLOT * c + 1 + j:SLOT * c + 2 + j]))
                need(count[0])
                run(V.tensor_tensor(terms[:, :, :], bank[:, 0:HD, SLOT * c:SLOT * (c + 1)],
                                    coef[:, SLOT * c:SLOT * (c + 1)].rearrange("p (o j) -> p o j", o=1)
                                    .to_broadcast([P, HD, SLOT]), ALU.mult))
                need(count[0])
                run(V.tensor_reduce(bank[:, 0:HD, SLOT * (c + 1)], terms[:, :, :], AX.X, ALU.add))
            need(count[0])
            for j in range(C):
                run(V.tensor_tensor(chunked(uk, C)[:, :, :, j], kc[:, :, :, j],
                                    coef_c[:, :, 1 + j:2 + j].rearrange("p c o -> p o c").to_broadcast([P, HD, NC]),
                                    ALU.mult))
            need(count[0])
            dve.wait_ge(m_spread, 1)
            run(V.tensor_tensor_scan(y_ch, m_full, uk, 0.0, ALU.mult, ALU.add))
            dve.wait_ge(qsq_done, 1)
            a = run(V.tensor_reduce(t("nq"), sq.rearrange("p (d t) -> p t d", d=HD), AX.X, ALU.add))
            need(a)
            V.tensor_scalar(t("nq"), t("nq"), 1.0e-28, None, ALU.max).then_inc(nq_done, 1)
            need(count[0])
            a = run(V.tensor_tensor(prod, y_ch, q_ch, ALU.mult))
            need(a)
            a = run(V.tensor_reduce(t("rr"), prod.rearrange("p (d t) -> p t d", d=HD), AX.X, ALU.add))
            dve.wait_ge(qnorm_done, 1)
            a = run(V.tensor_scalar(t("t5"), t("nrq"), 1.0e-6, None, ALU.add))
            need(a)
            a = run(V.reciprocal(t("rq"), t("t5")))
            need(a)
            a = tt(t("gq"), t("rq"), sig_bc[:, 1, :], ALU.mult)
            need(a)
            a = tt(t("r2"), t("rr"), t("gq"), ALU.mult)
            need(a)
            V.tensor_tensor(t("cc"), t("r2"), cosp, ALU.mult).then_inc(parts_done, 1)
            V.tensor_tensor(t("dd"), t("r2"), sinp, ALU.mult).then_inc(parts_done, 1)
            for i in range(2):
                dve.wait_ge(y_done, i + 1)
                for b in range(NB):
                    a = run(V.bn_stats(gst[:, NB * i + b, :], SB[0][:, i, S * b:S * (b + 1)]))
            need(a)
            for j in range(8):
                V.bn_aggr(gmv[:, j, :], gst[:, j, :]).then_inc(gst_done, 1)
            dve.wait_ge(gm_done, 1)
            a = run(V.tensor_copy(gmean[:, :], MI[:, 0:8]))
            need(a)
            a = run(V.tensor_tensor(gdm[:, :], gmv[:, :, 0], gmean[:, :], ALU.subtract))
            need(a)
            a = run(V.tensor_tensor(gdm[:, :], gdm[:, :], gdm[:, :], ALU.mult))
            need(a)
            V.tensor_tensor(gdv[:, :], gdm[:, :], gmv[:, :, 1], ALU.add).then_inc(gdv_done, 1)
            dve.wait_ge(grs_done, 1)
            for i in range(2):
                a = run(V.tensor_scalar(gsc[:, NB * i:NB * (i + 1)], grs[:, NB * i:NB * (i + 1)], col(f"gn_w{i}"), None, ALU.mult))
            need(a)
            a = run(V.tensor_tensor(gdm[:, :], gmean[:, :], gsc[:, :], ALU.mult))
            need(a)
            for i in range(2):
                V.tensor_scalar(gbi[:, NB * i:NB * (i + 1)], gdm[:, NB * i:NB * (i + 1)], -1.0, col(f"gn_b{i}"),
                                ALU.mult, ALU.add).then_inc(gbi_done, 1)
            for i in range(2):
                dve.wait_ge(yn_done, NB * (i + 1))
                a = run(V.tensor_tensor(yn[:, i, :], yn[:, i, :], zs[:, i, :], ALU.mult))
                need(a)
                V.scalar_tensor_tensor(y2[:, i, :], xc[:, i, :], col(f"d{i}"), yn[:, i, :], ALU.mult, ALU.add)\
                    .then_inc(y2_done, 1)
            dve.wait_ge(o2_done, 1)
            dve.wait_ge(x1h_done, 1)
            V.tensor_tensor(x2[:, :, :], SB[1][:, 0, :].rearrange("p (b d) -> p b d", b=NB), x1h[:, :, :], ALU.add)\
                .then_inc(x2_done, 1)
            dve.wait_ge(x2_done, 1)
            x_src = x2
            moments(3)
            a = run(V.tensor_tensor(res[:, :, :], x2[:, :, :],
                                    rows_sb[:, 2:3, :].to_broadcast([P, NB, DM]), ALU.add))
            dve.wait_ge(ln_rstd, 3)
            need(count[0])
            for b in range(NB):
                V.tensor_scalar(xn[:, b, :], x2[:, b, :], mv[:, b, 0:1], rstd[:, b:b + 1], ALU.subtract, ALU.mult)\
                    .then_inc(xn_ready, 1)
            dve.wait_ge(ffn_done, 1)
            V.tensor_tensor(res[:, :, :], res[:, :, :], SA[0][:, :].rearrange("p (b d) -> p b d", b=NB), ALU.add)\
                .then_inc(res_done, 1)

        @block.tensor
        def _(pe):
            def k_project(b):
                pe.wait_ge(s_ctx[min(b, 1)], 16)
                nc.tensor.matmul(SB[b // 2][:, b % 2, :], wk_sb[:, :], ctx_sb[:, b, :], start=True, stop=True)\
                    .then_inc(k_done, 1)

            def v_project(b, dst):
                for t in range(KT):
                    last = nc.tensor.matmul(dst[:, P * t:P * (t + 1)], ctx_sb[:, b, P * t:P * (t + 1)], wv_sb[:, :],
                                            start=True, stop=True)
                last.then_inc(v_done, 1)

            pe.wait_ge(s_wk, 16)
            k_project(0)
            k_project(1)
            pe.wait_ge(s_id, 16)
            for b in range(NB):
                pe.wait_ge(xn_ready, b + 1)
                last = nc.tensor.transpose(MI[:, P * b:P * (b + 1)], xn[:, b, :], id_sb[:, :])
            last.then_inc(xnT_done, 1)
            pe.wait_ge(s_wq, 16)
            pe.wait_ge(xnT_copied, 1)
            nc.tensor.matmul(SA[0][:, :], wq_sb[:, :], xn_t[:, :], start=True, stop=True).then_inc(q_done, 1)
            k_project(2)
            k_project(3)
            pe.wait_ge(s_wv, 16)
            for b in range(NB):
                pe.wait_ge(k_copied, 2 * b + 2)
                v_project(b, SB[b // 2][:, b % 2, :])

            def score(n):
                b, h = divmod(n, H)
                if h == 0:
                    pe.wait_ge(k_stacked[b], 16 * NTERM)
                if n == 0:
                    pe.wait_ge(q_stacked, 16 * (NTERM // 2))
                    pe.wait_ge(q_stacked_lo, 16 * (NTERM // 2))
                if n >= 2:
                    pe.wait_ge(max_done, n - 1)
                nc.tensor.matmul(SA[n % 2][:, :], q_stack[:, h, S * b:S * (b + 1)], k_stack[b][:, h, :],
                                 start=True, stop=True).then_inc(score_done, 1)

            def turn_max(b):
                pe.wait_ge(mneg_done, b + 1)
                if b >= 2:
                    pe.wait_ge(x1_done, b - 1)
                if b == 0:
                    pe.wait_ge(xnT_copied, 1)
                nc.tensor.transpose(MI[0:3 * H, 0:S // 2].bitcast(BF16), m_split[:, b, :], id_bf[:, :]).then_inc(mT_done, 1)

            def unit(n, todo):
                b, u = divmod(n, 8)
                t, half = divmod(u, 2)
                if n < 8 * NB:
                    if n < 2:
                        pe.wait_ge(v_copied, 2 * n + 2)
                    if u == 0:
                        pe.wait_ge(m_stacked, 16 * b + 16)
                        pe.wait_ge(mask_ready, b + 1)
                        pe.wait_ge(consts_ready, 4)
                    if n >= 2:
                        pe.wait_ge(unit_exp, n - 1)
                    for g in range(2):
                        for j in range(4):
                            h = 8 * half + 4 * g + j
                            nc.tensor.matmul(SB[n % 2][:, g, S * j:S * (j + 1)], k_stack[b][:, h, P * t:P * (t + 1)],
                                             q_stack[:, h, S * b:S * (b + 1)], start=(j == 0), stop=False,
                                             skip_group_check=True)
                        last = nc.tensor.matmul(SB[n % 2][:, g, :], mask_bf[:, b, P * t:P * (t + 1)],
                                                neg_id4[:, :, :].rearrange("p a s -> p (a s)"), start=False, stop=True,
                                                skip_group_check=True)
                        if g == 0 and todo:
                            score(todo[0])
                    last.then_inc(unit_scored, 1)
                if todo:
                    score(todo[1])
                if n >= 1:
                    b, u = divmod(n - 1, 8)
                    t, half = divmod(u, 2)
                    pe.wait_ge(unit_exp, n)
                    if u == 0:
                        if b == 0:
                            pe.wait_ge(ot_zeroed, 1)
                        else:
                            pe.wait_ge(o_copied, b)
                    for i in range(8):
                        h = 8 * half + i
                        g, j = divmod(h, 4)
                        last = nc.tensor.matmul(OT[32 * j:32 * j + DH + 1, S * g:S * (g + 1)], v_ones[:, b, t, h, :],
                                                probs[:, (n - 1) % 3, i, :], start=(t == 0 and g == 0),
                                                stop=(t == KT - 1), skip_group_check=True)
                        if i == 3 and todo:
                            score(todo[2])
                    last.then_inc(unit_pv, 1)
                elif todo:
                    score(todo[2])
                if todo:
                    score(todo[3])

            def turn_out(b):
                pe.wait_ge(o_copied, b + 1)
                if b >= 1:
                    pe.wait_ge(x1_done, b)
                pe.wait_ge(mT_copied, b + 1)
                for g in range(4):
                    last = nc.tensor.transpose(MI[:, S * g:S * (g + 1)], o_sb[:, b % 2, S * g:S * (g + 1)], id_sb[:, :])
                last.then_inc(oT_done, 1)

            def turn_attn(b):
                pe.wait_ge(attn_done, b + 1)
                nc.tensor.transpose(MI[:, 0:S], attn[:, b % 2, :], id_sb[:, :]).then_inc(aT_done, 1)

            def project_out(b):
                pe.wait_ge(aT_copied, b + 1)
                pe.wait_ge(s_wo, 16)
                nc.tensor.matmul(MI[:, 0:DM], attn_t[:, b % 2, :], wo_sb[:, :], start=True, stop=True).then_inc(wo_done, 1)

            MM = nc.tensor.matmul
            for h in range(12):
                score(h)
            pe.wait_ge(open_done, 1)
            MM(MI[0:1, 0:1], some_open[:, :], col("one"), start=True, stop=True).then_inc(count_done, 1)
            for h in range(12, H):
                score(h)
            pe.wait_ge(flag_done, 1)
            turn_max(0)

            def general_block(n):
                pe.wait_ge(g_ctx, 16 * n + 16)
                MM(SB[0][:, 0, :], wk_sb[:, :], ctx_sb[:, 0, :], start=True, stop=True).then_inc(g_kproj, 1)
                for t in range(KT):
                    last = MM(MI[:, P * t:P * (t + 1)], ctx_sb[:, 0, P * t:P * (t + 1)], wv_sb[:, :], start=True, stop=True)
                last.then_inc(g_vproj, 1)
                pe.wait_ge(g_kstacked, n * (16 * NTERM) + 16 * NTERM)
                for h in range(H):
                    if h >= 2:
                        pe.wait_ge(max_done, n * H + (H + h - 1))
                    MM(SA[h % 2][:, :], q_raw[:, h, :], k_stack[0][:, h, :], start=True, stop=True).then_inc(score_done, 1)
                pe.wait_ge(mneg_done, n + 2)
                pe.wait_ge(g_vcopied, n + 1)
                MM(MI[0:3 * H, 0:S], m_split[:, 0, :], id_bf[:, :], start=True, stop=True).then_inc(mT_done, 1)
                pe.wait_ge(m_stacked, 16 * n + 16)
                pe.wait_ge(g_maskset, n + 1)

                def values(u):
                    t, half = divmod(u, 2)
                    pe.wait_ge(unit_exp, n * UNITS + u + 1)
                    for i in range(8):
                        g, j = divmod(8 * half + i, 4)
                        last = MM(OT[32 * j:32 * j + DH + 1, S * g:S * (g + 1)], v_ones[:, 0, t, 8 * half + i, :],
                                  probs[:, u % 2, i, :], start=(t == 0 and g == 0), stop=(t == KT - 1),
                                  skip_group_check=True)
                    last.then_inc(unit_pv, 1)

                for u in range(UNITS):
                    t, half = divmod(u, 2)
                    if u >= 2:
                        pe.wait_ge(unit_exp, n * UNITS + u - 1)
                    for g in range(2):
                        for j in range(4):
                            h = 8 * half + 4 * g + j
                            MM(SB[u % 2][:, g, S * j:S * (j + 1)], k_stack[0][:, h, P * t:P * (t + 1)], q_cur[:, h, :],
                               start=(j == 0), stop=False, skip_group_check=True)
                        last = MM(SB[u % 2][:, g, :], mask_bf[:, 0, P * t:P * (t + 1)],
                                  neg_id4[:, :, :].rearrange("p a s -> p (a s)"), start=False, stop=True,
                                  skip_group_check=True)
                    last.then_inc(unit_scored, 1)
                    if u >= 1:
                        values(u - 1)
                values(UNITS - 1)
                pe.wait_ge(o_copied, n + 1)
                for g in range(4):
                    last = nc.tensor.transpose(MI[:, S * g:S * (g + 1)], o_sb[:, 0, S * g:S * (g + 1)], id_sb[:, :])
                last.then_inc(oT_done, 1)

            pe.wait_ge(flag_done, 1)
            with pe.If(pe.value_load(go_general[0:1, 0:1]) != 0):
                pe.wait_ge(v_copied, NB)
                pe.wait_ge(mT_copied, 1)
                pe.wait_ge(max_done, H)
                pe.wait_ge(ot_zeroed, 1)
                pe.wait_ge(consts_ready, 4)
                pe.wait_ge(s_wo, 16)
                with pe.Fori(0, NB) as b:
                    with pe.Fori(0, NBLK) as k:
                        pe.wait_ge(g_q, 4 * b + 4)
                        general_block(b * NBLK + k)
                    pe.wait_ge(attn_done, 2 * b + 2)
                    nc.tensor.transpose(MI[:, 0:S], attn[:, 0, :], id_sb[:, :]).then_inc(aT_done, 1)
                    pe.wait_ge(aT_copied, b + 1)
                    MM(MI[:, 0:DM], attn_t[:, 0, :], wo_sb[:, :], start=True, stop=True).then_inc(wo_done, 1)
            with pe.Else():
                for b in range(NB):
                    for u in range(8):
                        n = 8 * b + u
                        unit(n, [H * (b + 1) + 4 * u + i for i in range(4)] if b + 1 < NB and u < 4 else [])
                        if b >= 1:
                            if u == 0:
                                turn_out(b - 1)
                            if u == 2:
                                turn_attn(b - 1)
                            if u == 3:
                                project_out(b - 1)
                        if b + 1 < NB and u == 4:
                            turn_max(b + 1)
                unit(8 * NB, [])
                turn_out(NB - 1)
                turn_attn(NB - 1)
                project_out(NB - 1)

            pe.nop()
            pe.wait_ge(x1_done, NB)
            for b in range(NB):
                pe.wait_ge(xn_ready, NB + b + 1)
                last = nc.tensor.transpose(MI[:, S * b:S * (b + 1)], xr[:, b, :], id_sb[:, :])
            last.then_inc(xnT_done, 1)
            pe.wait_ge(s_late, 160)
            pe.wait_ge(xnT_copied, 2)
            for i in range(2):
                MM(SB[0][:, i, :], w_in_sb[:, DI + P * i:DI + P * (i + 1)], xr_t[:, :], start=True, stop=True).then_inc(xg_done, 1)
            for i in range(2):
                MM(SB[1][:, i, :], w_in_sb[:, 2 * DI + P * i:2 * DI + P * (i + 1)], xr_t[:, :], start=True, stop=True)\
                    .then_inc(kp_done, 1)
            MM(SA[0][0:2 * H, :], w_in_sb[:, 3 * DI:3 * DI + 2 * H], xr_t[:, :], start=True, stop=True).then_inc(vp_done, 1)
            MM(SA[1][:, :], w_in_sb[:, 0:P], xr_t[:, :], start=True, stop=True).then_inc(z_done, 1)
            MM(OT[:, :], w_in_sb[:, P:2 * P], xr_t[:, :], start=True, stop=True).then_inc(z_done, 1)
            for i in range(2):
                pe.wait_ge(xc_done, i + 1)
                last = MM(MI[0:7 * H, :], w_gate_sb[:, i, :], xc[:, i, :], start=(i == 0), stop=(i == 1))
            last.then_inc(gate_done, 1)
            pe.wait_ge(xg_copied, 2)
            for o in range(2):
                for i in range(2):
                    last = MM(SB[0][:, o, :], w_q_sb[:, i, P * o:P * (o + 1)], xc[:, i, :], start=(i == 0), stop=(i == 1))
                last.then_inc(qp_done, 1)
            pe.wait_ge(kp_copied, 2)
            MM(SB[1][:, 1, 0:DM], fat_sb[:, :], fb_sb[:, :], start=True, stop=True).then_inc(ab_mm_done, 1)
            pe.wait_ge(parts_done, 2)
            pe.wait_ge(wrs_done, 1)
            pe.wait_ge(qp_copied, 2)
            for i in range(2):
                for b in range(NB):
                    MM(SB[0][:, i, S * b:S * (b + 1)], w_rd[:, b, P * i:P * (i + 1)], T["cc"][:, :], start=True, stop=False)
                    last = MM(SB[0][:, i, S * b:S * (b + 1)], w_rs[:, b, P * i:P * (i + 1)], T["dd"][:, :], start=False, stop=True)
                last.then_inc(y_done, 1)
            pe.wait_ge(gst_done, 8)
            pe.wait_ge(gate_copied, 1)
            MM(MI[:, 0:8], avg_sb[:, :], gmv[:, :, 0], start=True, stop=True).then_inc(gm_done, 1)
            pe.wait_ge(gdv_done, 1)
            MM(MI[:, 8:16], avg_sb[:, :], gdv[:, :], start=True, stop=True).then_inc(gv_done, 1)
            pe.wait_ge(y2_done, 2)
            for b in range(NB):
                for i in range(2):
                    last = MM(SB[1][:, 0, S * b:S * (b + 1)], y2[:, i, S * b:S * (b + 1)], w_out_sb[:, i, :], start=(i == 0),
                              stop=(i == 1))
            last.then_inc(o2_done, 1)
            for b in range(NB):
                pe.wait_ge(xn_ready, 2 * NB + b + 1)
                last = nc.tensor.transpose(MI[:, S * b:S * (b + 1)], xn[:, b, :], id_sb[:, :])
            last.then_inc(xnT_done, 1)
            pe.wait_ge(xnT_copied, 3)
            for b in range(NB):
                last = MM(SA[0][:, S * b:S * (b + 1)], xn_t[:, S * b:S * (b + 1)], w_eff[:, :], start=True, stop=True)
            last.then_inc(ffn_done, 1)


INPUTS = ["x", "ctx_t", "mask", "wq", "wk", "wv", "wo", "vec", "rows", "ident", "avg", "w_in", "w_gate", "w_q",
          "w_read", "w_out", "ffn_w", "ffn_at", "ffn_b"]


def kernel(**inputs):
    import numpy as np
    import concourse.bacc as bacc
    from concourse.bass_utils import run_bass_kernel_spmd

    a = {k: np.asarray(v) for k, v in inputs.items()}
    f32 = np.float32

    cols = {n: np.zeros((P, 1), f32) for n in VEC}

    def put(name, v):
        cols[name][:v.shape[0], 0] = v

    by_dim = lambda w: w.reshape(H, DH, DM).transpose(1, 0, 2).reshape(DM, DM)
    put("bq", a["L0_xattn_bq"].reshape(H, DH).T.reshape(-1))
    put("bk", a["L0_xattn_bk"].reshape(H, DH).T.reshape(-1))
    put("rms", a["L0_attn_rms_w"])
    b_in = a["L0_attn_in_proj_b"]
    for i in range(2):
        put(f"z_b{i}", b_in[P * i:P * (i + 1)])
        put(f"xg_b{i}", b_in[DI + P * i:DI + P * (i + 1)])
        put(f"k_b{i}", b_in[2 * DI + P * i:2 * DI + P * (i + 1)])
        put(f"cb{i}", a["L0_attn_conv_b"][P * i:P * (i + 1)])
        put(f"gn_w{i}", a["L0_attn_gn_w"][P * i:P * (i + 1)])
        put(f"gn_b{i}", a["L0_attn_gn_b"][P * i:P * (i + 1)])
        put(f"d{i}", a["L0_attn_D_param"][P * i:P * (i + 1)])
        for j in range(4):
            put(f"cw{i}{j}", a["L0_attn_conv_w"][P * i:P * (i + 1), j])
    put("v_b", b_in[3 * DI:])
    put("gate_b", a["L0_attn_gate_b"].reshape(7, H).T.reshape(-1))
    put("log_dt", np.tile(a["L0_attn_log_dt_scale"], 8))
    put("freq", np.tile((f32(1.0) / f32(10000.0) ** (np.arange(H, dtype=f32) / f32(H))).astype(f32), 8))
    put("sgn", np.repeat(np.array([-1.0, 1.0], f32), 64))
    put("eps_ln", np.full(P, EPS_LN, f32))
    put("eps_rms", np.full(P, EPS_RMS, f32))
    put("one", np.ones(P, f32))
    put("root_shift", np.full(P, -15 * LN2, f32))
    rows = np.stack([a["L0_xattn_bv"], a["L0_xattn_bo"], a["L0_ffn_bias"]])
    rd = a["L0_attn_readout_w"].reshape(H, 2, DI)
    w_read = np.zeros((2, 2, NB, H, NB, DI), f32)
    for s in range(2):
        for b in range(NB):
            w_read[0, s, b, :, b, :] = rd[:, s]
            w_read[1, s, b, :, b, :] = rd[:, 1 - s]
    arrays = {
        "x": a["x"],
        "ctx_t": a["ctx_1024"].transpose(0, 2, 1),
        "mask": a["mask_BxSxS2_bk1"],
        "wq": by_dim(a["L0_xattn_Wq"]).T, "wk": by_dim(a["L0_xattn_Wk"]).T,
        "wv": a["L0_xattn_Wv"].T, "wo": a["L0_xattn_Wo"].T,
        "vec": np.concatenate([cols[n] for n in VEC], axis=1),
        "rows": np.broadcast_to(rows[None], (P, 3, DM)),
        "ident": np.eye(P, dtype=f32),
        "avg": np.kron(np.eye(P // GN, dtype=f32), np.full((GN, GN), 1.0 / GN, f32)),
        "w_in": a["L0_attn_in_proj_w"],
        "w_gate": a["L0_attn_gate_w"].reshape(2, P, 7, H).transpose(1, 0, 3, 2).reshape(P, 2, 7 * H),
        "w_q": a["L0_attn_Q_w"].reshape(2, P, DI).transpose(1, 0, 2),
        "w_read": w_read.reshape(2, P, NB, DI),
        "w_out": a["L0_attn_out_w"].reshape(2, P, DM).transpose(1, 0, 2),
        "ffn_w": a["L0_ffn_kernel"], "ffn_at": a["L0_ffn_a"].T, "ffn_b": a["L0_ffn_b"],
    }
    arrays = {k: np.ascontiguousarray(arrays[k]) for k in INPUTS}
    nc = bacc.Bacc("TRN2", target_bir_lowering=False, num_devices=1)
    aps = [nc.dram_tensor(f"in_{k}", v.shape, mybir.dt.from_np(v.dtype), kind="ExternalInput").ap()
           for k, v in arrays.items()]
    out = nc.dram_tensor("out", (NB, S, DM), F32, kind="ExternalOutput").ap()
    perceiver_kernel(nc, *aps, out)
    r = run_bass_kernel_spmd(nc, [{f"in_{k}": v for k, v in arrays.items()}], core_ids=[0])
    return r.results[0]["out"]
```

```python
from contextlib import ExitStack

import concourse.bass as bass
from concourse import mybir

ALU = mybir.AluOpType
ACT = mybir.ActivationFunctionType
F32 = mybir.dt.float32
BF16 = mybir.dt.bfloat16
U8 = mybir.dt.uint8
U16 = mybir.dt.uint16
I32 = mybir.dt.int32
AX = mybir.AxisListType

P = 128
NB = 4
S = 128
DM = 128
NK = 2048
H = 16
DH = DM // H
BLK = 512
KT = BLK // P
TOK = NB * S
DI = 256
LATE_LOADS = 11
HD = DI // H
C = 4
NC = S // C
NPAIR = C * (C - 1) // 2
BIG = 1.0e30
SCALE = float(DH) ** -0.5
EPS_LN = 1e-5
EPS_RMS = 1e-6
GN = 16
ROUND = 1.5 * 2.0 ** 23
LN2 = 0.6931471805599453
ONES_PAIR = 1.0 + 0x3F80 / 2.0 ** 23

NBLK = NK // BLK
UNITS = 2 * KT
ALL_MASKED = NB * (NK - BLK) // 2 * 0x0101
K_LEVEL = [0, 1, 2, 0, 1, 0]
Q_LEVEL = [0, 0, 0, 1, 1, 2]
NTERM = len(K_LEVEL)
MROW = NTERM * DH

VEC = {n: i for i, n in enumerate(
    ["bq", "bk", "rms", "xg_b0", "xg_b1", "k_b0", "k_b1", "z_b0", "z_b1", "v_b"]
    + [f"cw{i}{j}" for i in range(2) for j in range(4)]
    + ["cb0", "cb1", "gn_w0", "gn_w1", "gn_b0", "gn_b1", "d0", "d1", "gate_b", "log_dt", "freq", "sgn",
       "eps_ln", "eps_both", "root_back", "norm_floor", "one"])}
NVEC = len(VEC)


def perceiver_kernel(nc, x, ctx_t, mask, wq, wk, wv, wo, vec, rows, ident, avg, heads, w_in, w_gate, w_q, w_read,
                     w_out, ffn_w, ffn_at, ffn_b, out):
    ctx = ExitStack()
    with ctx:
        def sb(name, shape, dt=F32):
            return ctx.enter_context(nc.sbuf_tensor(name, shape, dt))

        def pb(name, shape, dt=F32):
            return ctx.enter_context(nc.psum_tensor(name, shape, dt))

        def sem(name):
            return ctx.enter_context(nc.semaphore(name))

        scratch = nc.dram_tensor("scratch", [2 * DI + 2 * H + 9 * H, TOK], F32, kind="Internal").ap()
        ROW_K, ROW_Q, ROW_V, ROW_G = 0, DI, 2 * DI, 2 * DI + 2 * H
        ROW_N = ROW_G + 7 * H

        x_sb = sb("x_sb", [P, NB, DM])
        ctx_sb = sb("ctx_sb", [P, NB, BLK])
        mask_sb = sb("mask_sb", [P, NB, NK], U8)
        mask_bf = sb("mask_bf", [P, NB, BLK], BF16)
        mask_neg = sb("mask_neg", [P, NB, BLK])
        vec_sb = sb("vec_sb", [P, NVEC])
        rows_sb = sb("rows_sb", [P, 3, DM])
        id_sb = sb("id_sb", [P, P])
        id_bf = sb("id_bf", [P, P], BF16)
        neg_id4 = sb("neg_id4", [P, 4, P], BF16)
        avg_sb = sb("avg_sb", [P, P])
        heads_sb = sb("heads_sb", [P, 2, H])
        wq_sb, wk_sb, wv_sb, wo_sb = (sb(n, [P, DM]) for n in ("wq_sb", "wk_sb", "wv_sb", "wo_sb"))
        w_in_sb = sb("w_in_sb", [P, 3 * DI + 2 * H])
        w_gate_sb = sb("w_gate_sb", [P, 2, 7 * H])
        w_q_sb = sb("w_q_sb", [P, 2, DI])
        w_rd = sb("w_rd", [P, NB, DI])
        w_rs = sb("w_rs", [P, NB, DI])
        w_out_sb = sb("w_out_sb", [P, 2, DM])
        ffn_w_sb = sb("ffn_w_sb", [P, DM])
        ffn_at_sb = sb("ffn_at_sb", [16, DM])
        ffn_b_sb = sb("ffn_b_sb", [16, DM])
        w_eff = sb("w_eff", [P, DM])
        stats = sb("stats", [P, NB, 6])
        mv = sb("mv", [P, NB, 2])
        lnv = sb("lnv", [P, NB])
        rstd = sb("rstd", [P, NB])
        var_eps = sb("var_eps", [P, NB])
        var_both = sb("var_both", [P, NB])
        newton = sb("newton", [P, NB])
        newton8 = sb("newton8", [P, 8])
        xn = sb("xn", [P, NB, DM])
        xn_t = sb("xn_t", [P, TOK])
        xb = sb("xb", [P, NB, DM])
        q_f = sb("q_f", [P, TOK])
        q_r = sb("q_r", [P, TOK])
        q_split = sb("q_split", [P, 3, TOK], BF16)
        k_f = sb("k_f", [P, NB, BLK])
        k_r = sb("k_r", [P, BLK])
        k_split = sb("k_split", [P, NB, 3, BLK], BF16)
        q_stack = sb("q_stack", [P, H, TOK], BF16)
        k_stack = [sb(f"k_stack{b}", [P, H, BLK], BF16) for b in range(NB)]
        v_ones = sb("v_ones", [P, NB, KT, H, DH + 1])
        junk = sb("junk", [P, 2, BLK], BF16)
        head_maxima = sb("head_maxima", [P, NB, H])
        no_key = sb("no_key", [P, H])
        neg_max = sb("neg_max", [P, H])
        neg_max_rest = sb("neg_max_rest", [P, H])
        m_split = sb("m_split", [P, NB, 3 * H], BF16)
        m_t = sb("m_t", [3 * H, NB + 1, S], BF16)
        probs = sb("probs", [P, 3, 8, S])
        probs_flat = probs[:, :, :, :].rearrange("p a h s -> p (a h s)")
        o_sb = sb("o_sb", [P, 2, 4 * S])
        rden = sb("rden", [P, H])
        attn = sb("attn", [P, 2, DM])
        attn_t = sb("attn_t", [P, 2, S])
        x1 = sb("x1", [P, NB, DM])

        def chain_view(stack, half):
            flat = stack[:, :, :].rearrange("p h k -> p (h k)").bitcast(F32)
            return flat[:, 2048 * half:2048 * (half + 1)]

        k_ch, q_ch = chain_view(k_stack[0], 0), chain_view(k_stack[0], 1)
        chunked = lambda v, n: v.rearrange("p (d c j) -> p d c j", c=NC, j=n)
        flat1 = k_stack[1][:, :, :].rearrange("p h k -> p (h k)").bitcast(F32)
        flat2 = k_stack[2][:, :, :].rearrange("p h k -> p (h k)").bitcast(F32)
        kappa = flat1[:, 0:(HD + 1) * S]
        kap_t = kappa.rearrange("p (d t) -> p d t", d=HD + 1)
        kap_c = chunked(kappa, C)
        pair_tmp = flat1[:, (HD + 1) * S:(HD + 1) * S + (HD + 1) * NC * 3]
        SLOT = C + 1
        NS = (NC + 1) * SLOT
        bank = flat2[:, 0:(HD + 1) * NS].rearrange("p (d n) -> p d n", d=HD + 1)
        bank_c = bank.rearrange("p d (c j) -> p d c j", j=SLOT)
        at = [(HD + 1) * NS]

        def carve(n):
            at[0] += n
            return flat2[:, at[0] - n:at[0]]

        gram, dcoef = (carve(NPAIR * NC) for _ in range(2))
        coef = carve(NC * SLOT)
        coef_c = coef.rearrange("p (c j) -> p c j", j=SLOT)
        m_pair = carve(3 * NC).rearrange("p (c j) -> p c j", j=3)
        m_three = carve(2 * NC).rearrange("p (c j) -> p c j", j=2)
        bcoef = carve(S).rearrange("p (c j) -> p c j", j=C)
        tot_buf = carve(4 * NC)
        inner = k_stack[3][:, :, :].rearrange("p h k -> p (h k)").bitcast(F32)[:, 2048:4096]
        squares = chain_view(k_stack[3], 0).rearrange("p (i t) -> p i t", i=4)
        by_t = lambda v: v.rearrange("p (d t) -> p d t", d=HD)
        xr = xn
        xr_t = xn_t
        ks_flat = k_split[:, :, :, :].rearrange("p b l k -> p (b l k)").bitcast(F32)
        ln_both = sb("ln_both", [P, NB])
        rstd_both = sb("rstd_both", [P, NB])
        x1_plus_norm = ks_flat[:, 1024:1536].rearrange("p (b d) -> p b d", b=NB)
        x1_norm = ks_flat[:, 1536:2048].rearrange("p (b d) -> p b d", b=NB)
        mask_flat = mask_sb[:, :, :].rearrange("p b k -> p (b k)").bitcast(F32)
        v_flat = v_ones[:, :, :, :, :].rearrange("p b t h e -> p (b t h e)")
        n_xg = 2 * NB * (S + 3)
        conv_in = mask_flat[:, 0:n_xg].rearrange("p (i b t) -> p i b t", i=2, b=NB)
        gate_ch = mask_flat[:, n_xg:n_xg + 7 * S].rearrange("p (g t) -> p g t", g=7)
        pair = lambda flat, n: flat[:, 2 * S * n:2 * S * (n + 1)].rearrange("p (a t) -> p a t", a=2)
        two = lambda v: v.rearrange("p (i t) -> p i t", i=2)
        spare = chain_view(k_stack[3], 1)
        conv, sigc = two(spare[:, 0:2 * TOK]), two(spare[:, 2 * TOK:4 * TOK])
        ctx_flat = ctx_sb[:, :, :].rearrange("p b k -> p (b k)")
        x_conv, z_silu = two(ctx_flat[:, 0:2 * TOK]), two(ctx_flat[:, 2 * TOK:4 * TOK])
        neg_flat = mask_neg[:, :, :].rearrange("p b k -> p (b k)")
        sigz = two(neg_flat[:, 0:2 * TOK])
        kq_rows = k_f[:, :, :]
        v_rows = q_f[0:2 * H, :]
        knorm_rows = k_r[0:H, :]
        qnorm_rows = q_split[:, :, :].rearrange("p l t -> p (l t)").bitcast(F32)[0:H, 0:TOK]
        g_rows = q_r[0:7 * H, :]
        v_own, v_swap = v_flat[:, 0:S], v_flat[:, S:2 * S]
        sig_bc, sig_br = pair(v_flat, 1), pair(v_flat, 2)
        sig_om = sb("sig_om", [P, S])
        names = ["key_sumsq", "ln_key", "key_rroot", "key_recip", "query_sumsq", "ln_query", "query_rroot",
                 "query_recip", "dt", "half_alpha_dt", "half_omega_dt", "w_sq", "a_sq", "one_plus_sq", "c_numer",
                 "det", "det_mirror", "det_recip", "mag_sq_raw", "ln_mag_sq", "ln_mag2", "decay", "decay_sq",
                 "c_numer_sq", "phasor_sumsq", "is_zero", "ln_sumsq", "phasor_rroot", "t1", "t2", "t3", "vp_arg",
                 "ln_vp_arg", "vp_rroot", "vp_scale", "v_cos", "v_sin", "v_turned", "beta_recip", "coupling",
                 "query_gate", "retrieved", "query_norm", "cos_part", "sin_part", "t4", "t5", "t6", "t7", "t8",
                 "turn_cos", "turn_sin", "pool_tmp"]
        q_flat = q_stack[:, :, :].rearrange("p h k -> p (h k)").bitcast(F32)
        room = [q_flat[:, S * i:S * (i + 1)] for i in range(32)] + [probs_flat[:, S * i:S * (i + 1)] for i in range(24)]
        T = dict(zip(names, room))
        abs_gates, exp_neg_abs, one_plus_exp, ln_one_plus, corr, softplus = (pair(v_flat, 3 + i) for i in range(6))
        exp_log_dt = sb("exp_log_dt", [P, 1])
        phasor = [pair(ks_flat, i) for i in range(2)]
        twist_by_re, twist_by_im = pair(ks_flat, 2), pair(ks_flat, 3)
        dot_junk = sb("dot_junk", [P, C, HD + 1])
        terms = sb("terms", [P, HD, SLOT])
        gn_stats = sb("gn_stats", [P, 8, 6])
        gn_mv = sb("gn_mv", [P, 8, 2])
        gn_mean = sb("gn_mean", [P, 8])
        gn_delta = sb("gn_delta", [P, 8])
        gn_spread = sb("gn_spread", [P, 8])
        gn_ln = sb("gn_ln", [P, 8])
        gn_var_eps = sb("gn_var_eps", [P, 8])
        gn_rstd = sb("gn_rstd", [P, 8])
        gn_scale = sb("gn_scale", [P, 8])
        gn_bias = sb("gn_bias", [P, 8])
        yn = sigc
        y2 = conv
        x2 = xb
        w_row_max = sb("w_row_max", [P, 1])
        w_max = sb("w_max", [P, 1])
        int4_scale = sb("int4_scale", [P, 1])
        int4_scale_recip = sb("int4_scale_recip", [P, 1])
        w_int4 = sb("w_int4", [P, DM])
        res = ks_flat[:, 2048:2560].rearrange("p (b d) -> p b d", b=NB)

        mask_sum = sb("mask_sum", [P, 1])
        some_open = sb("some_open", [P, 1])
        go_general = sb("go_general", [1, 1], I32)
        q_cur = k_stack[1][:, :, 0:S]
        q_raw = k_stack[2][:, :, 0:S]
        m_blk = sb("m_blk", [P, H])
        m_run = sb("m_run", [P, H])
        m_new = sb("m_new", [P, H])
        fade_arg = sb("fade_arg", [P, H])
        fade = sb("fade", [P, H])
        o_run = sb("o_run", [P, H, DH + 1])

        SA = [pb(f"SA{i}", [P, BLK]) for i in range(2)]
        SB = [pb(f"SB{i}", [P, 2, BLK]) for i in range(2)]
        MI = pb("MI", [P, BLK])
        OT = pb("OT", [P, BLK])

        s_x, s_vec, s_id, s_wq, s_wk, s_wv, s_wo, s_rows = (sem(n) for n in (
            "s_x", "s_vec", "s_id", "s_wq", "s_wk", "s_wv", "s_wo", "s_rows"))
        s_ctx = [sem(f"s_ctx{i}") for i in range(2)]
        s_mask = sem("s_mask")
        s_mask_rest = sem("s_mask_rest")
        late_weights_loaded = sem("late_weights_loaded")
        dve_early = sem("dve_early")
        kst0_filled = sem("kst0_filled")
        kst_filled = sem("kst_filled")
        qst_filled = sem("qst_filled")
        ot_zeroed = sem("ot_zeroed")
        consts_ready = sem("consts_ready")
        mask_ready = sem("mask_ready")
        v_ones_set = sem("v_ones_set")
        ln_var = sem("ln_var")
        ln_rstd = sem("ln_rstd")
        xn_ready = sem("xn_ready")
        xnT_done = sem("xnT_done")
        xnT_copied = sem("xnT_copied")
        q_done = sem("q_done")
        q_copied = sem("q_copied")
        q_split_done = sem("q_split_done")
        q_stacked = sem("q_stacked")
        q_stacked_lo = sem("q_stacked_lo")
        k_done = sem("k_done")
        k_copied = sem("k_copied")
        k_split_done = sem("k_split_done")
        k_stacked = [sem(f"k_stacked{b}") for b in range(NB)]
        v_done = sem("v_done")
        v_copied = sem("v_copied")
        score_done = sem("score_done")
        max_done = sem("max_done")
        neg_max_done = sem("neg_max_done")
        mT_done = sem("mT_done")
        mT_copied = sem("mT_copied")
        m_stacked = sem("m_stacked")
        m_stacked_hi = sem("m_stacked_hi")
        unit_scored = sem("unit_scored")
        unit_exp = sem("unit_exp")
        unit_pv = sem("unit_pv")
        o_copied = sem("o_copied")
        oT_done = sem("oT_done")
        attn_done = sem("attn_done")
        aT_done = sem("aT_done")
        aT_copied = sem("aT_copied")
        wo_done = sem("wo_done")
        x1_done = sem("x1_done")
        stored = sem("stored")
        act_done = sem("act_done")
        xb_done = sem("xb_done")

        rms_done = sem("rms_done")
        xg_done = sem("xg_done")
        xg_copied = sem("xg_copied")
        kp_done = sem("kp_done")
        kp_copied = sem("kp_copied")
        vp_done = sem("vp_done")
        vp_copied = sem("vp_copied")
        z_done = sem("z_done")
        conv_done = sem("conv_done")
        sigc_done = sem("sigc_done")
        xc_done = sem("xc_done")
        sigz_done = sem("sigz_done")
        gate_done = sem("gate_done")
        gate_copied = sem("gate_copied")
        qp_done = sem("qp_done")
        qp_copied = sem("qp_copied")
        pad_zeroed = sem("pad_zeroed")
        k_stored = sem("k_stored")
        v_stored = sem("v_stored")
        g_stored = sem("g_stored")
        q_stored = sem("q_stored")
        k_loaded = sem("k_loaded")
        v_loaded = sem("v_loaded")
        g_loaded = sem("g_loaded")
        q_loaded = sem("q_loaded")
        abs_done = sem("abs_done")
        one_plus_exp_done = sem("one_plus_exp_done")
        mag_sq_done = sem("mag_sq_done")
        phasor_sumsq_done = sem("phasor_sumsq_done")
        ln_mag2_done = sem("ln_mag2_done")
        vp_arg_done = sem("vp_arg_done")
        parts_done = sem("parts_done")
        y_done = sem("y_done")
        gn_stats_done = sem("gn_stats_done")
        gn_mean_done = sem("gn_mean_done")
        gn_spread_done = sem("gn_spread_done")
        gn_var_averaged = sem("gn_var_averaged")
        gn_rstd_done = sem("gn_rstd_done")
        gn_bias_done = sem("gn_bias_done")
        yn_done = sem("yn_done")
        y2_done = sem("y2_done")
        layer_projected = sem("layer_projected")
        x2_done = sem("x2_done")
        ffn_done = sem("ffn_done")
        res_done = sem("res_done")
        w_row_max_done = sem("w_row_max_done")
        w_max_done = sem("w_max_done")
        lowrank_done = sem("lowrank_done")
        w_rs_signed = sem("w_rs_signed")
        x1_norm_done = sem("x1_norm_done")
        x1_plus_norm_done = sem("x1_plus_norm_done")
        gates_sigmoid = sem("gates_sigmoid")
        gate_exps = sem("gate_exps")
        gate_logs = sem("gate_logs")
        decays_done = sem("decays_done")
        sum_done = sem("sum_done")
        open_done = sem("open_done")
        count_done = sem("count_done")
        flag_done = sem("flag_done")
        g_ctx = sem("g_ctx")
        g_mask = sem("g_mask")
        g_kproj = sem("g_kproj")
        g_kcopied = sem("g_kcopied")
        g_ksplit = sem("g_ksplit")
        g_kstacked = sem("g_kstacked")
        g_vproj = sem("g_vproj")
        g_vcopied = sem("g_vcopied")
        g_maskset = sem("g_maskset")
        g_q = sem("g_q")
        bank_set = sem("bank_set")
        gram_products = sem("gram_products")
        gn_var_done = sem("gn_var_done")
        knorm_loaded = sem("knorm_loaded")
        kroot_done = sem("kroot_done")
        qnorm_done = sem("qnorm_done")
        norm_copied = sem("norm_copied")
        norm_stored = sem("norm_stored")
        norm_loaded = sem("norm_loaded")
        squared = sem("squared")
        pool_done = sem("pool_done")
        phasors_done = sem("phasors_done")
        prefix_done = sem("prefix_done")
        fades_done = sem("fades_done")
        rq_done = sem("rq_done")
        turn_done = sem("turn_done")
        chunks_done = sem("chunks_done")
        pool_retrieved = sem("pool_retrieved")
        norms_summed = sem("norms_summed")
        g_masked = sem("g_masked")
        g_fade_arg = sem("g_fade_arg")
        g_fade = sem("g_fade")
        g_merged = sem("g_merged")
        g_step = sem("g_step")
        dve_post = sem("dve_post")

        PRE = H // 2
        FIRST = 13
        AHEAD_UNITS = 4

        def heads_of_unit(n):
            if n == 0:
                return range(FIRST, H)
            if n <= AHEAD_UNITS:
                return range(H + 4 * (n - 1), H + 4 * n)
            first = H + 4 * AHEAD_UNITS + 2 * (n - AHEAD_UNITS - 1)
            return range(min(first, NB * H), min(first + 2, NB * H))

        def col(name, n=P):
            return vec_sb[0:n, VEC[name]:VEC[name] + 1]

        key_chunks = chunked(k_ch, C)
        query_chunks = chunked(q_ch, C)
        gram_products_late = pair_tmp[:, 0:HD * NC * 3].rearrange("p (d c j) -> p d c j", d=HD, j=3)
        inner_c = chunked(inner, C)
        tot = [tot_buf[:, NC * 2 * i:NC * 2 * (i + 1)].rearrange("p (a c) -> p a c", a=2) for i in range(2)]
        FIRST_CHUNKS = 8
        DVE_CHUNKS = 4
        POOL_CHUNKS = [(0, 8), (8, 7), (15, 7), (22, NC - DVE_CHUNKS - 22)]

        def retrieve(eng, run, settle, c0, n):
            cs = slice(c0, c0 + n)
            mc = T["decay"][:, :].rearrange("p (o c j) -> p o c j", o=1, j=C)
            u = coef.rearrange("p (o c j) -> p o c j", o=1, j=SLOT)
            run(eng.tensor_tensor(inner_c[:, :, cs, 0:C - 1], key_chunks[:, :, cs, 0:C - 1],
                                  u[:, :, cs, 1:C].to_broadcast([P, HD, n, C - 1]), ALU.mult))
            before = bank_c[:, 0:HD, cs, 0]
            for j in range(C - 1):
                run(eng.tensor_tensor(inner_c[:, :, cs, C - 1], before, mc[:, :, cs, j].to_broadcast([P, HD, n]),
                                      ALU.mult))
                settle()
                run(eng.tensor_tensor(inner_c[:, :, cs, j], inner_c[:, :, cs, j], inner_c[:, :, cs, C - 1], ALU.add))
                settle()
                before = inner_c[:, :, cs, j]
            run(eng.tensor_tensor(inner_c[:, :, cs, 0:C - 1], inner_c[:, :, cs, 0:C - 1],
                                  query_chunks[:, :, cs, 0:C - 1], ALU.mult))
            run(eng.tensor_tensor(inner_c[:, :, cs, C - 1], bank_c[:, 0:HD, c0 + 1:c0 + n + 1, 0],
                                  query_chunks[:, :, cs, C - 1],
                                  ALU.mult))

        block = ctx.enter_context(nc.Block())

        @block.sync
        def _(sp):
            sp.dma_start(x_sb[:, :, :], x.rearrange("b s d -> s b d")).then_inc(s_x, 16)
            sp.dma_start(wk_sb[:, :], wk).then_inc(s_wk, 16)
            sp.dma_start(ctx_sb[:, 0, :], ctx_t[0, :, NK - BLK:NK]).then_inc(s_ctx[0], 16)
            sp.dma_start(wq_sb[:, :], wq).then_inc(s_wq, 16)
            sp.dma_start(ctx_sb[:, 1:NB, :], ctx_t[1:NB, :, NK - BLK:NK].rearrange("b d k -> d b k"))\
                .then_inc(s_ctx[1], 16)
            sp.dma_start(wv_sb[:, :], wv).then_inc(s_wv, 16)
            sp.dma_start(rows_sb[:, :, :], rows).then_inc(s_rows, 16)
            sp.dma_start(wo_sb[:, :], wo).then_inc(s_wo, 16)
            for b in range(NB):
                sp.wait_ge(k_split_done, b + 1)
                sp.wait_ge(kst_filled if b else kst0_filled, b or 3)
                for t in range(NTERM):
                    sp.dma_start(k_stack[b][DH * t:DH * (t + 1), :, :], k_split[:, b, K_LEVEL[t], :])\
                      .then_inc(k_stacked[b], 16)
                if b == 0:
                    sp.wait_ge(q_split_done, 1)
                    sp.wait_ge(qst_filled, 1)
                    for t in range(NTERM // 2):
                        sp.dma_start(q_stack[DH * t:DH * (t + 1), :, :], q_split[:, Q_LEVEL[t], :])\
                            .then_inc(q_stacked_lo, 16)
            sp.wait_ge(flag_done, 1)
            with sp.If(sp.value_load(go_general[0:1, 0:1]) != 0):
                for b in range(NB):
                    sp.wait_ge(k_stacked[b], 16 * NTERM)
                sp.wait_ge(mask_ready, NB)
                with sp.Fori(0, NB) as b:
                    with sp.Fori(0, NBLK) as k:
                        n = b * NBLK + k
                        sp.wait_ge(g_merged, n + 1)
                        sp.dma_start(ctx_sb[:, 0, :], ctx_t[bass.ds(b, 1), :, bass.ds(k * BLK, BLK)]
                                     .rearrange("o d k -> d (o k)")).then_inc(g_ctx, 16)
                        sp.dma_start(mask_sb[:, 0, 0:BLK], mask[bass.ds(b, 1), :, bass.ds(k * BLK, BLK)]
                                     .rearrange("o q k -> q (o k)")).then_inc(g_mask, 16)
                        sp.wait_ge(g_ksplit, n + 1)
                        for t in range(NTERM):
                            sp.dma_start(k_stack[0][DH * t:DH * (t + 1), :, :], k_split[:, 0, K_LEVEL[t], :])\
                              .then_inc(g_kstacked, 16)
                        sp.wait_ge(mT_copied, n + 2)
                        sp.dma_start(q_cur[MROW:MROW + 3, :, :], m_t[:, 0, :]).then_inc(m_stacked, 16)
            with sp.Else():
                sp.nop()
            sp.nop()
            sp.wait_ge(x1_done, 1)
            for dst, src in ((w_in_sb[:, :], w_in), (w_gate_sb[:, :, :], w_gate), (w_q_sb[:, :, :], w_q),
                             (w_rd[:, :, :], w_read[0]), (w_rs[:, :, :], w_read[1]), (w_out_sb[:, :, :], w_out),
                             (ffn_w_sb[:, :], ffn_w), (ffn_at_sb[:, :], ffn_at), (ffn_b_sb[:, :], ffn_b),
                             (avg_sb[:, :], avg), (heads_sb[:, :, :], heads)):
                sp.dma_start(dst, src).then_inc(late_weights_loaded, 16)
            sp.wait_ge(kp_copied, 2)
            sp.dma_start(scratch[ROW_K:ROW_K + DI, :].rearrange("(i p) t -> p i t", i=2), kq_rows[:, 0:2, :])\
                .then_inc(k_stored, 16)
            sp.wait_ge(k_stored, 16)
            for s in range(2):
                sp.dma_start(k_ch[64 * s:64 * (s + 1), :],
                             scratch[ROW_K:ROW_K + DI, :].rearrange("(h d) (b t) -> b h d t", d=HD, b=NB))\
                    .then_inc(k_loaded, 16)
            sp.wait_ge(gate_copied, 1)
            sp.dma_start(scratch[ROW_G:ROW_G + 7 * H, :], g_rows).then_inc(g_stored, 16)
            sp.wait_ge(norm_copied, 1)
            sp.dma_start(scratch[ROW_N:ROW_N + H, :], knorm_rows).then_inc(norm_stored, 16)
            sp.wait_ge(vp_copied, 1)
            sp.dma_start(scratch[ROW_V:ROW_V + 2 * H, :], v_rows).then_inc(v_stored, 16)
            sp.wait_ge(g_stored, 16)
            for s in range(2):
                sp.dma_start(gate_ch[64 * s:64 * (s + 1), :, :],
                             scratch[ROW_G:ROW_G + 7 * H, :].rearrange("(h g) (b t) -> b h g t", g=7, b=NB))\
                    .then_inc(g_loaded, 16)
            sp.wait_ge(norm_stored, 16)
            for s in range(2):
                sp.dma_start(T["key_sumsq"][64 * s:64 * (s + 1), :],
                             scratch[ROW_N:ROW_N + H, :].rearrange("h (b t) -> b h t", b=NB)).then_inc(knorm_loaded, 16)
            sp.wait_ge(v_stored, 16)
            v_src = scratch[ROW_V:ROW_V + 2 * H, :].rearrange("(h s) (b t) -> s b h t", s=2, b=NB)
            for s in range(2):
                sp.dma_start(v_own[64 * s:64 * (s + 1), :], v_src[s]).then_inc(v_loaded, 16)
                sp.dma_start(v_swap[64 * s:64 * (s + 1), :], v_src[1 - s]).then_inc(v_loaded, 16)
            sp.wait_ge(qp_copied, 2)
            sp.dma_start(scratch[ROW_Q:ROW_Q + DI, :].rearrange("(i p) t -> p i t", i=2), kq_rows[:, 2:4, :])\
                .then_inc(q_stored, 16)
            sp.wait_ge(q_stored, 16)
            for s in range(2):
                sp.dma_start(q_ch[64 * s:64 * (s + 1), :],
                             scratch[ROW_Q:ROW_Q + DI, :].rearrange("(h d) (b t) -> b h d t", d=HD, b=NB))\
                    .then_inc(q_loaded, 16)
            sp.wait_ge(norm_copied, 2)
            sp.dma_start(scratch[ROW_N + H:ROW_N + 2 * H, :], qnorm_rows).then_inc(norm_stored, 16)
            sp.wait_ge(norm_stored, 32)
            for s in range(2):
                sp.dma_start(T["query_sumsq"][64 * s:64 * (s + 1), :],
                             scratch[ROW_N + H:ROW_N + 2 * H, :].rearrange("h (b t) -> b h t",
                                                                           b=NB)).then_inc(norm_loaded, 16)
            sp.wait_ge(res_done, 1)
            sp.dma_start(out.rearrange("b s d -> s b d"), res[:, :, :]).then_inc(stored, 16)
            sp.wait_ge(stored, 16)

        @block.gpsimd
        def _(pool):
            pool.memset(q_stack[:, :, :].bitcast(F32), 0.0).then_inc(qst_filled, 1)
            pool.memset(v_ones[:, :, :, :, DH:DH + 1], 1.0).then_inc(v_ones_set, 1)
            pool.memset(k_stack[1][:, :, :].bitcast(F32), ONES_PAIR).then_inc(kst_filled, 1)
            pool.wait_ge(q_split_done, 1)
            pool.wait_ge(qst_filled, 1)
            for t in range(NTERM // 2, NTERM):
                pool.dma_start(q_stack[DH * t:DH * (t + 1), :, :], q_split[:, Q_LEVEL[t], :])\
                    .then_inc(q_stacked, 16)
            pool.dma_start(mask_sb[:, :, 0:NK - BLK], mask.rearrange("b q k -> q b k")[:, :, 0:NK - BLK])\
                .then_inc(s_mask_rest, 16)
            for b in range(NB):
                pool.wait_ge(s_mask, 16)
                last = NK - BLK
                pool.tensor_scalar(mask_neg[:, b, :], mask_sb[:, b, last:NK], -BIG, 1.0, ALU.mult, ALU.mult)
                pool.tensor_scalar(mask_bf[:, b, :], mask_sb[:, b, last:NK], 1.0, 1.0, ALU.mult, ALU.mult)\
                    .then_inc(mask_ready, 1)
                if b == 0:
                    for later in (2, 3):
                        pool.memset(k_stack[later][:, :, :].bitcast(F32), ONES_PAIR).then_inc(kst_filled, 1)
            pool.wait_ge(s_x, 16)
            pool.wait_ge(s_rows, 16)
            for b in range(NB):
                pool.tensor_tensor(xb[:, b, :], x_sb[:, b, :], rows_sb[:, 1, :], ALU.add).then_inc(xb_done, 1)
            pool.nop()
            G = nc.gpsimd
            pool.wait_ge(x1_done, NB)
            pool.memset(conv_in[:, :, :, 0:3], 0.0).then_inc(pad_zeroed, 1)
            pool.memset(bank[:, HD, :], 1.0).then_inc(bank_set, 1)
            pool.memset(bank[:, 0:HD, 0:1], 0.0).then_inc(bank_set, 1)
            pool.wait_ge(w_row_max_done, 1)
            pool.partition_all_reduce(w_max[:, :], w_row_max[:, :], P, bass.bass_isa.ReduceOp.max)\
                .then_inc(w_max_done, 1)
            pool.wait_ge(late_weights_loaded, 16 * LATE_LOADS)
            for i in range(2):
                pool.wait_ge(kp_copied, i + 1)
                G.tensor_tensor(squares[:, i, :], kq_rows[:, i, :], kq_rows[:, i, :], ALU.mult).then_inc(squared, 1)
            pool.tensor_scalar(w_rs[:, :, :], w_rs[:, :, :], col("sgn"), 1.0, ALU.mult, ALU.mult)\
                .then_inc(w_rs_signed, 1)
            pool.wait_ge(k_loaded, 32)
            G.tensor_tensor(gram_products_late[:, :, :, 0:2], key_chunks[:, :, :, 2:4],
                            key_chunks[:, :, :, 1:2].to_broadcast([P, HD, NC, 2]), ALU.mult)\
                .then_inc(gram_products, 1)
            G.tensor_tensor(gram_products_late[:, :, :, 2:3], key_chunks[:, :, :, 3:4], key_chunks[:, :, :, 2:3],
                            ALU.mult).then_inc(gram_products, 1)
            for i in range(2):
                pool.wait_ge(qp_copied, i + 1)
                G.tensor_tensor(squares[:, 2 + i, :], kq_rows[:, 2 + i, :], kq_rows[:, 2 + i, :], ALU.mult)\
                    .then_inc(squared, 1)
            pool.tensor_copy(bank_c[:, 0:HD, 0:NC, C:C + 1], key_chunks[:, :, :, C - 1:C]).then_inc(bank_set, 1)

            pool_n = [0]

            def run(ins):
                pool_n[0] += 1
                ins.then_inc(pool_done, 1)

            def settle():
                pool.wait_ge(pool_done, pool_n[0])

            def twist(re, im, dst, src, by, p0, p1):
                run(G.tensor_tensor(p0, src, by[0], ALU.mult))
                run(G.tensor_tensor(p1, src, by[1], ALU.mult))
                settle()
                run(G.tensor_tensor(re(dst), re(p0), im(p1), ALU.subtract))
                run(G.tensor_tensor(im(dst), im(p0), re(p1), ALU.add))

            pool.wait_ge(phasors_done, 2)
            inside = [v.rearrange("p a (c j) -> p a c j", j=C) for v in phasor]
            work = [v.rearrange("p a (c j) -> p a c j", j=C) for v in (twist_by_re, twist_by_im)]
            re4, im4 = (lambda v: v[:, 0, :, :]), (lambda v: v[:, 1, :, :])
            for r, off in enumerate((1, 2)):
                X, Y = inside[r % 2], inside[1 - r % 2]
                n = C - off
                run(G.tensor_copy(Y[:, :, :, 0:off], X[:, :, :, 0:off]))
                twist(re4, im4, Y[:, :, :, off:C], X[:, :, :, off:C],
                      [X[:, a:a + 1, :, 0:n].to_broadcast([P, 2, NC, n]) for a in range(2)],
                      work[0][:, :, :, 0:n], work[1][:, :, :, 0:n])
                settle()
            run(G.tensor_copy(tot[0], inside[0][:, :, :, C - 1]))
            settle()
            re3, im3 = (lambda v: v[:, 0, :]), (lambda v: v[:, 1, :])
            off, r = 1, 0
            while off < NC:
                X, Y = tot[r % 2], tot[1 - r % 2]
                n = NC - off
                run(G.tensor_copy(Y[:, :, 0:off], X[:, :, 0:off]))
                twist(re3, im3, Y[:, :, off:NC], X[:, :, off:NC],
                      [X[:, a:a + 1, 0:n].to_broadcast([P, 2, n]) for a in range(2)],
                      twist_by_re[:, :, 0:n], twist_by_im[:, :, 0:n])
                settle()
                off, r = 2 * off, r + 1
            before = tot[r % 2][:, :, 0:NC - 1].rearrange("p a (c o) -> p a c o", o=1)
            run(G.tensor_copy(inside[1][:, :, 0, :], inside[0][:, :, 0, :]))
            twist(re4, im4, inside[1][:, :, 1:NC, :], inside[0][:, :, 1:NC, :],
                  [before[:, a:a + 1, :, :].to_broadcast([P, 2, NC - 1, C]) for a in range(2)],
                  work[0][:, :, 1:NC, :], work[1][:, :, 1:NC, :])
            settle()
            pool.nop().then_inc(prefix_done, 1)
            pool.wait_ge(fades_done, 2)
            mc = T["decay"][:, :].rearrange("p (c j) -> p c j", j=C)
            for c0, c1 in ((0, FIRST_CHUNKS), (FIRST_CHUNKS, NC)):
                for j, fade_to_end in enumerate((m_three[:, c0:c1, 1:2], m_pair[:, c0:c1, 2:3], mc[:, c0:c1, 3:4])):
                    G.tensor_tensor(bank_c[:, 0:HD, c0:c1, 1 + j], key_chunks[:, :, c0:c1, j],
                                    fade_to_end.rearrange("p c o -> p o c").to_broadcast([P, HD, c1 - c0]), ALU.mult)\
                        .then_inc(bank_set, 1)
            def product(dst, x0, x1_):
                run(G.tensor_tensor(T[dst][:, :], T[x0][:, :], T[x1_][:, :], ALU.mult))
                settle()

            pool.wait_ge(rq_done, 1)
            product("pool_tmp", "query_sumsq", "query_rroot")
            product("pool_tmp", "pool_tmp", "query_rroot")
            run(G.tensor_scalar(T["pool_tmp"][:, :], T["pool_tmp"][:, :], -0.5, 1.5, ALU.mult, ALU.add))
            settle()
            product("query_rroot", "query_rroot", "pool_tmp")
            product("query_norm", "query_sumsq", "query_rroot")
            G.tensor_scalar(T["query_norm"][:, :], T["query_norm"][:, :], 1.0e-6, 0.0, ALU.add, ALU.add)\
                .then_inc(qnorm_done, 1)
            pool.wait_ge(rq_done, 2)
            product("pool_tmp", "query_recip", "query_norm")
            run(G.tensor_scalar(T["pool_tmp"][:, :], T["pool_tmp"][:, :], -1.0, 2.0, ALU.mult, ALU.add))
            settle()
            product("query_recip", "query_recip", "pool_tmp")
            run(G.tensor_tensor(T["query_gate"][:, :], T["query_recip"][:, :], sig_bc[:, 1, :], ALU.mult))
            settle()
            G.tensor_tensor(T["turn_cos"][:, :], T["query_gate"][:, :], phasor[1][:, 0, :], ALU.mult)\
                .then_inc(turn_done, 1)
            G.tensor_tensor(T["turn_sin"][:, :], T["query_gate"][:, :], phasor[1][:, 1, :], ALU.mult)\
                .then_inc(turn_done, 1)
            pool.wait_ge(q_loaded, 32)
            for g, (c0, n) in enumerate(POOL_CHUNKS):
                pool.wait_ge(chunks_done, g + 1)
                retrieve(G, run, settle, c0, n)
            settle()
            pool.nop().then_inc(pool_retrieved, 1)
            pool.wait_ge(x1_norm_done, NB)
            pool.tensor_tensor(x1_plus_norm[:, :, :], x1[:, :, :], x1_norm[:, :, :], ALU.add)\
                .then_inc(x1_plus_norm_done, 1)

        @block.scalar
        def _(act):
            act.dma_start(vec_sb[:, :], vec).then_inc(s_vec, 16)
            act.dma_start(id_sb[:, :], ident).then_inc(s_id, 16)
            act.preload_act_table_set("natural_log_exp_and_others")
            act.wait_ge(s_vec, 16)
            act.wait_ge(ln_var, 1)
            nc.scalar.activation(lnv[:, :], mv[:, :, 1], ACT.Ln, bias=col("eps_ln")).then_inc(act_done, 1)
            act.wait_ge(act_done, 1)
            nc.scalar.activation(rstd[:, :], lnv[:, :], ACT.Exp, scale=-0.5).then_inc(ln_rstd, 1)

            def k_evac(b):
                act.wait_ge(k_done, b + 1)
                src = SB[b // 2][:, b % 2, :]
                nc.scalar.activation(k_f[:, b, :], src, ACT.Identity, bias=col("bk")).then_inc(k_copied, 1)
                nc.scalar.activation(k_split[:, b, 0, :], src, ACT.Identity, bias=col("bk")).then_inc(k_copied, 1)

            act.wait_ge(xnT_done, 1)
            nc.scalar.activation(xn_t[:, :], MI[:, :], ACT.Copy).then_inc(xnT_copied, 1)
            k_evac(0)
            act.wait_ge(q_done, 1)
            nc.scalar.activation(q_f[:, :], SA[0][:, :], ACT.Identity, bias=col("bq")).then_inc(q_copied, 1)
            nc.scalar.activation(q_split[:, 0, :], SA[0][:, :], ACT.Identity, bias=col("bq")).then_inc(q_copied, 1)
            k_evac(1)
            mask_q = mask.rearrange("b q k -> q b k")
            act.dma_start(mask_sb[:, :, NK - BLK:NK], mask_q[:, :, NK - BLK:NK]).then_inc(s_mask, 16)
            k_evac(2)
            k_evac(3)

            def v_evac(b):
                act.wait_ge(v_done, b + 1)
                nc.scalar.activation(v_ones[:, b, :, :, 0:DH],
                                     SB[b // 2][:, b % 2, :].rearrange("p (t h d) -> p t h d", t=KT, h=H), ACT.Copy)\
                    .then_inc(v_copied, 1)

            act.wait_ge(v_ones_set, 1)
            for b in range(NB):
                v_evac(b)

            def m_evac(b, part=None):
                act.wait_ge(mT_done, b + 2 if b else part + 1)
                rows_ = 3 * H if b else 24
                nc.scalar.activation(m_t[0:rows_, b if part != 1 else NB, :], MI[0:rows_, 0:S // 2].bitcast(BF16),
                                     ACT.Copy)\
                    .then_inc(mT_copied, 1)

            def m_stack(b, part, src):
                act.dma_start(q_stack[MROW:MROW + 3, 8 * part:8 * part + 8, S * b:S * (b + 1)], src)\
                    .then_inc(m_stacked_hi if part else m_stacked, 16)

            act.wait_ge(s_mask_rest, 16)
            nc.scalar.activation(probs_flat.bitcast(BF16)[:, 0:NB * (NK - BLK) // 2].rearrange("p (b k) -> p b k",
                                                                                               b=NB),
                                 mask_sb[:, :, 0:NK - BLK].bitcast(U16), ACT.Copy, accum_out=mask_sum[:, :])\
                .then_inc(sum_done, 1)

            def general_block(n):
                act.wait_ge(g_kproj, n + 1)
                for dst in (k_f[:, 0, :], k_split[:, 0, 0, :]):
                    nc.scalar.activation(dst, SB[0][:, 0, :], ACT.Identity, bias=col("bk")).then_inc(g_kcopied, 1)
                act.wait_ge(g_fade_arg, n + 1)
                nc.scalar.activation(fade[:, :], fade_arg[:, :], ACT.Exp, scale=SCALE).then_inc(g_fade, 1)
                act.wait_ge(mT_done, n + 2)
                nc.scalar.activation(m_t[:, 0, :], MI[0:3 * H, 0:S], ACT.Copy).then_inc(mT_copied, 1)
                for u in range(UNITS):
                    act.wait_ge(unit_scored, n * UNITS + u + 1)
                    if u >= 2:
                        act.wait_ge(unit_pv, n * UNITS + u - 1)
                    nc.scalar.activation(probs[:, u % 2, :, :],
                                         SB[u % 2][:, :, :].rearrange("p a (c s) -> p (a c) s", c=4),
                                         ACT.Exp, scale=SCALE).then_inc(unit_exp, 1)
                act.wait_ge(unit_pv, n * UNITS + UNITS)
                nc.scalar.activation(o_sb[:, 0, :], OT[:, :], ACT.Copy).then_inc(o_copied, 1)

            m_evac(0, 0)
            act.wait_ge(flag_done, 1)
            with act.If(act.value_load(go_general[0:1, 0:1]) != 0):
                with act.Fori(0, NB) as b:
                    with act.Fori(0, NBLK) as k:
                        general_block(b * NBLK + k)
                    act.wait_ge(aT_done, b + 1)
                    nc.scalar.activation(attn_t[:, 0, :], MI[:, 0:S], ACT.Copy).then_inc(aT_copied, 1)
            with act.Else():
                act.wait_ge(mT_copied, 1)
                m_stack(0, 0, m_t[0:24, 0, :])
                for n in range(8 * NB):
                    b, u = divmod(n, 8)
                    act.wait_ge(unit_scored, n + 1)
                    if n >= 3:
                        act.wait_ge(unit_pv, n - 2)
                    nc.scalar.activation(probs[:, n % 3, :, :], SB[n % 2][:, :, :].rearrange("p a (c s) -> p (a c) s",
                                                                                             c=4),
                                         ACT.Exp, scale=SCALE).then_inc(unit_exp, 1)
                    if u == 0 and b >= 1:
                        act.wait_ge(unit_pv, n)
                        nc.scalar.activation(o_sb[:, (b - 1) % 2, :], OT[:, :], ACT.Copy).then_inc(o_copied, 1)
                    if u == 2 and b >= 1:
                        act.wait_ge(aT_done, b)
                        nc.scalar.activation(attn_t[:, (b - 1) % 2, :], MI[:, 0:S], ACT.Copy).then_inc(aT_copied, 1)
                    if n == 1:
                        m_evac(0, 1)
                        act.wait_ge(mT_copied, 2)
                        m_stack(0, 1, m_t[0:24, NB, :])
                    if u == 5 and b + 1 < NB:
                        m_evac(b + 1)
                        act.wait_ge(mT_copied, b + 3)
                        for part in range(2):
                            m_stack(b + 1, part, m_t[24 * part:24 * part + 24, b + 1, :])
                act.wait_ge(unit_pv, 8 * NB)
                nc.scalar.activation(o_sb[:, (NB - 1) % 2, :], OT[:, :], ACT.Copy).then_inc(o_copied, 1)
                act.wait_ge(aT_done, NB)
                nc.scalar.activation(attn_t[:, (NB - 1) % 2, :], MI[:, 0:S], ACT.Copy).then_inc(aT_copied, 1)

            act.nop()

            def root_recip(dst, tmp, src, eps, ready, value, done, scale=1.0):
                act.wait_ge(ready, value)
                n = act_n[0] = act_n[0] + 1
                nc.scalar.activation(tmp, src, ACT.Ln, bias=eps, scale=scale).then_inc(act_done, 1)
                act.wait_ge(act_done, n)
                nc.scalar.activation(dst, tmp, ACT.Exp, scale=-0.5).then_inc(done, 1)

            act_n = [1]
            root_recip(rstd_both[:, :], ln_both[:, :], mv[:, :, 1], col("eps_both"), ln_var, 2, rms_done,
                       scale=1.0 + EPS_RMS)
            root_recip(rstd[:, :], lnv[:, :], mv[:, :, 1], col("eps_ln"), ln_var, 2, ln_rstd)
            act.preload_act_table_set("sigmoid_and_others")
            act.wait_ge(xnT_done, 2)
            nc.scalar.activation(xr_t[:, :], MI[:, :], ACT.Copy, scale=col("rms")).then_inc(xnT_copied, 1)
            act.wait_ge(pad_zeroed, 1)
            for i in range(2):
                act.wait_ge(xg_done, i + 1)
                nc.scalar.activation(conv_in[:, i, :, 3:], SB[0][:, i, :].rearrange("p (b t) -> p b t", b=NB),
                                     ACT.Identity,
                                     bias=col(f"xg_b{i}")).then_inc(xg_copied, 1)
            for i in range(2):
                act.wait_ge(kp_done, i + 1)
                nc.scalar.activation(kq_rows[:, i, :], SB[1][:, i, :], ACT.Identity, bias=col(f"k_b{i}"))\
                    .then_inc(kp_copied, 1)
            act.wait_ge(vp_done, 1)
            nc.scalar.activation(v_rows, SA[0][0:2 * H, :], ACT.Identity, bias=col("v_b", 2 * H)).then_inc(vp_copied, 1)
            for i in range(2):
                act.wait_ge(conv_done, i + 1)
                nc.scalar.activation(sigc[:, i, :], conv[:, i, :], ACT.Sigmoid).then_inc(sigc_done, 1)
            for i in range(2):
                act.wait_ge(z_done, i + 1)
                nc.scalar.activation(sigz[:, i, :], (SA[1], OT)[i][:, :], ACT.Sigmoid, bias=col(f"z_b{i}"))\
                    .then_inc(sigz_done, 1)

            def root_of_norm(y, tmp, src):
                nc.scalar.activation(tmp, src, ACT.Ln, scale=2.0 ** 30, bias=col("norm_floor")).then_inc(act_done, 1)
                act_n[0] += 1
                act.wait_ge(act_done, act_n[0])
                return nc.scalar.activation(y, tmp, ACT.Exp, scale=-0.5, bias=col("root_back"))

            act.wait_ge(norms_summed, 1)
            nc.scalar.activation(knorm_rows, SB[1][0:H, 0, :], ACT.Copy).then_inc(norm_copied, 1)
            act.wait_ge(gate_done, 1)
            nc.scalar.activation(g_rows, MI[0:7 * H, :], ACT.Identity, bias=col("gate_b", 7 * H))\
                .then_inc(gate_copied, 1)
            for i in range(2):
                act.wait_ge(qp_done, i + 1)
                nc.scalar.activation(kq_rows[:, 2 + i, :], SB[0][:, i, :], ACT.Copy).then_inc(qp_copied, 1)
            act.wait_ge(g_loaded, 32)
            nc.scalar.activation(sig_om[:, :], gate_ch[:, 1, :], ACT.Sigmoid, scale=2.0).then_inc(gates_sigmoid, 1)
            nc.scalar.activation(sig_bc[:, :, :], gate_ch[:, 2:4, :], ACT.Sigmoid).then_inc(gates_sigmoid, 1)
            nc.scalar.activation(sig_br[:, :, :], gate_ch[:, 5:7, :], ACT.Sigmoid).then_inc(gates_sigmoid, 1)
            act.preload_act_table_set("natural_log_exp_and_others")
            nc.scalar.activation(abs_gates[:, :, :], gate_ch[:, 0:5:4, :], ACT.Abs).then_inc(abs_done, 1)
            act.wait_ge(abs_done, 1)
            nc.scalar.activation(exp_neg_abs[:, :, :], abs_gates[:, :, :], ACT.Exp, scale=-1.0).then_inc(gate_exps, 1)
            nc.scalar.activation(exp_log_dt[:, :], col("log_dt"), ACT.Exp).then_inc(gate_exps, 1)
            act.wait_ge(knorm_loaded, 32)
            root_of_norm(T["key_rroot"][:, :], T["ln_key"][:, :], T["key_sumsq"][:, :]).then_inc(kroot_done, 1)
            act.preload_act_table_set("natural_log")
            act.wait_ge(one_plus_exp_done, 1)
            nc.scalar.activation(ln_one_plus[:, :, :], one_plus_exp[:, :, :], ACT.Ln).then_inc(gate_logs, 1)

            act.wait_ge(mag_sq_done, 1)
            nc.scalar.activation(T["ln_mag_sq"][:, :], T["mag_sq_raw"][:, :], ACT.Ln).then_inc(gate_logs, 1)
            act.wait_ge(phasor_sumsq_done, 1)
            n = act_n[0] = act_n[0] + 1
            nc.scalar.activation(T["ln_sumsq"][:, :], T["phasor_sumsq"][:, :], ACT.Ln).then_inc(act_done, 1)
            act.preload_act_table_set("natural_log_exp_and_others")
            act.wait_ge(ln_mag2_done, 1)
            nc.scalar.activation(T["decay"][:, :], T["ln_mag2"][:, :], ACT.Exp).then_inc(decays_done, 1)
            nc.scalar.activation(T["decay_sq"][:, :], T["ln_mag2"][:, :], ACT.Exp, scale=2.0).then_inc(decays_done, 1)
            act.wait_ge(act_done, n)
            nc.scalar.activation(T["phasor_rroot"][:, :], T["ln_sumsq"][:, :], ACT.Exp, scale=-0.5)\
                .then_inc(decays_done, 1)
            act.wait_ge(vp_arg_done, 1)
            n = act_n[0] = act_n[0] + 1
            nc.scalar.activation(T["ln_vp_arg"][:, :], T["vp_arg"][:, :], ACT.Ln).then_inc(act_done, 1)
            act.wait_ge(act_done, n)
            nc.scalar.activation(T["vp_rroot"][:, :], T["ln_vp_arg"][:, :], ACT.Exp, scale=-0.5)\
                .then_inc(decays_done, 1)
            act.wait_ge(norms_summed, 2)
            nc.scalar.activation(qnorm_rows, SA[0][0:H, :], ACT.Copy).then_inc(norm_copied, 1)
            act.wait_ge(norm_loaded, 32)
            root_of_norm(T["query_rroot"][:, :], T["ln_query"][:, :], T["query_sumsq"][:, :]).then_inc(rq_done, 1)
            act.wait_ge(qnorm_done, 1)
            n = act_n[0] = act_n[0] + 1
            nc.scalar.activation(T["ln_query"][:, :], T["query_norm"][:, :], ACT.Ln).then_inc(act_done, 1)
            act.wait_ge(act_done, n)
            nc.scalar.activation(T["query_recip"][:, :], T["ln_query"][:, :], ACT.Exp, scale=-1.0).then_inc(rq_done, 1)
            root_recip(gn_rstd[:, :], gn_ln[:, :], gn_var_eps[:, :], 0.0, gn_var_done, 1, gn_rstd_done)
            for i in range(2):
                act.wait_ge(gn_bias_done, i + 1)
                for b in range(NB):
                    j = NB * i + b
                    nc.scalar.activation(yn[:, i, S * b:S * (b + 1)], SB[0][:, i, S * b:S * (b + 1)], ACT.Identity,
                                         scale=gn_scale[:, j:j + 1], bias=gn_bias[:, j:j + 1]).then_inc(yn_done, 1)
            root_recip(rstd[:, :], lnv[:, :], mv[:, :, 1], col("eps_ln"), ln_var, 3, ln_rstd)
            act.wait_ge(xnT_done, 3)
            nc.scalar.activation(xn_t[:, :], MI[:, :], ACT.Copy).then_inc(xnT_copied, 1)

        @block.vector
        def _(dve):
            count = [0]
            dve_done = dve_early

            def step(ins):
                count[0] += 1
                ins.then_inc(dve_done, 1)

            def link(ins):
                step(ins)
                dve.wait_ge(dve_done, count[0])

            def sharpen(y, x, tmp):
                dve.wait_ge(dve_done, count[0])
                link(nc.vector.tensor_tensor(tmp, x, y, ALU.mult))
                link(nc.vector.scalar_tensor_tensor(tmp, tmp, -0.5, y, ALU.mult, ALU.mult))
                link(nc.vector.scalar_tensor_tensor(y, tmp, 1.5, y, ALU.add, ALU.mult))

            nc.vector.memset(OT[:, :], 0.0).then_inc(ot_zeroed, 1)
            k0_filler = k_stack[0][:, :, :].rearrange("p h k -> p (h k)").bitcast(F32)
            nc.vector.memset(k0_filler[:, 0:1024], ONES_PAIR).then_inc(kst0_filled, 1)
            dve.wait_ge(s_x, 16)
            for b in range(NB):
                step(nc.vector.bn_stats(stats[:, b, :], x_sb[:, b, :]))
            dve.wait_ge(dve_done, count[0])
            for b in range(NB):
                last = nc.vector.bn_aggr(mv[:, b, :], stats[:, b, :])
                if b < NB - 1:
                    step(last)
            last.then_inc(ln_var, 1)
            dve.wait_ge(dve_done, count[0])
            nc.vector.memset(k0_filler[:, 1024:2048], ONES_PAIR).then_inc(kst0_filled, 1)
            dve.wait_ge(ln_var, 1)
            step(nc.vector.tensor_scalar(var_eps[:, :], mv[:, :, 1], EPS_LN, None, ALU.add))
            dve.wait_ge(ln_rstd, 1)
            sharpen(rstd[:, :], var_eps[:, :], newton[:, :])
            for b in range(NB):
                nc.vector.tensor_scalar(xn[:, b, :], x_sb[:, b, :], mv[:, b, 0:1], rstd[:, b:b + 1],
                                        ALU.subtract, ALU.mult).then_inc(xn_ready, 1)

            nc.vector.memset(k0_filler[:, 2048:4096], ONES_PAIR).then_inc(kst0_filled, 1)

            def split_keys(b):
                dve.wait_ge(k_copied, 2 * b + 2)
                link(nc.vector.tensor_tensor(k_r[:, :], k_f[:, b, :], k_split[:, b, 0, :], ALU.subtract))
                link(nc.vector.tensor_copy(k_split[:, b, 1, :], k_r[:, :]))
                nc.vector.tensor_tensor(k_split[:, b, 2, :], k_r[:, :], k_split[:, b, 1, :], ALU.subtract)\
                    .then_inc(k_split_done, 1)
                dve.wait_ge(k_split_done, b + 1)

            split_keys(0)
            dve.wait_ge(q_copied, 2)
            link(nc.vector.tensor_tensor(q_r[:, :], q_f[:, :], q_split[:, 0, :], ALU.subtract))
            link(nc.vector.tensor_copy(q_split[:, 1, :], q_r[:, :]))
            nc.vector.tensor_tensor(q_split[:, 2, :], q_r[:, :], q_split[:, 1, :], ALU.subtract)\
                .then_inc(q_split_done, 1)
            dve.wait_ge(s_id, 16)
            link(nc.vector.tensor_copy(id_bf[:, :], id_sb[:, :]))
            for j in range(4):
                nc.vector.tensor_scalar(neg_id4[:, j, :], id_sb[:, :], -BIG, None, ALU.mult).then_inc(consts_ready, 1)
            for b in range(1, NB):
                split_keys(b)

            def head_max(n):
                b, h = divmod(n, H)
                dve.wait_ge(score_done, n + 1)
                if h == 0:
                    dve.wait_ge(mask_ready, b + 1)
                if n >= 2:
                    dve.wait_ge(max_done, n - 1)
                nc.vector.tensor_tensor_reduce(junk[:, n % 2, :], SA[n % 2][:, :], mask_neg[:, b, :], 1.0, -3.0e38,
                                               ALU.add, ALU.max, head_maxima[:, b, h:h + 1]).then_inc(max_done, 1)

            def negate_max(b, part=None):
                dve.wait_ge(max_done, H * b + (H if part is None else 8 * part + 8))
                f = slice(0, 2) if part is None else slice(part, part + 1)
                hs = slice(8 * f.start, 8 * f.stop)
                halves = lambda v: v[:, hs].rearrange("p (f h) -> p f h", h=8)
                level = [m_split[:, b, :].rearrange("p (f l h) -> p f l h", f=2, l=3)[:, f, i, :] for i in range(3)]
                link(nc.vector.tensor_scalar(no_key[:, hs], head_maxima[:, b, hs], -0.5 * BIG, 2.0 * BIG, ALU.is_lt,
                                             ALU.mult))
                link(nc.vector.scalar_tensor_tensor(neg_max[:, hs], head_maxima[:, b, hs], -1.0, no_key[:, hs],
                                                    ALU.mult, ALU.subtract))
                link(nc.vector.tensor_copy(level[0], halves(neg_max)))
                link(nc.vector.tensor_tensor(halves(neg_max_rest), halves(neg_max), level[0], ALU.subtract))
                link(nc.vector.tensor_copy(level[1], halves(neg_max_rest)))
                nc.vector.tensor_tensor(level[2], halves(neg_max_rest), level[1], ALU.subtract)\
                    .then_inc(neg_max_done, 1)
                dve.wait_ge(neg_max_done, b + 2 if b else part + 1)

            def normalise(b):
                dve.wait_ge(oT_done, b + 1)
                o_v = MI[:, :].rearrange("p (h e) -> p h e", h=H)
                link(nc.vector.reciprocal(rden[:, :].rearrange("p (h e) -> p h e", e=1), o_v[:, :, DH:DH + 1]))
                link(nc.vector.tensor_tensor(attn[:, b % 2, :].rearrange("p (h d) -> p h d", h=H), o_v[:, :, 0:DH],
                                             rden[:, :].rearrange("p (h e) -> p h e", e=1).to_broadcast([P, H, DH]),
                                             ALU.mult))
                nc.vector.tensor_tensor(attn[:, b % 2, :], attn[:, b % 2, :], rows_sb[:, 0, :], ALU.add)\
                    .then_inc(attn_done, 1)

            def residual(b):
                dve.wait_ge(wo_done, b + 1)
                dve.wait_ge(xb_done, NB)
                nc.vector.tensor_tensor(x1[:, b, :], MI[:, 0:DM], xb[:, b, :], ALU.add).then_inc(x1_done, 1)

            for h in range(PRE - 1):
                head_max(h)
            dve.wait_ge(sum_done, 1)
            nc.vector.tensor_scalar(some_open[:, :], mask_sum[:, :], float(ALL_MASKED), None, ALU.is_lt)\
                .then_inc(open_done, 1)
            head_max(PRE - 1)
            negate_max(0, 0)
            dve.wait_ge(count_done, 1)
            nc.vector.tensor_copy(go_general[:, :], OT[0:1, 0:1]).then_inc(flag_done, 1)
            dve.wait_ge(s_rows, 16)
            dve.wait_ge(flag_done, 1)
            V = nc.vector

            def general_block(n):
                dve.wait_ge(g_merged, n + 1)
                dve.wait_ge(g_kcopied, 2 * n + 2)
                g_n = n * 15
                V.tensor_tensor(k_r[:, :], k_f[:, 0, :], k_split[:, 0, 0, :], ALU.subtract).then_inc(g_step, 1)
                dve.wait_ge(g_step, g_n + 1)
                V.tensor_copy(k_split[:, 0, 1, :], k_r[:, :]).then_inc(g_step, 1)
                dve.wait_ge(g_step, g_n + 2)
                V.tensor_tensor(k_split[:, 0, 2, :], k_r[:, :], k_split[:, 0, 1, :], ALU.subtract).then_inc(g_ksplit, 1)
                dve.wait_ge(g_vproj, n + 1)
                V.tensor_tensor(v_ones[:, 0, :, :, 0:DH], MI[:, :].rearrange("p (t h d) -> p t h d", t=KT, h=H),
                                rows_sb[:, 0, :].rearrange("p (o h d) -> p o h d", o=1,
                                                           h=H).to_broadcast([P, KT, H, DH]),
                                ALU.add).then_inc(g_vcopied, 1)
                dve.wait_ge(g_mask, 16 * n + 16)
                V.tensor_scalar(mask_neg[:, 0, :], mask_sb[:, 0, 0:BLK], -BIG, None, ALU.mult).then_inc(g_step, 1)
                V.tensor_scalar(mask_bf[:, 0, :], mask_sb[:, 0, 0:BLK], 1.0, None, ALU.mult).then_inc(g_maskset, 1)
                dve.wait_ge(g_step, g_n + 3)
                for h in range(H):
                    dve.wait_ge(score_done, n * H + (PRE + h + 1))
                    if h >= 2:
                        dve.wait_ge(max_done, n * H + (PRE + h - 1))
                    masked = probs_flat[:, BLK * (h % 2):BLK * (h % 2) + BLK]
                    V.tensor_tensor(masked, SA[h % 2][:, :], mask_neg[:, 0, :], ALU.add).then_inc(g_masked, 1)
                    dve.wait_ge(g_masked, n * H + h + 1)
                    V.tensor_reduce(m_blk[:, h:h + 1], masked, AX.X, ALU.max).then_inc(max_done, 1)
                dve.wait_ge(max_done, n * H + (H + PRE))
                V.tensor_tensor(m_new[:, :], m_blk[:, :], m_run[:, :], ALU.max).then_inc(g_step, 1)
                dve.wait_ge(g_step, g_n + 4)
                V.tensor_tensor(fade_arg[:, :], m_run[:, :], m_new[:, :], ALU.subtract).then_inc(g_fade_arg, 1)
                dve.wait_ge(g_fade_arg, n + 1)
                V.tensor_copy(m_run[:, :], m_new[:, :]).then_inc(g_step, 1)
                V.tensor_scalar(no_key[:, :], m_new[:, :], -0.5 * BIG, 2.0 * BIG, ALU.is_lt, ALU.mult)\
                    .then_inc(g_step, 1)
                dve.wait_ge(g_step, g_n + 6)
                V.scalar_tensor_tensor(neg_max[:, :], m_new[:, :], -1.0, no_key[:, :], ALU.mult, ALU.subtract)\
                    .then_inc(g_step, 1)
                dve.wait_ge(g_step, g_n + 7)
                V.tensor_copy(m_split[:, 0, 0:H], neg_max[:, :]).then_inc(g_step, 1)
                dve.wait_ge(g_step, g_n + 8)
                V.tensor_tensor(neg_max_rest[:, :], neg_max[:, :], m_split[:, 0, 0:H], ALU.subtract).then_inc(g_step, 1)
                dve.wait_ge(g_step, g_n + 9)
                V.tensor_copy(m_split[:, 0, H:2 * H], neg_max_rest[:, :]).then_inc(g_step, 1)
                dve.wait_ge(g_step, g_n + 10)
                V.tensor_tensor(m_split[:, 0, 2 * H:3 * H], neg_max_rest[:, :], m_split[:, 0, H:2 * H], ALU.subtract)\
                    .then_inc(neg_max_done, 1)
                dve.wait_ge(g_fade, n + 1)
                V.tensor_tensor(o_run[:, :, :], o_run[:, :, :], fade[:, :].rearrange("p (h e) -> p h e", e=1)
                                .to_broadcast([P, H, DH + 1]), ALU.mult).then_inc(g_step, 1)
                dve.wait_ge(g_step, g_n + 11)
                dve.wait_ge(oT_done, n + 1)
                V.tensor_tensor(o_run[:, :, :], o_run[:, :, :], MI[:, :].rearrange("p (h e) -> p h e",
                                                                                   h=H)[:, :, 0:DH + 1],
                                ALU.add).then_inc(g_step, 4)
                dve.wait_ge(g_step, g_n + 15)
                V.tensor_copy(m_blk[:, :], m_new[:, :]).then_inc(g_merged, 1)

            with dve.If(dve.value_load(go_general[0:1, 0:1]) != 0):
                dve.wait_ge(q_stacked, 16 * (NTERM // 2))
                dve.wait_ge(q_stacked_lo, 16 * (NTERM // 2))
                dve.wait_ge(k_stacked[1], 16 * NTERM)
                dve.wait_ge(k_stacked[2], 16 * NTERM)
                dve.wait_ge(mask_ready, NB)
                dve.wait_ge(xb_done, NB)
                V.memset(m_blk[:, :], 0.0).then_inc(g_merged, 1)
                V.memset(m_run[:, :], -3.0e38).then_inc(g_q, 1)
                V.memset(o_run[:, :, :], 0.0).then_inc(g_q, 1)
                with dve.Fori(0, NB) as b:
                    V.tensor_copy(q_cur, q_stack[:, :, bass.ds(b * S, S)]).then_inc(g_q, 1)
                    V.tensor_copy(q_raw, q_stack[:, :, bass.ds(b * S, S)]).then_inc(g_q, 1)
                    with dve.Fori(0, NBLK) as k:
                        dve.wait_ge(g_q, 4 * b + 4)
                        general_block(b * NBLK + k)
                    dve.wait_ge(g_merged, b * NBLK + NBLK + 1)
                    V.reciprocal(rden[:, :].rearrange("p (h e) -> p h e", e=1), o_run[:, :, DH:DH + 1])\
                        .then_inc(attn_done, 1)
                    dve.wait_ge(attn_done, 2 * b + 1)
                    V.tensor_tensor(attn[:, 0, :].rearrange("p (h d) -> p h d", h=H), o_run[:, :, 0:DH],
                                    rden[:, :].rearrange("p (h e) -> p h e", e=1).to_broadcast([P, H, DH]),
                                    ALU.mult).then_inc(attn_done, 1)
                    dve.wait_ge(wo_done, b + 1)
                    V.tensor_tensor(x1[:, bass.ds(b, 1), :].rearrange("p o d -> p (o d)"), MI[:, 0:DM],
                                    xb[:, bass.ds(b, 1), :].rearrange("p o d -> p (o d)"), ALU.add).then_inc(x1_done, 1)
                    dve.wait_ge(x1_done, b + 1)
                    V.memset(m_run[:, :], -3.0e38).then_inc(g_q, 1)
                    V.memset(o_run[:, :, :], 0.0).then_inc(g_q, 1)
            with dve.Else():
                for b in range(NB):
                    for u in range(8):
                        if b == 0 and u == 0:
                            for h in range(PRE, FIRST):
                                head_max(h)
                        for h in heads_of_unit(8 * b + u):
                            head_max(h)
                        if b == 0 and u == 0:
                            negate_max(0, 1)
                        if u == 1 and b >= 1:
                            normalise(b - 1)
                        if u == 3 and b >= 1:
                            residual(b - 1)
                        if b + 1 < NB and u == 4:
                            negate_max(b + 1)
                normalise(NB - 1)
                residual(NB - 1)

            dve.nop()
            count[0] = 0
            dve_done = dve_post

            def need(n):
                dve.wait_ge(dve_done, n)

            def run(ins):
                step(ins)
                return count[0]

            def moments(nth):
                for b in range(NB):
                    a = run(V.bn_stats(stats[:, b, :], x_src[:, b, :]))
                need(a)
                for b in range(NB):
                    a = V.bn_aggr(mv[:, b, :], stats[:, b, :])
                    if b < NB - 1:
                        step(a)
                a.then_inc(ln_var, 1)
                dve.wait_ge(ln_var, nth)

            dve.wait_ge(x1_done, NB)
            x_src = x1
            moments(2)
            run(V.tensor_scalar(var_both[:, :], mv[:, :, 1], 1.0 + EPS_RMS, EPS_LN * EPS_RMS, ALU.mult, ALU.add))
            run(V.tensor_scalar(var_eps[:, :], mv[:, :, 1], EPS_LN, None, ALU.add))
            dve.wait_ge(rms_done, 1)
            sharpen(rstd_both[:, :], var_both[:, :], newton[:, :])
            for b in range(NB):
                V.tensor_scalar(xr[:, b, :], x1[:, b, :], mv[:, b, 0:1], rstd_both[:, b:b + 1], ALU.subtract, ALU.mult)\
                    .then_inc(xn_ready, 1)
            dve.wait_ge(ln_rstd, 2)
            sharpen(rstd[:, :], var_eps[:, :], newton[:, :])
            for b in range(NB):
                V.tensor_scalar(x1_norm[:, b, :], x1[:, b, :], mv[:, b, 0:1], rstd[:, b:b + 1], ALU.subtract, ALU.mult)\
                    .then_inc(x1_norm_done, 1)
            dve.wait_ge(late_weights_loaded, 16 * LATE_LOADS)
            V.tensor_reduce(w_row_max[:, :], ffn_w_sb[:, :], AX.X, ALU.max, apply_absolute_value=True)\
                .then_inc(w_row_max_done, 1)

            dve.wait_ge(xg_copied, 1)
            for i in range(2):
                dve.wait_ge(xg_copied, i + 1)
                acc = conv[:, i, :].rearrange("p (b t) -> p b t", b=NB)
                link(V.tensor_scalar(acc, conv_in[:, i, :, 0:S], col(f"cw{i}0"), col(f"cb{i}"), ALU.mult, ALU.add))
                for j in range(1, 4):
                    last = V.scalar_tensor_tensor(acc, conv_in[:, i, :, j:j + S], col(f"cw{i}{j}"), acc, ALU.mult,
                                                  ALU.add)
                    if j < 3:
                        link(last)
                last.then_inc(conv_done, 1)
            for i in range(2):
                dve.wait_ge(sigc_done, i + 1)
                V.tensor_tensor(x_conv[:, i, :], conv[:, i, :], sigc[:, i, :], ALU.mult).then_inc(xc_done, 1)
            for i in range(2):
                dve.wait_ge(sigz_done, i + 1)
                run(V.scalar_tensor_tensor(z_silu[:, i, :], (SA[1], OT)[i][:, :], col(f"z_b{i}"), sigz[:, i, :],
                                           ALU.add, ALU.mult))
            dve.wait_ge(w_max_done, 1)
            link(V.tensor_scalar(int4_scale[:, :], w_max[:, :], 1.0 / 7.0, None, ALU.mult))
            link(V.reciprocal(int4_scale_recip[:, :], int4_scale[:, :]))
            link(V.tensor_scalar(w_int4[:, :], ffn_w_sb[:, :], int4_scale_recip[:, 0:1], None, ALU.mult))
            link(V.tensor_scalar(w_int4[:, :], w_int4[:, :], ROUND, -ROUND, ALU.add, ALU.add))
            link(V.tensor_scalar(w_int4[:, :], w_int4[:, :], -8.0, 7.0, ALU.max, ALU.min))
            dve.wait_ge(lowrank_done, 1)
            run(V.scalar_tensor_tensor(w_eff[:, :], w_int4[:, :], int4_scale[:, 0:1], SB[1][:, 1, 0:DM], ALU.mult,
                                       ALU.add))

            t = lambda n: T[n][:, :]

            def tt(o, x0, x1_, op):
                return run(V.tensor_tensor(o, x0, x1_, op))

            dve.wait_ge(k_loaded, 32)
            need(count[0])
            gram_products_first = spare[:, 0:HD * NC * 3].rearrange("p (d c j) -> p d c j", d=HD, j=3)
            gram_of = gram.rearrange("p (g c j) -> p g c j", g=2, j=3)
            coupling_of = dcoef.rearrange("p (g c j) -> p g c j", g=2, j=3)
            a = run(V.tensor_tensor(gram_products_first, key_chunks[:, :, :, 1:4],
                                    key_chunks[:, :, :, 0:1].to_broadcast([P, HD, NC, 3]), ALU.mult))
            need(a)
            for g, products in enumerate((gram_products_first, gram_products_late)):
                if g == 1:
                    dve.wait_ge(gram_products, 2)
                run(V.tensor_reduce(gram_of[:, g, :, :].rearrange("p c j -> p (c j)"),
                                    products.rearrange("p d c j -> p (c j) d"), AX.X, ALU.add))

            dve.wait_ge(gate_exps, 2)
            V.tensor_scalar(one_plus_exp[:, :, :], exp_neg_abs[:, :, :], 1.0, None, ALU.add)\
                .then_inc(one_plus_exp_done, 1)
            dve.wait_ge(one_plus_exp_done, 1)
            a = run(V.scalar_tensor_tensor(corr[:, :, :], one_plus_exp[:, :, :], -1.0, exp_neg_abs[:, :, :], ALU.add,
                                           ALU.subtract))
            need(a)
            a = run(V.scalar_tensor_tensor(corr[:, :, :], gate_ch[:, 0:5:4, :], 0.0, corr[:, :, :], ALU.max,
                                           ALU.subtract))
            need(a)
            dve.wait_ge(knorm_loaded, 32)
            dve.wait_ge(kroot_done, 1)
            sharpen(t("key_rroot"), t("key_sumsq"), t("t2"))
            link(V.tensor_tensor(t("t2"), t("key_sumsq"), t("key_rroot"), ALU.mult))
            link(V.tensor_scalar(t("t2"), t("t2"), 1.0e-6, None, ALU.add))
            run(V.reciprocal(t("key_recip"), t("t2")))
            dve.wait_ge(gate_logs, 1)
            a = tt(softplus[:, :, :], ln_one_plus[:, :, :], corr[:, :, :], ALU.add)
            need(a)
            a = run(V.tensor_scalar(t("dt"), softplus[:, 1, :], exp_log_dt[:, 0:1], 1.0e-4, ALU.mult, ALU.add))
            need(a)
            dve.wait_ge(gates_sigmoid, 3)
            run(V.scalar_tensor_tensor(t("half_alpha_dt"), t("dt"), 0.5, softplus[:, 0, :], ALU.mult, ALU.mult))
            a = run(V.scalar_tensor_tensor(t("half_omega_dt"), sig_om[:, :], col("freq"), t("dt"), ALU.mult, ALU.mult))
            need(a)
            tt(t("a_sq"), t("half_alpha_dt"), t("half_alpha_dt"), ALU.mult)
            a = tt(t("w_sq"), t("half_omega_dt"), t("half_omega_dt"), ALU.mult)
            need(a)
            a = tt(t("t1"), t("a_sq"), t("w_sq"), ALU.add)
            need(a)
            run(V.tensor_scalar(t("one_plus_sq"), t("t1"), 1.0, None, ALU.add))
            a = run(V.tensor_scalar(t("c_numer"), t("t1"), -1.0, 1.0, ALU.mult, ALU.add))
            need(a)
            run(V.scalar_tensor_tensor(t("det"), t("half_alpha_dt"), 2.0, t("one_plus_sq"), ALU.mult, ALU.add))
            run(V.scalar_tensor_tensor(t("det_mirror"), t("half_alpha_dt"), -2.0, t("one_plus_sq"), ALU.mult, ALU.add))
            a = tt(t("c_numer_sq"), t("c_numer"), t("c_numer"), ALU.mult)
            need(a)
            a = run(V.reciprocal(t("det_recip"), t("det")))
            b_ = run(V.scalar_tensor_tensor(t("t2"), t("w_sq"), 4.0, t("c_numer_sq"), ALU.mult, ALU.add))
            need(a)
            a = tt(t("t3"), t("det_mirror"), t("det_recip"), ALU.mult)
            need(b_)
            b_ = run(V.tensor_scalar(t("is_zero"), t("t2"), 0.0, None, ALU.is_equal))
            need(a)
            V.tensor_scalar(t("mag_sq_raw"), t("t3"), 1.0e-16, 1.0, ALU.max, ALU.min).then_inc(mag_sq_done, 1)
            need(b_)
            V.tensor_tensor(t("phasor_sumsq"), t("t2"), t("is_zero"), ALU.add).then_inc(phasor_sumsq_done, 1)
            a = tt(t("t4"), t("c_numer"), t("is_zero"), ALU.add)
            dve.wait_ge(gate_logs, 2)
            V.scalar_tensor_tensor(t("ln_mag2"), t("ln_mag_sq"), 4.0, sig_br[:, 1, :], ALU.mult, ALU.mult)\
                .then_inc(ln_mag2_done, 1)
            dve.wait_ge(decays_done, 3)
            dve.wait_ge(phasor_sumsq_done, 1)
            a = tt(t("t5"), t("phasor_rroot"), t("phasor_rroot"), ALU.mult)
            need(a)
            a = tt(t("t6"), t("t5"), t("phasor_sumsq"), ALU.mult)
            need(a)
            a = run(V.tensor_scalar(t("t7"), t("t6"), -0.5, 1.5, ALU.mult, ALU.add))
            need(a)
            a = tt(t("t8"), t("phasor_rroot"), t("t7"), ALU.mult)
            need(a)
            V.tensor_tensor(phasor[0][:, 0, :], t("t4"), t("t8"), ALU.mult).then_inc(phasors_done, 1)
            V.scalar_tensor_tensor(phasor[0][:, 1, :], t("half_omega_dt"), 2.0, t("t8"), ALU.mult, ALU.mult)\
                .then_inc(phasors_done, 1)
            dve.wait_ge(decays_done, 3)
            mc = t("decay").rearrange("p (c j) -> p c j", j=C)
            ctc = t("coupling").rearrange("p (c j) -> p c j", j=C)
            a = run(V.tensor_scalar(t("t1"), t("decay_sq"), -1.0, 1.0, ALU.mult, ALU.add))
            b_ = run(V.tensor_tensor(m_pair, mc[:, :, 0:3], mc[:, :, 1:4], ALU.mult))
            need(a)
            V.tensor_scalar(t("vp_arg"), t("t1"), 0.0, 1.0e-6, ALU.max, ALU.add).then_inc(vp_arg_done, 1)
            need(b_)
            V.tensor_tensor(m_three, m_pair[:, :, 0:2], mc[:, :, 2:4], ALU.mult).then_inc(fades_done, 1)
            V.tensor_tensor(coef_c[:, :, 0:1], m_pair[:, :, 0:1], m_pair[:, :, 2:3], ALU.mult).then_inc(fades_done, 1)
            a = tt(t("beta_recip"), sig_br[:, 0, :], t("key_recip"), ALU.mult)
            need(a)
            a = run(V.scalar_tensor_tensor(t("t3"), t("beta_recip"), -1.0, t("decay"), ALU.mult, ALU.mult))
            need(a)
            a = tt(t("coupling"), t("t3"), t("key_recip"), ALU.mult)
            need(a)
            dve.wait_ge(fades_done, 2)
            run(V.tensor_copy(bcoef[:, :, 0:1], ctc[:, :, 0:1]))
            run(V.tensor_tensor(bcoef[:, :, 1:2], ctc[:, :, 1:2], mc[:, :, 0:1], ALU.mult))
            run(V.tensor_tensor(bcoef[:, :, 2:3], ctc[:, :, 2:3], m_pair[:, :, 0:1], ALU.mult))
            a = run(V.tensor_tensor(bcoef[:, :, 3:4], ctc[:, :, 3:4], m_three[:, :, 0:1], ALU.mult))
            run(V.tensor_tensor(coupling_of[:, 0, :, :], gram_of[:, 0, :, :], ctc[:, :, 1:4], ALU.mult))
            run(V.tensor_tensor(coupling_of[:, 1, :, 0:2], gram_of[:, 1, :, 0:2], ctc[:, :, 2:4], ALU.mult))
            b_ = run(V.tensor_tensor(coupling_of[:, 1, :, 2:3], gram_of[:, 1, :, 2:3], ctc[:, :, 3:4], ALU.mult))
            need(a)
            wide = lambda v, rows, n: v.rearrange("p c j -> p (c j)").rearrange("p (o x) -> p o x", o=1)\
                .to_broadcast([P, rows, NC * n])
            a = run(V.tensor_tensor(kap_t[:, 0:HD, :], by_t(k_ch), wide(bcoef, HD, C), ALU.mult))
            need(b_)
            run(V.tensor_tensor(coupling_of[:, 0, :, 1:2], coupling_of[:, 0, :, 1:2], mc[:, :, 1:2], ALU.mult))
            run(V.tensor_tensor(coupling_of[:, 0, :, 2:3], coupling_of[:, 0, :, 2:3], m_pair[:, :, 1:2], ALU.mult))
            run(V.tensor_tensor(coupling_of[:, 1, :, 1:2], coupling_of[:, 1, :, 1:2], mc[:, :, 2:3], ALU.mult))
            need(count[0])

            def eliminate(lo, hi):
                rows_ = hi - lo
                for i in range(C - 1):
                    n = C - 1 - i
                    weight = coupling_of[:, min(i, 1), :, 0:n] if i < 2 else coupling_of[:, 1, :, 2:3]
                    tmp = pair_tmp[:, 0:rows_ * NC * n].rearrange("p (d c j) -> p d c j", d=rows_, j=n)
                    for j in range(n):
                        run(V.tensor_tensor(tmp[:, :, :, j], kap_c[:, lo:hi, :, i],
                                            weight[:, :, j:j + 1].rearrange("p c o -> p o c").to_broadcast([P, rows_, NC]),
                                            ALU.mult))
                    need(count[0])
                    run(V.tensor_tensor(kap_c[:, lo:hi, :, i + 1:C], kap_c[:, lo:hi, :, i + 1:C], tmp, ALU.add))
                    need(count[0])

            eliminate(0, HD)
            cosp, sinp = phasor[1][:, 0, :], phasor[1][:, 1, :]
            dve.wait_ge(v_loaded, 64)
            dve.wait_ge(decays_done, 4)
            dve.wait_ge(vp_arg_done, 1)
            sharpen(t("vp_rroot"), t("vp_arg"), t("t2"))
            link(V.tensor_tensor(t("t2"), t("vp_rroot"), t("vp_arg"), ALU.mult))
            a = tt(t("vp_scale"), sig_bc[:, 0, :], t("t2"), ALU.mult)
            need(a)
            tt(t("t4"), t("beta_recip"), t("vp_scale"), ALU.mult)
            dve.wait_ge(prefix_done, 1)
            run(V.tensor_tensor(t("v_cos"), v_own[:, :], cosp, ALU.mult))
            a = run(V.scalar_tensor_tensor(t("v_sin"), v_swap[:, :], col("sgn"), sinp, ALU.mult, ALU.mult))
            need(a)
            a = tt(t("v_turned"), t("v_cos"), t("v_sin"), ALU.add)
            need(a)
            run(V.tensor_tensor(kap_t[:, HD, :], t("v_turned"), t("t4"), ALU.mult))
            need(count[0])
            eliminate(HD, HD + 1)
            dve.wait_ge(bank_set, 6)
            group_ends = [c0 + n for c0, n in POOL_CHUNKS]
            for c in range(NC):
                need(count[0])
                for j in range(C):
                    run(V.tensor_tensor_reduce(dot_junk[:, j, :], bank[:, :, SLOT * c], kap_t[:, :, C * c + j], 1.0,
                                               0.0,
                                               ALU.mult, ALU.add, coef[:, SLOT * c + 1 + j:SLOT * c + 2 + j]))
                need(count[0])
                if c == FIRST_CHUNKS:
                    dve.wait_ge(bank_set, 9)
                run(V.tensor_tensor(terms[:, :, :], bank[:, 0:HD, SLOT * c:SLOT * (c + 1)],
                                    coef[:, SLOT * c:SLOT * (c + 1)].rearrange("p (o j) -> p o j", o=1)
                                    .to_broadcast([P, HD, SLOT]), ALU.mult))
                need(count[0])
                last = V.tensor_reduce(bank[:, 0:HD, SLOT * (c + 1)], terms[:, :, :], AX.X, ALU.add)
                if c + 1 in group_ends:
                    last.then_inc(chunks_done, 1)
                    dve.wait_ge(chunks_done, 1 + group_ends.index(c + 1))
                else:
                    run(last)
            dve.wait_ge(q_loaded, 32)
            need(count[0])
            retrieve(V, run, lambda: need(count[0]), NC - DVE_CHUNKS, DVE_CHUNKS)
            need(count[0])
            dve.wait_ge(pool_retrieved, 1)
            a = run(V.tensor_reduce(t("retrieved"), inner.rearrange("p (d t) -> p t d", d=HD), AX.X, ALU.add))
            dve.wait_ge(turn_done, 2)
            need(a)
            V.tensor_tensor(t("cos_part"), t("retrieved"), t("turn_cos"), ALU.mult).then_inc(parts_done, 1)
            V.tensor_tensor(t("sin_part"), t("retrieved"), t("turn_sin"), ALU.mult).then_inc(parts_done, 1)
            for i in range(2):
                dve.wait_ge(y_done, i + 1)
                for b in range(NB):
                    a = run(V.bn_stats(gn_stats[:, NB * i + b, :], SB[0][:, i, S * b:S * (b + 1)]))
            need(a)
            for j in range(8):
                V.bn_aggr(gn_mv[:, j, :], gn_stats[:, j, :]).then_inc(gn_stats_done, 1)
            dve.wait_ge(gn_mean_done, 1)
            a = run(V.tensor_copy(gn_mean[:, :], MI[:, 0:8]))
            need(a)
            a = run(V.tensor_tensor(gn_delta[:, :], gn_mv[:, :, 0], gn_mean[:, :], ALU.subtract))
            need(a)
            a = run(V.tensor_tensor(gn_delta[:, :], gn_delta[:, :], gn_delta[:, :], ALU.mult))
            need(a)
            V.tensor_tensor(gn_spread[:, :], gn_delta[:, :], gn_mv[:, :, 1], ALU.add).then_inc(gn_spread_done, 1)
            dve.wait_ge(gn_var_averaged, 1)
            V.tensor_scalar(gn_var_eps[:, :], MI[:, 8:16], EPS_LN, None, ALU.add).then_inc(gn_var_done, 1)
            dve.wait_ge(gn_var_done, 1)
            dve.wait_ge(gn_rstd_done, 1)
            sharpen(gn_rstd[:, :], gn_var_eps[:, :], newton8[:, :])
            for i in range(2):
                a = run(V.tensor_scalar(gn_scale[:, NB * i:NB * (i + 1)], gn_rstd[:, NB * i:NB * (i + 1)],
                                        col(f"gn_w{i}"), None, ALU.mult))
            need(a)
            a = run(V.tensor_tensor(gn_delta[:, :], gn_mean[:, :], gn_scale[:, :], ALU.mult))
            need(a)
            for i in range(2):
                V.tensor_scalar(gn_bias[:, NB * i:NB * (i + 1)], gn_delta[:, NB * i:NB * (i + 1)], -1.0,
                                col(f"gn_b{i}"),
                                ALU.mult, ALU.add).then_inc(gn_bias_done, 1)
            for i in range(2):
                dve.wait_ge(yn_done, NB * (i + 1))
                a = run(V.tensor_tensor(yn[:, i, :], yn[:, i, :], z_silu[:, i, :], ALU.mult))
                need(a)
                V.scalar_tensor_tensor(y2[:, i, :], x_conv[:, i, :], col(f"d{i}"), yn[:, i, :], ALU.mult, ALU.add)\
                    .then_inc(y2_done, 1)
            dve.wait_ge(layer_projected, 1)
            dve.wait_ge(x1_plus_norm_done, 1)
            V.tensor_tensor(x2[:, :, :], SB[1][:, 0, :].rearrange("p (b d) -> p b d", b=NB), x1_plus_norm[:, :, :],
                            ALU.add)\
                .then_inc(x2_done, 1)
            dve.wait_ge(x2_done, 1)
            x_src = x2
            moments(3)
            a = run(V.tensor_tensor(res[:, :, :], x2[:, :, :],
                                    rows_sb[:, 2:3, :].to_broadcast([P, NB, DM]), ALU.add))
            run(V.tensor_scalar(var_eps[:, :], mv[:, :, 1], EPS_LN, None, ALU.add))
            dve.wait_ge(ln_rstd, 3)
            sharpen(rstd[:, :], var_eps[:, :], newton[:, :])
            need(count[0])
            for b in range(NB):
                V.tensor_scalar(xn[:, b, :], x2[:, b, :], mv[:, b, 0:1], rstd[:, b:b + 1], ALU.subtract, ALU.mult)\
                    .then_inc(xn_ready, 1)
            dve.wait_ge(ffn_done, 1)
            V.tensor_tensor(res[:, :, :], res[:, :, :], SA[0][:, :].rearrange("p (b d) -> p b d", b=NB), ALU.add)\
                .then_inc(res_done, 1)

        @block.tensor
        def _(pe):
            def k_project(b):
                pe.wait_ge(s_ctx[min(b, 1)], 16)
                nc.tensor.matmul(SB[b // 2][:, b % 2, :], wk_sb[:, :], ctx_sb[:, b, :], start=True, stop=True)\
                    .then_inc(k_done, 1)

            def v_project(b, dst):
                for t in range(KT):
                    last = nc.tensor.matmul(dst[:, P * t:P * (t + 1)], ctx_sb[:, b, P * t:P * (t + 1)], wv_sb[:, :],
                                            start=True, stop=True)
                last.then_inc(v_done, 1)

            pe.wait_ge(s_wk, 16)
            k_project(0)
            pe.wait_ge(s_id, 16)
            for b in range(NB):
                pe.wait_ge(xn_ready, b + 1)
                last = nc.tensor.transpose(MI[:, P * b:P * (b + 1)], xn[:, b, :], id_sb[:, :])
            last.then_inc(xnT_done, 1)
            pe.wait_ge(s_wq, 16)
            pe.wait_ge(xnT_copied, 1)
            nc.tensor.matmul(SA[0][:, :], wq_sb[:, :], xn_t[:, :], start=True, stop=True).then_inc(q_done, 1)
            k_project(1)
            k_project(2)
            k_project(3)
            pe.wait_ge(s_wv, 16)
            for b in range(NB):
                pe.wait_ge(k_copied, 2 * b + 2)
                v_project(b, SB[b // 2][:, b % 2, :])

            def score(n):
                b, h = divmod(n, H)
                if h == 0:
                    pe.wait_ge(k_stacked[b], 16 * NTERM)
                if n == 0:
                    pe.wait_ge(q_stacked, 16 * (NTERM // 2))
                    pe.wait_ge(q_stacked_lo, 16 * (NTERM // 2))
                if n >= 2:
                    pe.wait_ge(max_done, n - 1)
                nc.tensor.matmul(SA[n % 2][:, :], q_stack[:, h, S * b:S * (b + 1)], k_stack[b][:, h, :],
                                 start=True, stop=True).then_inc(score_done, 1)

            def turn_max(b, part=None):
                pe.wait_ge(neg_max_done, b + 2 if b else part + 1)
                if b >= 2:
                    pe.wait_ge(x1_done, b - 1)
                if b == 0:
                    pe.wait_ge(xnT_copied, 1)
                if b == 0 and part == 1:
                    pe.wait_ge(mT_copied, 1)
                columns = slice(0, 3 * H) if b else slice(24 * part, 24 * part + 24)
                rows_ = 3 * H if b else 24
                nc.tensor.transpose(MI[0:rows_, 0:S // 2].bitcast(BF16), m_split[:, b, columns], id_bf[:, :])\
                    .then_inc(mT_done, 1)

            def unit(n, todo):
                b, u = divmod(n, 8)
                half, t = divmod(u, KT)
                if n < 8 * NB:
                    if n < 2:
                        pe.wait_ge(v_copied, 2 * n + 2)
                    if u == 0:
                        pe.wait_ge(m_stacked, 16 * b + 16)
                        pe.wait_ge(mask_ready, b + 1)
                        pe.wait_ge(consts_ready, 4)
                    if u == KT:
                        pe.wait_ge(m_stacked_hi, 16 * b + 16)
                    if n >= 2:
                        pe.wait_ge(unit_exp, n - 1)
                    for g in range(2):
                        for j in range(4):
                            h = 8 * half + 4 * g + j
                            nc.tensor.matmul(SB[n % 2][:, g, S * j:S * (j + 1)], k_stack[b][:, h, P * t:P * (t + 1)],
                                             q_stack[:, h, S * b:S * (b + 1)], start=(j == 0), stop=False,
                                             skip_group_check=True)
                        last = nc.tensor.matmul(SB[n % 2][:, g, :], mask_bf[:, b, P * t:P * (t + 1)],
                                                neg_id4[:, :, :].rearrange("p a s -> p (a s)"), start=False, stop=True,
                                                skip_group_check=True)
                        if g == 0 and u > 0 and todo:
                            score(todo[0])
                    last.then_inc(unit_scored, 1)
                if n >= 1:
                    b, u = divmod(n - 1, 8)
                    half, t = divmod(u, KT)
                    pe.wait_ge(unit_exp, n)
                    if u == 0:
                        if b == 0:
                            pe.wait_ge(ot_zeroed, 1)
                        else:
                            pe.wait_ge(o_copied, b)
                    for i in range(8):
                        h = 8 * half + i
                        g, j = divmod(h, 4)
                        last = nc.tensor.matmul(OT[32 * j:32 * j + DH + 1, S * g:S * (g + 1)], v_ones[:, b, t, h, :],
                                                probs[:, (n - 1) % 3, i, :], start=(t == 0 and g == 0),
                                                stop=(t == KT - 1), skip_group_check=True)
                        if i == 3 and n % 8 and len(todo) > 2:
                            score(todo[1])
                    last.then_inc(unit_pv, 1)
                for h in todo[0 if n % 8 == 0 else 1 + (len(todo) > 2):]:
                    score(h)

            def turn_out(b):
                pe.wait_ge(o_copied, b + 1)
                if b >= 1:
                    pe.wait_ge(x1_done, b)
                pe.wait_ge(mT_copied, b + 2)
                for g in range(4):
                    last = nc.tensor.transpose(MI[:, S * g:S * (g + 1)], o_sb[:, b % 2, S * g:S * (g + 1)], id_sb[:, :])
                last.then_inc(oT_done, 1)

            def turn_attn(b):
                pe.wait_ge(attn_done, b + 1)
                nc.tensor.transpose(MI[:, 0:S], attn[:, b % 2, :], id_sb[:, :]).then_inc(aT_done, 1)

            def project_out(b):
                pe.wait_ge(aT_copied, b + 1)
                pe.wait_ge(s_wo, 16)
                nc.tensor.matmul(MI[:, 0:DM], attn_t[:, b % 2, :], wo_sb[:, :], start=True, stop=True)\
                    .then_inc(wo_done, 1)

            MM = nc.tensor.matmul
            for h in range(PRE):
                score(h)
            pe.wait_ge(ot_zeroed, 1)
            pe.wait_ge(open_done, 1)
            MM(OT[0:1, 0:1], some_open[:, :], col("one"), start=True, stop=True).then_inc(count_done, 1)
            turn_max(0, 0)

            def general_block(n):
                pe.wait_ge(g_ctx, 16 * n + 16)
                MM(SB[0][:, 0, :], wk_sb[:, :], ctx_sb[:, 0, :], start=True, stop=True).then_inc(g_kproj, 1)
                for t in range(KT):
                    last = MM(MI[:, P * t:P * (t + 1)], ctx_sb[:, 0, P * t:P * (t + 1)], wv_sb[:, :], start=True,
                              stop=True)
                last.then_inc(g_vproj, 1)
                pe.wait_ge(g_kstacked, n * (16 * NTERM) + 16 * NTERM)
                for h in range(H):
                    if h >= 2:
                        pe.wait_ge(max_done, n * H + (PRE + h - 1))
                    MM(SA[h % 2][:, :], q_raw[:, h, :], k_stack[0][:, h, :], start=True, stop=True)\
                        .then_inc(score_done, 1)
                pe.wait_ge(neg_max_done, n + 2)
                pe.wait_ge(g_vcopied, n + 1)
                MM(MI[0:3 * H, 0:S], m_split[:, 0, :], id_bf[:, :], start=True, stop=True).then_inc(mT_done, 1)
                pe.wait_ge(m_stacked, 16 * n + 16)
                pe.wait_ge(g_maskset, n + 1)

                def values(u):
                    t, half = divmod(u, 2)
                    pe.wait_ge(unit_exp, n * UNITS + u + 1)
                    for i in range(8):
                        g, j = divmod(8 * half + i, 4)
                        last = MM(OT[32 * j:32 * j + DH + 1, S * g:S * (g + 1)], v_ones[:, 0, t, 8 * half + i, :],
                                  probs[:, u % 2, i, :], start=(t == 0 and g == 0), stop=(t == KT - 1),
                                  skip_group_check=True)
                    last.then_inc(unit_pv, 1)

                for u in range(UNITS):
                    t, half = divmod(u, 2)
                    if u >= 2:
                        pe.wait_ge(unit_exp, n * UNITS + u - 1)
                    for g in range(2):
                        for j in range(4):
                            h = 8 * half + 4 * g + j
                            MM(SB[u % 2][:, g, S * j:S * (j + 1)], k_stack[0][:, h, P * t:P * (t + 1)], q_cur[:, h, :],
                               start=(j == 0), stop=False, skip_group_check=True)
                        last = MM(SB[u % 2][:, g, :], mask_bf[:, 0, P * t:P * (t + 1)],
                                  neg_id4[:, :, :].rearrange("p a s -> p (a s)"), start=False, stop=True,
                                  skip_group_check=True)
                    last.then_inc(unit_scored, 1)
                    if u >= 1:
                        values(u - 1)
                values(UNITS - 1)
                pe.wait_ge(o_copied, n + 1)
                for g in range(4):
                    last = nc.tensor.transpose(MI[:, S * g:S * (g + 1)], o_sb[:, 0, S * g:S * (g + 1)], id_sb[:, :])
                last.then_inc(oT_done, 1)

            pe.wait_ge(flag_done, 1)
            with pe.If(pe.value_load(go_general[0:1, 0:1]) != 0):
                pe.wait_ge(v_copied, NB)
                pe.wait_ge(mT_copied, 1)
                pe.wait_ge(max_done, PRE)
                pe.wait_ge(ot_zeroed, 1)
                pe.wait_ge(consts_ready, 4)
                pe.wait_ge(s_wo, 16)
                with pe.Fori(0, NB) as b:
                    with pe.Fori(0, NBLK) as k:
                        pe.wait_ge(g_q, 4 * b + 4)
                        general_block(b * NBLK + k)
                    pe.wait_ge(attn_done, 2 * b + 2)
                    nc.tensor.transpose(MI[:, 0:S], attn[:, 0, :], id_sb[:, :]).then_inc(aT_done, 1)
                    pe.wait_ge(aT_copied, b + 1)
                    MM(MI[:, 0:DM], attn_t[:, 0, :], wo_sb[:, :], start=True, stop=True).then_inc(wo_done, 1)
            with pe.Else():
                for b in range(NB):
                    for u in range(8):
                        n = 8 * b + u
                        if n == 0:
                            for h in range(PRE, FIRST):
                                score(h)
                        unit(n, heads_of_unit(n))
                        if n == 1:
                            turn_max(0, 1)
                        if b >= 1:
                            if u == 0:
                                turn_out(b - 1)
                            if u == 2:
                                turn_attn(b - 1)
                            if u == 3:
                                project_out(b - 1)
                        if b + 1 < NB and u == 5:
                            turn_max(b + 1)
                unit(8 * NB, [])
                turn_out(NB - 1)
                turn_attn(NB - 1)
                project_out(NB - 1)

            pe.nop()
            pe.wait_ge(x1_done, NB)
            for b in range(NB):
                pe.wait_ge(xn_ready, NB + b + 1)
                last = nc.tensor.transpose(MI[:, S * b:S * (b + 1)], xr[:, b, :], id_sb[:, :])
            last.then_inc(xnT_done, 1)
            pe.wait_ge(late_weights_loaded, 16 * LATE_LOADS)
            pe.wait_ge(xnT_copied, 2)
            for i in range(2):
                MM(SB[0][:, i, :], w_in_sb[:, DI + P * i:DI + P * (i + 1)], xr_t[:, :], start=True, stop=True)\
                    .then_inc(xg_done, 1)
            for i in range(2):
                MM(SB[1][:, i, :], w_in_sb[:, 2 * DI + P * i:2 * DI + P * (i + 1)], xr_t[:, :], start=True, stop=True)\
                    .then_inc(kp_done, 1)
            MM(SA[0][0:2 * H, :], w_in_sb[:, 3 * DI:3 * DI + 2 * H], xr_t[:, :], start=True, stop=True)\
                .then_inc(vp_done, 1)
            MM(SA[1][:, :], w_in_sb[:, 0:P], xr_t[:, :], start=True, stop=True).then_inc(z_done, 1)
            MM(OT[:, :], w_in_sb[:, P:2 * P], xr_t[:, :], start=True, stop=True).then_inc(z_done, 1)
            pe.wait_ge(kp_copied, 2)
            MM(SB[1][:, 1, 0:DM], ffn_at_sb[:, :], ffn_b_sb[:, :], start=True, stop=True).then_inc(lowrank_done, 1)
            for i in range(2):
                pe.wait_ge(squared, 0 + i + 1)
                pe.wait_ge(kp_copied, 2)
                last = MM(SB[1][0:H, 0, :], heads_sb[:, i, :], squares[:, 0 + i, :], start=(i == 0), stop=(i == 1))
            last.then_inc(norms_summed, 1)
            for i in range(2):
                pe.wait_ge(xc_done, i + 1)
                last = MM(MI[0:7 * H, :], w_gate_sb[:, i, :], x_conv[:, i, :], start=(i == 0), stop=(i == 1))
            last.then_inc(gate_done, 1)
            pe.wait_ge(xg_copied, 2)
            for o in range(2):
                for i in range(2):
                    last = MM(SB[0][:, o, :], w_q_sb[:, i, P * o:P * (o + 1)], x_conv[:, i, :], start=(i == 0),
                              stop=(i == 1))
                last.then_inc(qp_done, 1)
            for i in range(2):
                pe.wait_ge(squared, 2 + i + 1)
                pe.wait_ge(vp_copied, 1)
                last = MM(SA[0][0:H, :], heads_sb[:, i, :], squares[:, 2 + i, :], start=(i == 0), stop=(i == 1))
            last.then_inc(norms_summed, 1)
            pe.wait_ge(parts_done, 2)
            pe.wait_ge(w_rs_signed, 1)
            pe.wait_ge(qp_copied, 2)
            for i in range(2):
                for b in range(NB):
                    MM(SB[0][:, i, S * b:S * (b + 1)], w_rd[:, b, P * i:P * (i + 1)], T["cos_part"][:, :], start=True,
                       stop=False)
                    last = MM(SB[0][:, i, S * b:S * (b + 1)], w_rs[:, b, P * i:P * (i + 1)], T["sin_part"][:, :],
                              start=False, stop=True)
                last.then_inc(y_done, 1)
            pe.wait_ge(gn_stats_done, 8)
            pe.wait_ge(gate_copied, 1)
            MM(MI[:, 0:8], avg_sb[:, :], gn_mv[:, :, 0], start=True, stop=True).then_inc(gn_mean_done, 1)
            pe.wait_ge(gn_spread_done, 1)
            MM(MI[:, 8:16], avg_sb[:, :], gn_spread[:, :], start=True, stop=True).then_inc(gn_var_averaged, 1)
            for i in range(2):
                pe.wait_ge(y2_done, i + 1)
                for b in range(NB):
                    last = MM(SB[1][:, 0, S * b:S * (b + 1)], y2[:, i, S * b:S * (b + 1)], w_out_sb[:, i, :],
                              start=(i == 0 and b == 0), stop=(i == 1), skip_group_check=True)
            last.then_inc(layer_projected, 1)
            for b in range(NB):
                pe.wait_ge(xn_ready, 2 * NB + b + 1)
                last = nc.tensor.transpose(MI[:, S * b:S * (b + 1)], xn[:, b, :], id_sb[:, :])
            last.then_inc(xnT_done, 1)
            pe.wait_ge(xnT_copied, 3)
            for b in range(NB):
                last = MM(SA[0][:, S * b:S * (b + 1)], xn_t[:, S * b:S * (b + 1)], w_eff[:, :], start=True, stop=True)
            last.then_inc(ffn_done, 1)


INPUTS = ["x", "ctx_t", "mask", "wq", "wk", "wv", "wo", "vec", "rows", "ident", "avg", "heads", "w_in", "w_gate", "w_q",
          "w_read", "w_out", "ffn_w", "ffn_at", "ffn_b"]


def kernel(**inputs):
    import numpy as np
    import concourse.bacc as bacc
    from concourse.bass_utils import run_bass_kernel_spmd

    a = {k: np.asarray(v) for k, v in inputs.items()}
    f32 = np.float32

    cols = {n: np.zeros((P, 1), f32) for n in VEC}

    def put(name, v):
        cols[name][:v.shape[0], 0] = v

    by_dim = lambda w: w.reshape(H, DH, DM).transpose(1, 0, 2).reshape(DM, DM)
    put("bq", a["L0_xattn_bq"].reshape(H, DH).T.reshape(-1))
    put("bk", a["L0_xattn_bk"].reshape(H, DH).T.reshape(-1))
    put("rms", a["L0_attn_rms_w"])
    b_in = a["L0_attn_in_proj_b"]
    for i in range(2):
        put(f"z_b{i}", b_in[P * i:P * (i + 1)])
        put(f"xg_b{i}", b_in[DI + P * i:DI + P * (i + 1)])
        put(f"k_b{i}", b_in[2 * DI + P * i:2 * DI + P * (i + 1)])
        put(f"cb{i}", a["L0_attn_conv_b"][P * i:P * (i + 1)])
        put(f"gn_w{i}", a["L0_attn_gn_w"][P * i:P * (i + 1)])
        put(f"gn_b{i}", a["L0_attn_gn_b"][P * i:P * (i + 1)])
        put(f"d{i}", a["L0_attn_D_param"][P * i:P * (i + 1)])
        for j in range(4):
            put(f"cw{i}{j}", a["L0_attn_conv_w"][P * i:P * (i + 1), j])
    put("v_b", b_in[3 * DI:])
    put("gate_b", a["L0_attn_gate_b"].reshape(7, H).T.reshape(-1))
    put("log_dt", np.tile(a["L0_attn_log_dt_scale"], 8))
    put("freq", np.tile((f32(1.0) / f32(10000.0) ** (np.arange(H, dtype=f32) / f32(H))).astype(f32), 8))
    put("sgn", np.repeat(np.array([-1.0, 1.0], f32), 64))
    put("eps_ln", np.full(P, EPS_LN, f32))
    put("eps_both", np.full(P, EPS_LN * EPS_RMS, f32))
    put("root_back", np.full(P, 15 * LN2, f32))
    put("norm_floor", np.full(P, 1.0e-28 * 2.0 ** 30, f32))
    put("one", np.ones(P, f32))
    rows = np.stack([a["L0_xattn_bv"], a["L0_xattn_bo"], a["L0_ffn_bias"]])
    rd = a["L0_attn_readout_w"].reshape(H, 2, DI)
    w_read = np.zeros((2, 2, NB, H, NB, DI), f32)
    for s in range(2):
        for b in range(NB):
            w_read[0, s, b, :, b, :] = rd[:, s]
            w_read[1, s, b, :, b, :] = rd[:, 1 - s]
    arrays = {
        "x": a["x"],
        "ctx_t": a["ctx_1024"].transpose(0, 2, 1),
        "mask": a["mask_BxSxS2_bk1"],
        "wq": by_dim(a["L0_xattn_Wq"]).T, "wk": by_dim(a["L0_xattn_Wk"]).T,
        "wv": a["L0_xattn_Wv"].T, "wo": a["L0_xattn_Wo"].T,
        "vec": np.concatenate([cols[n] for n in VEC], axis=1),
        "rows": np.broadcast_to(rows[None], (P, 3, DM)),
        "ident": np.eye(P, dtype=f32),
        "avg": np.kron(np.eye(P // GN, dtype=f32), np.full((GN, GN), 1.0 / GN, f32)),
        "heads": np.repeat(np.eye(H, dtype=f32), HD, axis=0).reshape(2, P, H).transpose(1, 0, 2),
        "w_in": a["L0_attn_in_proj_w"],
        "w_gate": a["L0_attn_gate_w"].reshape(2, P, 7, H).transpose(1, 0, 3, 2).reshape(P, 2, 7 * H),
        "w_q": a["L0_attn_Q_w"].reshape(2, P, DI).transpose(1, 0, 2),
        "w_read": w_read.reshape(2, P, NB, DI),
        "w_out": a["L0_attn_out_w"].reshape(2, P, DM).transpose(1, 0, 2),
        "ffn_w": a["L0_ffn_kernel"], "ffn_at": a["L0_ffn_a"].T, "ffn_b": a["L0_ffn_b"],
    }
    arrays = {k: np.ascontiguousarray(arrays[k]) for k in INPUTS}
    nc = bacc.Bacc("TRN2", target_bir_lowering=False, num_devices=1)
    aps = [nc.dram_tensor(f"in_{k}", v.shape, mybir.dt.from_np(v.dtype), kind="ExternalInput").ap()
           for k, v in arrays.items()]
    out = nc.dram_tensor("out", (NB, S, DM), F32, kind="ExternalOutput").ap()
    perceiver_kernel(nc, *aps, out)
    r = run_bass_kernel_spmd(nc, [{f"in_{k}": v for k, v in arrays.items()}], core_ids=[0])
    return r.results[0]["out"]
```
